# Optimizing a Trainium2 kernel written in Bass

```python
import numpy as np
import jax
import jax.numpy as jnp

def _softmax(x, axis=-1):
    return jax.nn.softmax(x, axis=axis)

def _gelu(x):
    return jax.nn.gelu(x, approximate=True)

def _silu(x):
    return jax.nn.silu(x)

def _sigmoid(x):
    return jax.nn.sigmoid(x)

def _layernorm(x, axis=-1, eps=1e-05):
    m = jnp.mean(x, axis=axis, keepdims=True)
    v = jnp.var(x, axis=axis, keepdims=True)
    return (x - m) / jnp.sqrt(v + eps)

def _scatter_add(tgt, idx, src, axis=0):
    return tgt.at[idx].add(src)

def _segment_sum(src, seg, n):
    return jax.ops.segment_sum(src, seg, n)
kernel_name = 'mk_seq_preln_d1_jaxref_r8_4e3b61'

def setup_inputs(seed: int=0):
    np.random.seed(seed)
    _w = jnp.asarray

    def _L0_attn_setup():
        import jax, jax.numpy as jnp
        import numpy as np
        T, N, D, H = (128, 32, 128, 128)
        LR = 0.001

        def _recon(params, z):
            W1, b1, W2, b2 = params
            h = jax.nn.gelu(z @ W1.T + b1, approximate=False)
            return z + h @ W2.T + b2
        key = jax.random.key(seed)
        ks = jax.random.split(key, 6)
        sd = 1.0 / np.sqrt(D)
        sh = 1.0 / np.sqrt(H)
        s4 = 1.0 / np.sqrt(H // 4)
        return {'in_seq': jax.random.normal(ks[0], (T, N, D), jnp.float32), 't_k': jax.random.normal(ks[1], (H, D), jnp.float32) * sd, 't_v': jax.random.normal(ks[2], (H, D), jnp.float32) * sd, 't_q': jax.random.normal(ks[3], (H, D), jnp.float32) * sd, 'W1': jax.random.normal(ks[4], (H // 4, H), jnp.float32) * sh, 'b1': jnp.zeros((H // 4,), jnp.float32), 'W2': jax.random.normal(ks[5], (H, H // 4), jnp.float32) * s4, 'b2': jnp.zeros((H,), jnp.float32)}
    _L0_attn_in = _L0_attn_setup()

    def _L0_ffn_setup():
        import math
        import jax
        import jax.numpy as jnp
        import numpy as np
        B, T, D = (1, 256, 128)
        H, KV, DH = (16, 4, 64)
        E, TOPK, DFF = (32, 4, 128)
        WINDOW = 128
        EPS = 1e-05
        ROPE_BASE = 150000.0
        ROPE_SCALE = 32.0

        def _rmsnorm(x, w):
            rms = jax.lax.rsqrt(jnp.mean(x * x, axis=-1, keepdims=True) + EPS)
            return w * (x * rms)

        def _apply_rope(x, sin, cos):
            x1, x2 = (x[..., ::2], x[..., 1::2])
            out = jnp.stack([x1 * cos - x2 * sin, x1 * sin + x2 * cos], axis=-1)
            return out.reshape(x.shape)
        key = jax.random.key(seed)
        ks = jax.random.split(key, 12)
        s = 0.02
        return {'x': jax.random.normal(ks[0], (B, T, D), jnp.float32), 'attn_norm_w': 1.0 + 0.02 * jax.random.normal(ks[1], (D,), jnp.float32), 'ffn_norm_w': 1.0 + 0.02 * jax.random.normal(ks[2], (D,), jnp.float32), 'qkv_w': s * jax.random.normal(ks[3], (D, H * DH + 2 * KV * DH), jnp.float32), 'qkv_b': s * jax.random.normal(ks[4], (H * DH + 2 * KV * DH,), jnp.float32), 'proj_w': s * jax.random.normal(ks[5], (H * DH, D), jnp.float32), 'proj_b': s * jax.random.normal(ks[6], (D,), jnp.float32), 'attn_sink': 0.5 * jax.random.normal(ks[7], (H,), jnp.float32), 'gate_w': s * jax.random.normal(ks[8], (D, E), jnp.float32), 'gate_b': s * jax.random.normal(ks[9], (E,), jnp.float32), 'W_up': s * jax.random.normal(ks[10], (E, D, 2 * DFF), jnp.float32), 'W_down': s * jax.random.normal(ks[11], (E, DFF, D), jnp.float32)}
    _L0_ffn_in = _L0_ffn_setup()
    _d = {'L0_attn_in_seq': _L0_attn_in['in_seq'], 'L0_attn_t_k': _L0_attn_in['t_k'], 'L0_attn_t_v': _L0_attn_in['t_v'], 'L0_attn_t_q': _L0_attn_in['t_q'], 'L0_attn_W1': _L0_attn_in['W1'], 'L0_attn_b1': _L0_attn_in['b1'], 'L0_attn_W2': _L0_attn_in['W2'], 'L0_attn_b2': _L0_attn_in['b2'], 'L0_ffn_attn_norm_w': _L0_ffn_in['attn_norm_w'], 'L0_ffn_ffn_norm_w': _L0_ffn_in['ffn_norm_w'], 'L0_ffn_qkv_w': _L0_ffn_in['qkv_w'], 'L0_ffn_qkv_b': _L0_ffn_in['qkv_b'], 'L0_ffn_proj_w': _L0_ffn_in['proj_w'], 'L0_ffn_proj_b': _L0_ffn_in['proj_b'], 'L0_ffn_attn_sink': _L0_ffn_in['attn_sink'], 'L0_ffn_gate_w': _L0_ffn_in['gate_w'], 'L0_ffn_gate_b': _L0_ffn_in['gate_b'], 'L0_ffn_W_up': _L0_ffn_in['W_up'], 'L0_ffn_W_down': _L0_ffn_in['W_down']}
    _x0 = _d['L0_attn_in_seq']
    _d['L0_attn_in_seq'] = jax.random.normal(jax.random.fold_in(jax.random.key(seed), 1), (16, 256, 128), dtype=_x0.dtype)
    del _x0
    return _d

def reference(L0_attn_in_seq, L0_attn_t_k, L0_attn_t_v, L0_attn_t_q, L0_attn_W1, L0_attn_b1, L0_attn_W2, L0_attn_b2, L0_ffn_attn_norm_w, L0_ffn_ffn_norm_w, L0_ffn_qkv_w, L0_ffn_qkv_b, L0_ffn_proj_w, L0_ffn_proj_b, L0_ffn_attn_sink, L0_ffn_gate_w, L0_ffn_gate_b, L0_ffn_W_up, L0_ffn_W_down):

    def _L0_attn_ref(in_seq, t_k, t_v, t_q, W1, b1, W2, b2):
        import jax, jax.numpy as jnp
        import numpy as np
        T, N, D, H = (128, 32, 128, 128)
        LR = 0.001

        def _recon(params, z):
            W1, b1, W2, b2 = params
            h = jax.nn.gelu(z @ W1.T + b1, approximate=False)
            return z + h @ W2.T + b2

        def loss_fn(params, z, y):
            return jnp.mean((_recon(params, z) - y) ** 2)

        def step(params, x):
            z = x @ t_k.T
            y = x @ t_v.T
            grads = jax.grad(loss_fn)(params, z, y)
            new_params = jax.tree_util.tree_map(lambda p, g: jax.lax.stop_gradient(p - LR * g), params, grads)
            out = _recon(new_params, x @ t_q.T)
            return (new_params, out)
        _, outs = jax.lax.scan(step, (W1, b1, W2, b2), in_seq)
        return outs

    def _L0_ffn_ref(x, attn_norm_w, ffn_norm_w, qkv_w, qkv_b, proj_w, proj_b, attn_sink, gate_w, gate_b, W_up, W_down):
        import math
        import jax
        import jax.numpy as jnp
        import numpy as np
        B, T, D = (1, 256, 128)
        H, KV, DH = (16, 4, 64)
        E, TOPK, DFF = (32, 4, 128)
        WINDOW = 128
        EPS = 1e-05
        ROPE_BASE = 150000.0
        ROPE_SCALE = 32.0

        def _rmsnorm(x, w):
            rms = jax.lax.rsqrt(jnp.mean(x * x, axis=-1, keepdims=True) + EPS)
            return w * (x * rms)

        def _apply_rope(x, sin, cos):
            x1, x2 = (x[..., ::2], x[..., 1::2])
            out = jnp.stack([x1 * cos - x2 * sin, x1 * sin + x2 * cos], axis=-1)
            return out.reshape(x.shape)
        Bx, Tx, Dx = x.shape
        h = _rmsnorm(x, attn_norm_w)
        qkv = h @ qkv_w + qkv_b
        q = qkv[..., :H * DH].reshape(Bx, Tx, H, DH).transpose(0, 2, 1, 3)
        k = qkv[..., H * DH:H * DH + KV * DH].reshape(Bx, Tx, KV, DH).transpose(0, 2, 1, 3)
        v = qkv[..., H * DH + KV * DH:].reshape(Bx, Tx, KV, DH).transpose(0, 2, 1, 3)
        pos = jnp.arange(Tx, dtype=jnp.float32) / ROPE_SCALE
        inv_freq = 1.0 / ROPE_BASE ** (jnp.arange(0, DH, 2, dtype=jnp.float32) / DH)
        freqs = pos[:, None] * inv_freq[None, :]
        sin, cos = (jnp.sin(freqs), jnp.cos(freqs))
        q = _apply_rope(q, sin, cos)
        k = _apply_rope(k, sin, cos)
        rep = H // KV
        k = jnp.repeat(k, rep, axis=1)
        v = jnp.repeat(v, rep, axis=1)
        logits = jnp.einsum('bhqd,bhkd->bhqk', q, k) / math.sqrt(DH)
        i = jnp.arange(Tx)[:, None]
        j = jnp.arange(Tx)[None, :]
        mask = (j > i) | (i - j > WINDOW)
        logits = jnp.where(mask, -jnp.inf, logits)
        lse = jax.nn.logsumexp(logits, axis=-1, keepdims=True)
        denom_log = jnp.logaddexp(lse, attn_sink.reshape(1, H, 1, 1))
        attn = jnp.exp(logits - denom_log)
        y = jnp.einsum('bhqk,bhkd->bhqd', attn, v)
        y = y.transpose(0, 2, 1, 3).reshape(Bx, Tx, H * DH)
        x = x + (y @ proj_w + proj_b)
        h2 = _rmsnorm(x, ffn_norm_w).reshape(Bx * Tx, Dx)
        glogits = h2 @ gate_w + gate_b
        topv, topi = jax.lax.top_k(glogits, TOPK)
        gw = jax.nn.softmax(topv, axis=-1)
        N = Bx * Tx
        combine = jnp.zeros((N, E), x.dtype).at[jnp.arange(N)[:, None], topi].add(gw)

        def body(acc, we):
            wu, wd, ce = we
            ug = h2 @ wu
            u, g = (ug[:, :DFF], ug[:, DFF:])
            return (acc + ce[:, None] * (jax.nn.silu(g) * u @ wd), None)
        y2, _ = jax.lax.scan(body, jnp.zeros_like(h2), (W_up, W_down, combine.T))
        return x + y2.reshape(Bx, Tx, Dx)
    x = L0_attn_in_seq
    x = x + _L0_attn_ref(_layernorm(x, axis=-1), L0_attn_t_k, L0_attn_t_v, L0_attn_t_q, L0_attn_W1, L0_attn_b1, L0_attn_W2, L0_attn_b2)
    x = x + _L0_ffn_ref(_layernorm(x, axis=-1), L0_ffn_attn_norm_w, L0_ffn_ffn_norm_w, L0_ffn_qkv_w, L0_ffn_qkv_b, L0_ffn_proj_w, L0_ffn_proj_b, L0_ffn_attn_sink, L0_ffn_gate_w, L0_ffn_gate_b, L0_ffn_W_up, L0_ffn_W_down)
    return x

_drawn_inputs = setup_inputs


def setup_inputs(seed=0):
    import zlib

    import numpy as np

    out = dict(_drawn_inputs(seed))
    spreads = {'L0_attn_b1': (0.0, 0.1), 'L0_attn_b2': (0.0, 0.1)}
    factors = {'L0_attn_t_k': 8.0,
     'L0_attn_t_v': 8.0,
     'L0_ffn_attn_norm_w': 8.0,
     'L0_ffn_ffn_norm_w': 8.0,
     'L0_ffn_qkv_w': 4.43,
     'L0_ffn_qkv_b': 8.0,
     'L0_ffn_proj_w': 4.651,
     'L0_ffn_proj_b': 6.765,
     'L0_ffn_attn_sink': 8.0,
     'L0_ffn_gate_w': 8.0,
     'L0_ffn_gate_b': 8.0,
     'L0_ffn_W_up': 8.0,
     'L0_ffn_W_down': 8.0}
    for name, (base, spread) in spreads.items():
        noise = np.random.default_rng([zlib.crc32(name.encode()), seed]).standard_normal(out[name].shape)
        drawn = base * np.exp(spread * noise) if base else spread * noise
        out[name] = jnp.asarray(drawn.astype(out[name].dtype))
    for name, factor in factors.items():
        out[name] = (out[name] * factor).astype(out[name].dtype)
    return out
```

```python
from contextlib import ExitStack

import concourse.bass as bass
import concourse.mybir as mybir

F32 = mybir.dt.float32
BF16 = mybir.dt.bfloat16
I32 = mybir.dt.int32
U32 = mybir.dt.uint32
ALU = mybir.AluOpType
ACT = mybir.ActivationFunctionType
AX = mybir.AxisListType

P = 128
SEQS, TOK, D = 16, 256, 128
TPS = TOK // P
TILES = SEQS * TPS
HID = 32
LR = 0.001
GRAD_SCALE = -LR * 2.0 / (TOK * D)
HEADS, KV, DH = 16, 4, 64
PAIRS = HEADS // 2
HALF = DH // 2
QKV = (HEADS + 2 * KV) * DH
UNITS = 12
CHUNKS = 3 * TPS
EXPERTS, TOPK, DFF = 32, 4, 128
EPS = 1e-5
TINY = 1e-30
INV_SQRT_2PI = 0.3989422804014327
REGION = SEQS * TOK + P
MAX_TILES = 160
GROUP = 4
GROUPS = MAX_TILES // GROUP
TAIL = MAX_TILES - SEQS * TOK * TOPK // P
ROWS = EXPERTS * REGION + TAIL * P


def tiles(ap):
    return ap.rearrange("p (t d) -> p t d", t=TPS)


def hold(eng, sem, value, held):
    eng.wait_ge(sem, value)
    eng.sem_inc(held, 1)


def after(eng, sem, value):
    if not isinstance(value, int) or value > 0:
        eng.wait_ge(sem, value)


def pair_heads(p):
    g2, j = p // 4, p % 4
    return (2 * g2) * 4 + j, (2 * g2 + 1) * 4 + j


def unit(u):
    j, kind = u // 3, u % 3
    if kind < 2:
        p = 2 * j + kind
        return [p], True, slice(2 * p, 2 * p + 2)
    return [2 * j, 2 * j + 1], False, slice(4 * j, 4 * j + 4)


def program(nc, a, out):
    with ExitStack() as ctx:
        def sb(name, shape, dt=F32):
            return ctx.enter_context(nc.sbuf_tensor(name, shape, dt))

        m = {"nc": nc, "a": a, "out": out}
        m["x"] = sb("x_all", [P, TILES, D])
        m["ident"] = sb("ident_sb", [P, P])
        m["ident_bf"] = sb("ident_bf", [P, P], BF16)
        m["mask2"] = sb("mask2", [P, 2, 2 * P], BF16)
        m["mask1"] = sb("mask1", [P, 4, P], BF16)
        m["before"] = sb("before_bf", [P, P], BF16)
        m["ones_bf"] = sb("ones_bf", [P, P], BF16)
        m["rope"] = sb("rope_sb", [P, TPS, 2, HALF])
        m["neghalf"] = sb("neghalf", [P, TILES])
        m["wqkv"] = sb("wqkv_sb", [P, QKV])
        m["wproj"] = sb("wproj_sb", [P, PAIRS, D])
        m["norms"] = sb("norms_sb", [P, 2])
        m["gate"] = sb("gate_sb", [P, EXPERTS])
        m["bias3"] = sb("bias3_bf", [3, QKV + D + EXPERTS], BF16)
        m["negsink"] = sb("negsink", [P, HEADS])
        m["wup"] = sb("wup_sb", [P, EXPERTS * 2 * DFF])
        m["wdown"] = sb("wdown_sb", [P, EXPERTS * D])
        m["masksum"] = sb("masksum", [P, EXPERTS], BF16)
        m["iota_e"] = sb("iota_e", [P, EXPERTS])
        m["base_e"] = sb("base_e", [P, EXPERTS])
        m["tile_rows"] = sb("tile_rows", [P, EXPERTS])
        m["slots"] = sb("slots_all", [P, TILES, TOPK])
        m["weights"] = sb("weights_all", [P, TILES, TOPK])
        m["fast"] = sb("fast", [P, 2 * HID])
        m["fast2"] = sb("fast2", [HID + 1, P])
        m["b1"] = sb("b1_sb", [HID, 1])
        m["tkT"], m["tvT"], m["tqT"] = sb("tkT_sb", [P, P]), sb("tvT_sb", [P, P]), sb("tqT_sb", [P, P])
        m["xs"] = nc.dram_tensor("expert_rows", [ROWS, D], F32, kind="Internal").ap()
        m["ys"] = nc.dram_tensor("expert_out", [MAX_TILES * P, D], F32, kind="Internal").ap()
        for n in ("attn_loaded", "moe_loaded", "tail_zeroed"):
            m[n] = ctx.enter_context(nc.semaphore(n))
        m["zeros"] = sb("zeros", [P, D])
        prepare(m)
        layers(m)
        experts(m)
        combine(m)


ATTN_LOADS, MOE_LOADS = 4, 2


def prepare(m):
    nc, a = m["nc"], m["a"]
    with ExitStack() as ctx:
        def sb(name, shape, dt=F32):
            return ctx.enter_context(nc.sbuf_tensor(name, shape, dt))

        def sem(name):
            return ctx.enter_context(nc.semaphore(name))
        NB = QKV + D + EXPERTS
        mask_f = sb("mask_f", [P, 2 * P])
        before_f = sb("before_f", [P, P])
        b3, rest = sb("b3", [3, NB]), sb("rest", [3, NB])
        part, pick = sb("part", [3, NB], BF16), sb("pick", [3, NB], BF16)
        loaded, step_done, filled = sem("p_loaded"), sem("p_step"), sem("p_filled")
        block = ctx.enter_context(nc.Block())
        small = [
            (m["x"][:, 0:8, :], a["x"][0:8 * P, :].rearrange("(t p) d -> p t d", p=P)),
            (m["ident"][:], a["ident"]),
            (m["tkT"][:], a["tkT"]), (m["tvT"][:], a["tvT"]), (m["tqT"][:], a["tqT"]),
            (m["fast"][:, 0:HID], a["W1T"]), (m["fast"][:, HID:], a["W2"]),
            (m["fast2"][0:HID, :], a["W2T"]), (m["fast2"][HID:HID + 1, :], a["b2"]), (m["b1"][:], a["b1"]),
            (m["x"][:, 8:, :], a["x"][8 * P:, :].rearrange("(t p) d -> p t d", p=P)),
            (mask_f[:], a["mask"]),
            (before_f[:], a["before"]),
            (b3[:], a["bias"].partition_broadcast(3)),
            (m["negsink"][:], a["sink"].partition_broadcast(P)),
            (m["iota_e"][:], a["iota_e"].partition_broadcast(P)),
        ]
        attn = [
            (m["rope"][:], a["rope"].rearrange("(t p) c f -> p t c f", p=P)),
            (m["norms"][:], a["norms"]),
            (m["wqkv"][:], a["wqkv"]),
            (m["wproj"][:], a["wproj"].rearrange("(c p) d -> p c d", p=P)),
        ]
        moe = [
            (m["wup"][:].rearrange("p (e f) -> p e f", e=EXPERTS), a["wup"].rearrange("e d f -> d e f")),
            (m["wdown"][:].rearrange("p (e f) -> p e f", e=EXPERTS), a["wdown"].rearrange("e d f -> d e f")),
        ]
        assert len(attn) == ATTN_LOADS and len(moe) == MOE_LOADS

        @block.sync
        def _(sp):
            for dst, src in small + [(m["gate"][:], a["gate"])]:
                sp.dma_start(dst, src).then_inc(loaded, 16)
            for dst, src in attn:
                sp.dma_start(dst, src).then_inc(m["attn_loaded"], 16)
            for dst, src in moe:
                sp.dma_start(dst, src).then_inc(m["moe_loaded"], 16)
            sp.wait_ge(filled, 1)
            for j in range(TAIL):
                row = EXPERTS * REGION + j * P
                sp.dma_start(m["xs"][row:row + P, :], m["zeros"][:]).then_inc(m["tail_zeroed"], 16)
            sp.wait_ge(loaded, 16 * (len(small) + 1))

        @block.gpsimd
        def _(pool):
            nc.gpsimd.memset(m["zeros"][:], 0.0).then_inc(filled, 1)
            nc.gpsimd.memset(m["neghalf"][:], -0.5)
            nc.gpsimd.memset(m["ones_bf"][:], 1.0)
            nc.gpsimd.memset(m["masksum"][:], 0.0)

        @block.vector
        def _(v):
            V, n = nc.vector, [0]

            def step(ins):
                n[0] += 1
                ins.then_inc(step_done, 1)
                v.wait_ge(step_done, n[0])
            v.wait_ge(loaded, 16 * (len(small) + 1))
            V.tensor_copy(m["ident_bf"][:], m["ident"][:])
            V.tensor_copy(m["before"][:], before_f[:])
            V.tensor_copy(m["mask2"][:], mask_f[:, None, :].broadcast_to([P, 2, 2 * P]))
            V.tensor_copy(m["mask1"][:], mask_f[:, None, P:].broadcast_to([P, 4, P]))
            V.tensor_scalar(m["tile_rows"][:], m["iota_e"][:], float(P), None, ALU.mult)
            V.tensor_scalar(m["base_e"][:], m["iota_e"][:], float(REGION), None, ALU.mult)
            V.tensor_scalar(m["negsink"][:], m["negsink"][:], -1.0, None, ALU.mult)
            step(V.tensor_copy(part[:], b3[:]))
            step(V.tensor_scalar(m["bias3"][:], part[:], m["ident"][0:3, 0:1], None, ALU.mult))
            src, dst = b3, rest
            for r in range(1, 3):
                step(V.tensor_tensor(dst[:], src[:], part[:], ALU.subtract))
                step(V.tensor_copy(part[:], dst[:]))
                step(V.tensor_scalar(pick[:], part[:], m["ident"][0:3, r:r + 1], None, ALU.mult))
                step(V.tensor_tensor(m["bias3"][:], m["bias3"][:], pick[:], ALU.add))
                src, dst = dst, src


def layers(m):
    nc, x, ident = m["nc"], m["x"], m["ident"]
    fast, fast2, b1 = m["fast"], m["fast2"], m["b1"]
    with ExitStack() as ctx:
        def sb(name, shape, dt=F32):
            return ctx.enter_context(nc.sbuf_tensor("l_" + name, shape, dt))

        def ps(name):
            return ctx.enter_context(nc.psum_tensor("l_" + name, [P, 512], F32))

        dkvT = sb("dkvT", [P, P])
        stats0, mv0, rstd0 = sb("stats0", [P, TILES, 6]), sb("mv0", [P, TILES, 2]), sb("rstd0", [P, TILES])
        xn, xnT = sb("xn", [P, TPS, D]), sb("xnT", [P, 2, TOK])
        zT, z = sb("zT", [P, 2, TOK]), sb("z", [P, TPS, D])
        aT, hT2 = sb("aT", [HID, 2, TOK]), sb("hT2", [HID + 1, 2, TOK])
        h, r, rT = sb("h", [P, TPS, HID + 1]), sb("r", [P, TPS, D]), sb("rT", [P, TOK])
        a_tok, expo, tanh, num, den, inv, cdf, apdf, da = (
            sb(n, [P, TPS, HID]) for n in "a_tok expo tanh num den inv cdf apdf da".split())
        warm = sb("warm", [1, 1])
        stats, mv = sb("stats", [P, TPS, 6]), sb("mv", [P, TPS, 2])
        mean_all, rs_all = sb("mean_all", [P, TILES]), sb("rs_all", [P, TILES])
        rs, sq, rms = sb("rs", [P, TPS]), sb("sq", [P, TPS]), sb("rms", [P, TPS])
        hn, hT = sb("hn", [P, TPS, D]), sb("hT", [P, TOK])
        t_cos, t_sin = sb("t_cos", [P, 512]), sb("t_sin", [P, 512])
        qT = sb("qT", [P, 2, PAIRS, TOK])
        kpad = sb("kpad", [P, 2, 2, 2, TOK])
        vv = sb("vv", [P, 2, TPS, KV * DH])
        mx, nm, es, sums, rec = (sb(n, [P, 2, 4]) for n in "mx nm es sums rec".split())
        prob, probT = sb("prob", [P, 2, 512]), sb("probT", [P, 2, 512])
        yT = sb("yT", [P, 2, PAIRS, TOK])
        xx, x2, x2sq, h2 = (sb(n, [P, TPS, D]) for n in "xx x2 x2sq h2".split())
        ss, h2T = sb("ss", [P, TPS]), sb("h2T", [P, TOK])
        glog, top, idx = sb("glog", [P, TPS, EXPERTS]), sb("top", [P, TPS, 8]), sb("idx", [P, TPS, 8], U32)
        idxf, ntop, wsum = sb("idxf", [P, TPS, 8]), sb("ntop", [P, TPS]), sb("wsum", [P, TPS])
        wexp, wrec = sb("wexp", [P, TPS, TOPK]), sb("wrec", [P, TPS])
        hot, prod = sb("hot", [P, TPS, TOPK, EXPERTS]), sb("prod", [P, TPS, TOPK, EXPERTS])
        picked, place = sb("picked", [P, TPS, EXPERTS], BF16), sb("place", [P, TPS, EXPERTS])
        slotf, slot = sb("slotf", [P, TPS, TOPK]), sb("slot", [P, TPS * TOPK], U32)
        score = [ps(f"score{i}") for i in range(3)]
        turned = [ps(f"turned{i}") for i in range(2)]
        side_q, side_f, side_g = ps("side_q"), ps("side_f"), ps("side_g")
        names = (
            "ready stat0 rs0 xn xT_ps xT z_ps zT a_ps aT az_ps a_tok z expo gelu tanh slope apdf sloped "
            "rT_ps rT hr_ps h r dh_ps da g_ps w out_ps x1 "
            "stat small norms hn hn_ps hT qkv_ps cos sin added qk_ps qk_out v_out "
            "s_ps mx nm es_in exped den rec normed t_ps probT y_ps yT "
            "proj_ps xx x2 ss rms2 h2 h2_ps h2T gate_ps glog top w_in wexp wrec idx idxf hot picked rank_ps "
            "place prod slotf slot sent x_sum held_v held_p").split()
        s = {n: ctx.enter_context(nc.semaphore("l_" + n)) for n in names}
        block = ctx.enter_context(nc.Block())
        FIRST, LAST = 4, SEQS - 3

        def live(k):
            return not isinstance(k, int) or 0 <= k < SEQS

        def run(eng, iteration):
            for n in range(FIRST):
                iteration(n, n % 2)
            with eng.Fori(0, (LAST + 1 - FIRST) // 2) as j:
                for par in range(2):
                    iteration(j * 2 + (FIRST + par), par)
            for n in range(LAST + 1, SEQS + 4):
                iteration(n, n % 2)

        def tile_of(q, t):
            return bass.ds(q * TPS + t, 1)

        def at_unit(n, par, u):
            A, p = n - 3, (par + 1) % 2
            if u >= UNITS:
                A, p, u = A + 1, 1 - p, u - UNITS
            elif u < 0:
                A, p, u = A - 1, 1 - p, u + UNITS
            return A, p, u, A * UNITS + (u + 1)

        @block.tensor
        def _(pe):
            mm, tr = nc.tensor.matmul, nc.tensor.transpose

            def bias(dst, c0, c1):
                mm(dst, m["ones_bf"][0:3, :], m["bias3"][:, c0:c1], start=True, stop=False)

            def scores(n, par, u):
                A, ap, u, done = at_unit(n, par, u)
                if not live(A):
                    return
                pairs, second, _ = unit(u)
                g2 = pairs[0] // 4
                dst = score[u % 3]
                if u == 0:
                    pe.wait_ge(s["qk_out"], A * CHUNKS + 4)
                if u == 6:
                    pe.wait_ge(s["qk_out"], A * CHUNKS + CHUNKS)
                after(pe, s["exped"], done - 3)
                if second:
                    mm(dst[:], m["ident_bf"][:], m["mask2"][:], start=True, stop=False)
                    mm(dst[:], qT[:, ap, pairs[0], P:TOK], kpad[:, ap, g2, :, :], start=False, stop=True) \
                        .then_inc(s["s_ps"], 1)
                else:
                    mm(dst[:], m["ident_bf"][:], m["mask1"][:], start=True, stop=False)
                    for k, p in enumerate(pairs):
                        ins = mm(dst[:, k * 2 * P:(k + 1) * 2 * P], qT[:, ap, p, 0:P], kpad[:, ap, g2, :, 0:P],
                                 start=False, stop=(k == 1))
                    ins.then_inc(s["s_ps"], 1)

            def turn_probs(n, par, u):
                A, ap, u, done = at_unit(n, par, u)
                if not live(A):
                    return
                after(pe, s["yT"], done - 2)
                pe.wait_ge(s["normed"], done)
                for k in range(4):
                    ins = tr(turned[u % 2][:, k * P:(k + 1) * P], prob[:, u % 2, k * P:(k + 1) * P], ident[:])
                ins.then_inc(s["t_ps"], 1)

            def values(n, par, u):
                A, ap, u, done = at_unit(n, par, u)
                if not live(A):
                    return
                pairs, second, _ = unit(u)
                g2 = pairs[0] // 4
                pe.wait_ge(s["probT"], done)
                for k in range(2):
                    for hh in range(2):
                        g = 2 * g2 + hh
                        blk = 2 * hh + k if second else 2 * k + hh
                        dst = turned[u % 2][hh * DH:(hh + 1) * DH, 0:P] if second else \
                            turned[u % 2][hh * DH:(hh + 1) * DH, k * P:(k + 1) * P]
                        ins = mm(dst, vv[:, ap, k if second else 0, g * DH:(g + 1) * DH],
                                 probT[:, u % 2, blk * P:(blk + 1) * P],
                                 start=(k == 0 or not second), stop=(k == 1 or not second))
                ins.then_inc(s["y_ps"], 1)

            def x_turn(n, par):
                F = n
                if not live(F):
                    return
                after(pe, s["hT"], n - 1)
                pe.wait_ge(s["xn"], F * TPS + TPS)
                for t in range(TPS):
                    ins = tr(side_f[:, t * P:(t + 1) * P], xn[:, t, :], ident[:])
                ins.then_inc(s["xT_ps"], 1)

            def z_products(n, par):
                F, O = n, n - 1
                if not (live(F) or live(O)):
                    return
                if live(F):
                    pe.wait_ge(s["xT"], F + 1)
                    ins = mm(side_f[:, 0:TOK], m["tkT"][:], xnT[:, par, :], start=True, stop=True)
                else:
                    pe.wait_ge(s["hT"], O)
                if live(O):
                    ins = mm(side_f[:, TOK:], m["tqT"][:], xnT[:, 1 - par, :], start=True, stop=True)
                ins.then_inc(s["z_ps"], 1)

            def a_products(n, par):
                F, O = n, n - 1
                if not (live(F) or live(O)):
                    return
                pe.wait_ge(s["zT"], n + 1)
                after(pe, s["w"], 3 * n)
                if live(F):
                    ins = mm(side_f[0:HID, 0:TOK], fast[:, 0:HID], zT[:, 0, :], start=True, stop=True)
                if live(O):
                    ins = mm(side_f[0:HID, TOK:], fast[:, 0:HID], zT[:, 1, :], start=True, stop=True)
                ins.then_inc(s["a_ps"], 1)

            def z_rows(n, par):
                F = n
                if not live(F):
                    return
                pe.wait_ge(s["aT"], n + 1)
                for t in range(TPS):
                    mm(side_f[:, P + t * P:P + (t + 1) * P], xnT[:, par, t * P:(t + 1) * P], m["tkT"][:],
                       start=True, stop=True)
                for t in range(TPS):
                    ins = tr(side_f[:, t * HID:(t + 1) * HID], aT[:, 0, t * P:(t + 1) * P], ident[0:HID, 0:HID])
                ins.then_inc(s["az_ps"], 1)

            def residual_cols(n, par):
                F = n
                if not live(F):
                    return
                pe.wait_ge(s["a_tok"], F + 1)
                pe.wait_ge(s["z"], F + 1)
                mm(side_f[:, 0:TOK], dkvT[:], xnT[:, par, :], start=True, stop=False)
                pe.wait_ge(s["gelu"], n + 1)
                mm(side_f[:, 0:TOK], fast2[:], hT2[:, 0, :], start=False, stop=True).then_inc(s["rT_ps"], 1)

            def residual_rows(n, par):
                F = n
                if not live(F):
                    return
                pe.wait_ge(s["rT"], F + 1)
                for t in range(TPS):
                    dst, tok = side_f[:, P + t * P:P + (t + 1) * P], slice(t * P, (t + 1) * P)
                    mm(dst, xnT[:, par, tok], dkvT[:], start=True, stop=False)
                    mm(dst, hT2[:, 0, tok], fast2[:], start=False, stop=True)
                for t in range(TPS):
                    ins = tr(side_f[:, t * (HID + 1):(t + 1) * (HID + 1)], hT2[:, 0, t * P:(t + 1) * P],
                             ident[0:HID + 1, 0:HID + 1])
                ins.then_inc(s["hr_ps"], 1)

            def hidden_grad(n, par):
                F = n
                if not live(F):
                    return
                pe.wait_ge(s["h"], F + 1)
                pe.wait_ge(s["r"], F + 1)
                for t in range(TPS):
                    ins = mm(side_f[:, t * HID:(t + 1) * HID], rT[:, t * P:(t + 1) * P], fast[:, HID:],
                             start=True, stop=True)
                ins.then_inc(s["dh_ps"], 1)

            def output(n, par):
                O = n - 1
                if not live(O):
                    return
                after(pe, s["da"], n + 1 if live(n) else 0)
                if not live(n):
                    pe.wait_ge(s["gelu"], n + 1)
                for t in range(TPS):
                    dst, tok = side_f[:, t * P:(t + 1) * P], slice(t * P, (t + 1) * P)
                    mm(dst, xnT[:, 1 - par, tok], m["tqT"][:], start=True, stop=False)
                    ins = mm(dst, hT2[:, 1, tok], fast2[:], start=False, stop=True)
                ins.then_inc(s["out_ps"], 1)

            def gradients(n, par):
                F, B = n, n - 4
                if not live(F):
                    return
                pe.wait_ge(s["da"], F + 1)
                after(pe, s["place"], 3 * (B + 1))
                for t in range(TPS):
                    mm(side_g[:, HID:2 * HID], r[:, t, :], h[:, t, 0:HID], start=(t == 0), stop=(t == TPS - 1))
                for t in range(TPS):
                    mm(side_g[0:HID + 1, P:2 * P], h[:, t, :], r[:, t, :], start=(t == 0), stop=(t == TPS - 1))
                for t in range(TPS):
                    mm(side_g[:, 0:HID], z[:, t, :], da[:, t, :], start=(t == 0), stop=(t == TPS - 1))
                for t in range(TPS):
                    ins = mm(side_g[0:HID, 2 * P:2 * P + 1], da[:, t, :], h[:, t, HID:HID + 1],
                             start=(t == 0), stop=(t == TPS - 1))
                ins.then_inc(s["g_ps"], 1)

            def norm_turn(n, par):
                O = n - 1
                if not live(O):
                    return
                pe.wait_ge(s["x1"], O + 1)
                pe.wait_ge(s["hn"], O * TPS + TPS)
                for t in range(TPS):
                    ins = tr(side_f[:, t * P:(t + 1) * P], hn[:, t, :], ident[:])
                ins.then_inc(s["hn_ps"], 1)

            def qkv(n, par, c):
                N = n - 2
                if not live(N):
                    return
                t, part = c % 2, (2, 0, 1)[c // 2]
                if c == 0:
                    pe.wait_ge(s["hT"], N + 1)
                after(pe, s["qk_out"], N * CHUNKS + c)
                bias(side_q[:], part * 512, (part + 1) * 512)
                mm(side_q[:], hT[:, t * P:(t + 1) * P], m["wqkv"][:, part * 512:(part + 1) * 512],
                   start=False, stop=True).then_inc(s["qkv_ps"], 1)

            def qk_turn(n, par, c):
                N = n - 2
                if not live(N):
                    return
                if c < 2:
                    pe.wait_ge(s["v_out"], N * TPS + c + 1)
                pe.wait_ge(s["added"], N * CHUNKS + c + 1)
                for k in range(2 if c < 2 else 4):
                    ins = tr(side_q[:, k * P:(k + 1) * P], t_cos[:, k * P:(k + 1) * P], ident[:])
                ins.then_inc(s["qk_ps"], 1)

            def project(n, par):
                B = n - 4
                if not live(B):
                    return
                pe.wait_ge(s["yT"], B * UNITS + UNITS)
                after(pe, s["w"], 3 * (n if live(n - 1) else 0))
                for t in range(TPS):
                    cols = slice(t * P, (t + 1) * P)
                    bias(side_g[:, cols], QKV, QKV + D)
                    for p in range(PAIRS):
                        ins = mm(side_g[:, cols], yT[:, par, p, cols], m["wproj"][:, p, :], start=False,
                                 stop=(p == PAIRS - 1))
                ins.then_inc(s["proj_ps"], 1)

            def h2_turn(n, par):
                B = n - 4
                if not live(B):
                    return
                pe.wait_ge(s["h2"], B * TPS + TPS)
                for t in range(TPS):
                    ins = tr(side_g[:, t * P:(t + 1) * P], h2[:, t, :], ident[:])
                ins.then_inc(s["h2_ps"], 1)

            def gate(n, par):
                B = n - 4
                if not live(B):
                    return
                pe.wait_ge(s["h2T"], B + 1)
                for t in range(TPS):
                    cols = slice(t * EXPERTS, (t + 1) * EXPERTS)
                    bias(side_g[:, cols], QKV + D, QKV + D + EXPERTS)
                    ins = mm(side_g[:, cols], h2T[:, t * P:(t + 1) * P], m["gate"][:], start=False, stop=True)
                ins.then_inc(s["gate_ps"], 1)

            def ranks(n, par):
                B = n - 4
                if not live(B):
                    return
                pe.wait_ge(s["picked"], B * TPS + TPS)
                for t in range(TPS):
                    cols = slice(t * EXPERTS, (t + 1) * EXPERTS)
                    mm(side_g[:, cols], m["ones_bf"][:], m["masksum"][:], start=True, stop=False)
                    if t == 1:
                        mm(side_g[:, cols], m["ones_bf"][:], picked[:, 0, :], start=False, stop=False)
                    ins = mm(side_g[:, cols], m["before"][:], picked[:, t, :], start=False, stop=True)
                ins.then_inc(s["rank_ps"], 1)

            side = {0: [], 1: [x_turn], 2: [z_products, project], 3: [a_products], 4: [z_rows],
                    5: [residual_cols, h2_turn], 6: [residual_rows, gate], 7: [hidden_grad], 8: [output, ranks],
                    9: [], 10: [gradients], 11: [norm_turn]}

            def iteration(n, par):
                for u in range(UNITS):
                    scores(n, par, u + 2)
                    if u % 2 == 0:
                        qkv(n, par, u // 2)
                    turn_probs(n, par, u)
                    for stage in side[u]:
                        stage(n, par)
                    values(n, par, u - 1)
                    if u % 2 == 1:
                        qk_turn(n, par, u // 2)

            pe.wait_ge(s["ready"], 4)
            pe.wait_ge(m["attn_loaded"], ATTN_LOADS * 16)
            run(pe, iteration)

        @block.vector
        def _(v):
            V = nc.vector

            def maxima(n, par, u):
                A, ap, u, done = at_unit(n, par, u)
                if not live(A):
                    return
                _, second, cols = unit(u)
                b, w = u % 2, cols.stop - cols.start
                sink = m["negsink"][:, cols]
                v.wait_ge(s["s_ps"], done)
                V.tensor_reduce(mx[:, b, 0:w], score[u % 3][:].rearrange("p (h k) -> p h k", h=w), AX.X,
                                ALU.max).then_inc(s["mx"], 1)
                v.wait_ge(s["mx"], done)
                V.scalar_tensor_tensor(out=nm[:, b, 0:w], in0=mx[:, b, 0:w], scalar=-0.125, in1=sink,
                                       op0=ALU.mult, op1=ALU.min).then_inc(s["nm"], 1)
                v.wait_ge(s["nm"], done)
                V.tensor_tensor(es[:, b, 0:w], nm[:, b, 0:w], sink, ALU.subtract).then_inc(s["es_in"], 1)

            def normalise(n, par, u):
                A, ap, u, done = at_unit(n, par, u)
                if not live(A):
                    return
                _, second, cols = unit(u)
                b, w = u % 2, cols.stop - cols.start
                v.wait_ge(s["exped"], done)
                V.tensor_tensor(sums[:, b, 0:w], sums[:, b, 0:w], es[:, b, 0:w], ALU.add).then_inc(s["den"], 1)
                v.wait_ge(s["den"], done)
                V.reciprocal(rec[:, b, 0:w], sums[:, b, 0:w]).then_inc(s["rec"], 1)
                v.wait_ge(s["rec"], done)
                k = 512 // w
                for j in range(w):
                    ins = V.tensor_scalar(prob[:, b, j * k:(j + 1) * k], prob[:, b, j * k:(j + 1) * k],
                                          rec[:, b, j:j + 1], None, ALU.mult)
                ins.then_inc(s["normed"], 1)

            def x_norm(n, par):
                F = n + 1
                if not live(F):
                    return
                after(v, s["xT_ps"], F)
                for t in range(TPS):
                    V.tensor_scalar(xn[:, t, :], x[:, tile_of(F, t), :].squeeze(1), mv0[:, tile_of(F, t), 0],
                                    rstd0[:, tile_of(F, t)], ALU.subtract, ALU.mult).then_inc(s["xn"], 1)

            def a_bias(n, par):
                F, O = n, n - 1
                if not (live(F) or live(O)):
                    return
                lo, hi = (0 if live(F) else TOK), (512 if live(O) else TOK)
                v.wait_ge(s["a_ps"], n + 1)
                V.tensor_scalar(aT[:].rearrange("p a t -> p (a t)")[:, lo:hi], side_f[0:HID, lo:hi], b1[:], TINY,
                                ALU.add, ALU.add).then_inc(s["aT"], 1)

            def a_rows(n, par):
                F = n
                if not live(F):
                    return
                v.wait_ge(s["az_ps"], F + 1)
                V.tensor_copy(a_tok[:], tiles(side_f[:, 0:TPS * HID])).then_inc(s["a_tok"], 1)
                V.tensor_copy(z[:], tiles(side_f[:, P:P + TOK])).then_inc(s["z"], 1)
                v.wait_ge(s["a_tok"], F + 1)
                V.scalar_tensor_tensor(out=expo[:], in0=a_tok[:], scalar=0.25, in1=a_tok[:],
                                       op0=ALU.mult, op1=ALU.mult).then_inc(s["expo"], 1)
                V.reciprocal(inv[:], a_tok[:]).then_inc(s["slope"], 1)

            def slope_pdf(n, par):
                F = n
                if not live(F):
                    return
                v.wait_ge(s["tanh"], F + 1)
                V.tensor_scalar(den[:], tanh[:], 1.0, None, ALU.add).then_inc(s["slope"], 1)
                V.tensor_scalar(num[:], tanh[:], -INV_SQRT_2PI, INV_SQRT_2PI, ALU.mult, ALU.add) \
                    .then_inc(s["slope"], 1)
                v.wait_ge(s["slope"], 6 * F + 2)
                V.reciprocal(den[:], den[:]).then_inc(s["slope"], 1)
                v.wait_ge(s["slope"], 6 * F + 3)
                V.tensor_tensor(num[:], num[:], a_tok[:], ALU.mult).then_inc(s["slope"], 1)
                v.wait_ge(s["slope"], 6 * F + 5)
                V.tensor_tensor(apdf[:], num[:], den[:], ALU.mult).then_inc(s["apdf"], 1)

            def slope_cdf(n, par):
                F = n
                if not live(F):
                    return
                v.wait_ge(s["hr_ps"], F + 1)
                V.tensor_copy(h[:], tiles(side_f[:, 0:TPS * (HID + 1)])).then_inc(s["h"], 1)
                V.tensor_copy(r[:], tiles(side_f[:, P:P + TOK])).then_inc(s["r"], 1)
                v.wait_ge(s["h"], F + 1)
                V.tensor_tensor(cdf[:], inv[:], h[:, :, 0:HID], ALU.mult).then_inc(s["slope"], 1)
                v.wait_ge(s["apdf"], F + 1)
                v.wait_ge(s["slope"], 6 * F + 6)
                V.tensor_tensor(cdf[:], cdf[:], apdf[:], ALU.add).then_inc(s["sloped"], 1)

            def hidden_grad(n, par):
                F = n
                if not live(F):
                    return
                v.wait_ge(s["sloped"], F + 1)
                v.wait_ge(s["dh_ps"], F + 1)
                V.tensor_tensor(da[:], tiles(side_f[:, 0:TPS * HID]), cdf[:], ALU.mult).then_inc(s["da"], 1)

            def output(n, par):
                O = n - 1
                if not live(O):
                    return
                v.wait_ge(s["out_ps"], O + 1)
                xt = x[:, bass.ds(O * TPS, TPS), :]
                V.tensor_tensor(xt, tiles(side_f[:, 0:TOK]), xt, ALU.add).then_inc(s["x1"], 1)
                hold(v, s["x1"], O + 1, s["held_v"])
                for t in range(TPS):
                    V.bn_stats(stats[:, t, :], x[:, tile_of(O, t), :].squeeze(1)).then_inc(s["stat"], 1)
                hold(v, s["stat"], 4 * O + 2, s["held_v"])
                for t in range(TPS):
                    V.bn_aggr(mv[:, t, :], stats[:, t, :]).then_inc(s["stat"], 1)

            def normed_rows(n, par):
                O = n - 1
                if not live(O):
                    return
                v.wait_ge(s["norms"], O + 1)
                for t in range(TPS):
                    V.tensor_scalar(hn[:, t, :], x[:, tile_of(O, t), :].squeeze(1), mv[:, t, 0:1], rms[:, t:t + 1],
                                    ALU.subtract, ALU.mult).then_inc(s["hn"], 1)

            def update(n, par):
                F = n
                if not live(F):
                    return
                v.wait_ge(s["g_ps"], F + 1)
                V.scalar_tensor_tensor(out=fast[:], in0=side_g[:, 0:2 * HID], scalar=GRAD_SCALE, in1=fast[:],
                                       op0=ALU.mult, op1=ALU.add).then_inc(s["w"], 1)
                V.scalar_tensor_tensor(out=fast2[:], in0=side_g[0:HID + 1, P:2 * P], scalar=GRAD_SCALE,
                                       in1=fast2[:], op0=ALU.mult, op1=ALU.add).then_inc(s["w"], 1)
                V.scalar_tensor_tensor(out=b1[:], in0=side_g[0:HID, 2 * P:2 * P + 1], scalar=GRAD_SCALE,
                                       in1=b1[:], op0=ALU.mult, op1=ALU.add).then_inc(s["w"], 1)

            def rope(n, par, c):
                N = n - 2
                if not live(N):
                    return
                t, heads = c % 2, (4 if c < 2 else 8)
                v.wait_ge(s["qkv_ps"], N * CHUNKS + c + 1)
                after(v, s["qk_ps"], N * CHUNKS + c)
                src = side_q[:, 0:heads * DH].rearrange("p (h a f) -> p h a f", h=heads, a=2)
                cos = m["rope"][:, t, 0, :][:, None, None, :].broadcast_to([P, heads, 2, HALF])
                sin = m["rope"][:, t, 1, :][:, None, :].broadcast_to([P, heads, HALF])
                dc = t_cos[:, 0:heads * DH].rearrange("p (h a f) -> p h a f", h=heads, a=2)
                dn = t_sin[:, 0:heads * DH].rearrange("p (h a f) -> p h a f", h=heads, a=2)
                V.tensor_tensor(dc, src, cos, ALU.mult).then_inc(s["cos"], 1)
                V.scalar_tensor_tensor(out=dn[:, :, 0, :], in0=src[:, :, 1, :], scalar=-1.0, in1=sin,
                                       op0=ALU.mult, op1=ALU.mult).then_inc(s["sin"], 1)
                V.tensor_tensor(dn[:, :, 1, :], src[:, :, 0, :], sin, ALU.mult).then_inc(s["sin"], 1)

            def attended(n, par):
                B = n - 4
                if not live(B):
                    return
                after(v, s["x_sum"], B)
                for t in range(TPS):
                    V.tensor_scalar(xx[:, t, :], x[:, tile_of(B, t), :].squeeze(1), mean_all[:, tile_of(B, t)],
                                    rs_all[:, tile_of(B, t)], ALU.subtract, ALU.mult).then_inc(s["xx"], 1)
                v.wait_ge(s["xx"], TPS * B + TPS)
                v.wait_ge(s["proj_ps"], B + 1)
                V.tensor_tensor(x2[:], tiles(side_g[:, 0:TOK]), xx[:], ALU.add).then_inc(s["x2"], 1)
                v.wait_ge(s["x2"], B + 1)
                for t in range(TPS):
                    V.tensor_tensor_reduce(out=x2sq[:, t, :], in0=x2[:, t, :], in1=x2[:, t, :], scale=1.0,
                                           scalar=0.0, op0=ALU.mult, op1=ALU.add,
                                           accum_out=ss[:, t:t + 1]).then_inc(s["ss"], 1)

            def h2_rows(n, par):
                B = n - 4
                if not live(B):
                    return
                after(v, s["sent"], B * (TPS * TOPK * 16))
                v.wait_ge(s["rms2"], 2 * B + 2)
                for t in range(TPS):
                    V.tensor_scalar(h2[:, t, :], x2[:, t, :], ss[:, t:t + 1], None, ALU.mult).then_inc(s["h2"], 1)

            def pick(n, par):
                B = n - 4
                if not live(B):
                    return
                v.wait_ge(s["gate_ps"], B + 1)
                V.tensor_copy(glog[:], side_g[:, 0:TPS * EXPERTS].rearrange("p (t e) -> p t e", t=TPS)) \
                    .then_inc(s["glog"], 1)
                hold(v, s["glog"], B + 1, s["held_v"])
                for t in range(TPS):
                    V.max(top[:, t, :], glog[:, t, :]).then_inc(s["top"], 1)
                v.wait_ge(s["top"], TPS * B + TPS)
                V.tensor_scalar(ntop[:], top[:, :, 0], -1.0, None, ALU.mult).then_inc(s["w_in"], 1)
                for t in range(TPS):
                    V.max_index(idx[:, t, :], top[:, t, :], glog[:, t, :]).then_inc(s["idx"], 1)

            def one_hot(n, par):
                B = n - 4
                if not live(B):
                    return
                v.wait_ge(s["idx"], TPS * B + TPS)
                V.tensor_copy(idxf[:], idx[:]).then_inc(s["idxf"], 1)
                v.wait_ge(s["idxf"], B + 1)
                for t in range(TPS):
                    V.tensor_tensor(hot[:, t], m["iota_e"][:, None, :].broadcast_to([P, TOPK, EXPERTS]),
                                    idxf[:, t, 0:TOPK][:, :, None].broadcast_to([P, TOPK, EXPERTS]), ALU.is_equal) \
                        .then_inc(s["hot"], 1)
                v.wait_ge(s["hot"], TPS * B + TPS)
                with nc.allow_low_precision("sums of four 0/1 values, exact in bfloat16"):
                    for t in range(TPS):
                        V.tensor_reduce(picked[:, t, :], hot[:, t].rearrange("p k e -> p e k"), AX.X, ALU.add) \
                            .then_inc(s["picked"], 1)

            def places(n, par):
                B = n - 4
                if not live(B):
                    return
                v.wait_ge(s["rank_ps"], B + 1)
                V.tensor_tensor(place[:], side_g[:, 0:TPS * EXPERTS].rearrange("p (t e) -> p t e", t=TPS),
                                m["base_e"][:, None, :].broadcast_to([P, TPS, EXPERTS]), ALU.add) \
                    .then_inc(s["place"], 1)
                for t in range(TPS):
                    v.wait_ge(s["place"], 3 * B + 1 + t)
                    V.tensor_tensor(m["masksum"][:], m["masksum"][:], picked[:, t, :], ALU.add) \
                        .then_inc(s["place"], 1)
                for t in range(TPS):
                    V.tensor_tensor(prod[:, t], hot[:, t], place[:, t, :][:, None, :]
                                    .broadcast_to([P, TOPK, EXPERTS]), ALU.mult).then_inc(s["prod"], 1)
                v.wait_ge(s["prod"], TPS * B + TPS)
                V.tensor_reduce(slotf[:], prod[:], AX.X, ALU.add).then_inc(s["slotf"], 1)
                v.wait_ge(s["slotf"], B + 1)
                V.tensor_copy(m["slots"][:, bass.ds(B * TPS, TPS), :], slotf[:])
                V.tensor_copy(slot[:].rearrange("p (t k) -> p t k", t=TPS), slotf[:]).then_inc(s["slot"], 1)
                v.wait_ge(s["wexp"], TPS * B + TPS)
                V.reciprocal(wrec[:], wsum[:]).then_inc(s["wrec"], 1)
                v.wait_ge(s["wrec"], B + 1)
                V.tensor_tensor(m["weights"][:, bass.ds(B * TPS, TPS), :], wexp[:],
                                wrec[:, :, None].broadcast_to([P, TPS, TOPK]), ALU.mult)

            side = {0: [], 1: [], 2: [], 3: [attended, a_bias], 4: [a_rows, h2_rows], 5: [slope_pdf],
                    6: [slope_cdf], 7: [pick, hidden_grad], 8: [one_hot], 9: [output, places], 10: [normed_rows, x_norm],
                    11: [update]}

            def iteration(n, par):
                for u in range(UNITS):
                    maxima(n, par, u + 1)
                    normalise(n, par, u)
                    if u % 2 == 0:
                        rope(n, par, u // 2)
                    for stage in side[u]:
                        stage(n, par)

            V.memset(hT2[HID:HID + 1, :, :], 1.0).then_inc(s["ready"], 1)
            V.tensor_tensor(dkvT[:], m["tkT"][:], m["tvT"][:], ALU.subtract).then_inc(s["ready"], 1)
            for t in range(TILES):
                V.bn_stats(stats0[:, t, :], x[:, t, :]).then_inc(s["stat0"], 1)
            v.wait_ge(s["stat0"], TILES)
            for t in range(TILES):
                V.bn_aggr(mv0[:, t, :], stats0[:, t, :]).then_inc(s["stat0"], 1)
            v.wait_ge(s["rs0"], 2)
            x_norm(-1, 1)
            run(v, iteration)

        @block.scalar
        def _(act):
            A_ = nc.scalar

            def exps(n, par, u):
                A, ap, u, done = at_unit(n, par, u)
                if not live(A):
                    return
                _, second, cols = unit(u)
                b, w = u % 2, cols.stop - cols.start
                act.wait_ge(s["es_in"], done)
                A_.activation(es[:, b, 0:w], es[:, b, 0:w], ACT.Exp)
                after(act, s["t_ps"], done - 2)
                k = 512 // w
                for j in range(w):
                    cols = slice(j * k, (j + 1) * k)
                    ins = A_.activation(prob[:, b, cols], score[u % 3][:, cols], ACT.Exp, bias=nm[:, b, j:j + 1],
                                        scale=0.125, accum_out=sums[:, b, j:j + 1])
                ins.then_inc(s["exped"], 1)

            def take_probs(n, par, u):
                A, ap, u, done = at_unit(n, par, u)
                if not live(A):
                    return
                act.wait_ge(s["t_ps"], done)
                after(act, s["y_ps"], done - 2)
                A_.copy(probT[:, u % 2, :], turned[u % 2][:]).then_inc(s["probT"], 1)

            def take_y(n, par, u):
                A, ap, u, done = at_unit(n, par, u)
                if not live(A):
                    return
                pairs, second, _ = unit(u)
                act.wait_ge(s["y_ps"], done)
                if second:
                    A_.copy(yT[:, ap, pairs[0], P:TOK], turned[u % 2][:, 0:P]).then_inc(s["yT"], 1)
                else:
                    A_.copy(yT[:, ap, pairs[0]:pairs[0] + 2, 0:P],
                            turned[u % 2][:, 0:2 * P].rearrange("p (k t) -> p k t", k=2)).then_inc(s["yT"], 1)

            def xT_out(n, par):
                if not live(n):
                    return
                act.wait_ge(s["xT_ps"], n + 1)
                A_.copy(xnT[:, par, :], side_f[:, 0:TOK]).then_inc(s["xT"], 1)

            def zT_out(n, par):
                F, O = n, n - 1
                if not (live(F) or live(O)):
                    return
                lo, hi = (0 if live(F) else 1), (2 if live(O) else 1)
                act.wait_ge(s["z_ps"], n + 1)
                A_.copy(zT[:, lo:hi, :], side_f[:].rearrange("p (a t) -> p a t", a=2)[:, lo:hi, :]) \
                    .then_inc(s["zT"], 1)

            def gelus(n, par):
                F, O = n, n - 1
                if not (live(F) or live(O)):
                    return
                lo, hi = (0 if live(F) else 1), (2 if live(O) else 1)
                act.wait_ge(s["aT"], n + 1)
                A_.activation(hT2[0:HID, lo:hi, :], aT[:, lo:hi, :], ACT.Gelu).then_inc(s["gelu"], 1)
                if live(F):
                    act.wait_ge(s["expo"], F + 1)
                    A_.activation(tanh[:], expo[:], ACT.Tanh).then_inc(s["tanh"], 1)

            def rT_out(n, par):
                if not live(n):
                    return
                act.wait_ge(s["rT_ps"], n + 1)
                A_.copy(rT[:], side_f[:, 0:TOK]).then_inc(s["rT"], 1)

            def hT_out(n, par):
                O = n - 1
                if not live(O):
                    return
                after(act, s["qkv_ps"], O * CHUNKS)
                act.wait_ge(s["hn_ps"], O + 1)
                A_.activation(hT[:], side_f[:, 0:TOK], ACT.Copy, scale=m["norms"][:, 0:1]).then_inc(s["hT"], 1)

            def v_out(n, par, c):
                N = n - 2
                if not live(N):
                    return
                act.wait_ge(s["sin"], 2 * (N * CHUNKS + c) + 2)
                after(act, s["y_ps"], (N - 1) * UNITS)
                A_.copy(vv[:, par, c, :], side_q[:, KV * DH:2 * KV * DH]).then_inc(s["v_out"], 1)

            def qk_out(n, par, c):
                N = n - 2
                if not live(N):
                    return
                t = c % 2
                tok = slice(t * P, (t + 1) * P)
                act.wait_ge(s["qk_ps"], N * CHUNKS + c + 1)
                if c < 2:
                    for half in range(2):
                        rows = slice(half * DH, (half + 1) * DH)
                        ins = A_.copy(kpad[rows, par, :, half, tok],
                                      side_q[rows, 0:2 * P].rearrange("p (g t) -> p g t", g=2))
                else:
                    p0 = 4 * (c // 2 - 1)
                    ins = A_.copy(qT[:, par, p0:p0 + 4, tok], side_q[:].rearrange("p (b t) -> p b t", b=4))
                ins.then_inc(s["qk_out"], 1)

            def h2T_out(n, par):
                B = n - 4
                if not live(B):
                    return
                act.wait_ge(s["h2_ps"], B + 1)
                A_.activation(h2T[:], side_g[:, 0:TOK], ACT.Copy, scale=m["norms"][:, 1:2]).then_inc(s["h2T"], 1)

            def weights(n, par):
                B = n - 4
                if not live(B):
                    return
                act.wait_ge(s["w_in"], B + 1)
                for t in range(TPS):
                    A_.activation(wexp[:, t, :], top[:, t, 0:TOPK], ACT.Exp, bias=ntop[:, t:t + 1],
                                  accum_out=wsum[:, t:t + 1]).then_inc(s["wexp"], 1)

            side = {1: [xT_out], 2: [zT_out], 4: [gelus], 5: [rT_out, h2T_out], 8: [weights], 11: [hT_out]}

            def iteration(n, par):
                for u in range(UNITS):
                    exps(n, par, u + 1)
                    take_probs(n, par, u)
                    if u in (0, 2):
                        v_out(n, par, u // 2)
                    for stage in side.get(u, []):
                        stage(n, par)
                    take_y(n, par, u - 1)
                    if u % 2 == 1:
                        qk_out(n, par, u // 2)

            act.wait_ge(m["attn_loaded"], ATTN_LOADS * 16)
            run(act, iteration)

        @block.gpsimd
        def _(pool):
            g = nc.gpsimd

            def rope_add(n, par, c):
                N = n - 2
                if not live(N):
                    return
                w = (4 if c < 2 else 8) * DH
                pool.wait_ge(s["sin"], 2 * (N * CHUNKS + c) + 2)
                g.tensor_tensor(t_cos[:, 0:w], t_cos[:, 0:w], t_sin[:, 0:w], ALU.add).then_inc(s["added"], 1)

            def norms(n, par):
                O = n - 1
                if not live(O):
                    return
                hold(pool, s["stat"], 4 * O + 4, s["held_p"])
                g.tensor_scalar(rs[:], mv[:, :, 1], EPS, None, ALU.add).then_inc(s["small"], 1)
                g.tensor_copy(mean_all[:, bass.ds(O * TPS, TPS)], mv[:, :, 0])
                pool.wait_ge(s["small"], O * 6 + 1)
                g.tensor_tensor(rs[:], rs[:], m["neghalf"][:, 0:TPS], ALU.pow).then_inc(s["small"], 1)
                pool.wait_ge(s["small"], O * 6 + 2)
                g.tensor_tensor(sq[:], rs[:], rs[:], ALU.mult).then_inc(s["small"], 1)
                g.tensor_copy(rs_all[:, bass.ds(O * TPS, TPS)], rs[:])
                pool.wait_ge(s["small"], O * 6 + 3)
                g.tensor_tensor(sq[:], sq[:], mv[:, :, 1], ALU.mult).then_inc(s["small"], 1)
                hold(pool, s["small"], O * 6 + 4, s["held_p"])
                g.tensor_scalar(sq[:], sq[:], EPS, None, ALU.add).then_inc(s["small"], 1)
                pool.wait_ge(s["small"], O * 6 + 5)
                g.tensor_tensor(sq[:], sq[:], m["neghalf"][:, 0:TPS], ALU.pow).then_inc(s["small"], 1)
                pool.wait_ge(s["small"], O * 6 + 6)
                g.tensor_tensor(rms[:], sq[:], rs[:], ALU.mult).then_inc(s["norms"], 1)

            def rms2(n, par):
                B = n - 4
                if not live(B):
                    return
                hold(pool, s["ss"], B * 2 + 2, s["held_p"])
                g.tensor_scalar(ss[:], ss[:], 1.0 / D, EPS, ALU.mult, ALU.add).then_inc(s["rms2"], 1)
                pool.wait_ge(s["rms2"], 2 * B + 1)
                g.tensor_tensor(ss[:], ss[:], m["neghalf"][:, 0:TPS], ALU.pow).then_inc(s["rms2"], 1)
                xt = x[:, bass.ds(B * TPS, TPS), :]
                g.tensor_tensor(xt, xt, x2[:], ALU.add).then_inc(s["x_sum"], 1)

            def send(n, par):
                B = n - 4
                if not live(B):
                    return
                pool.wait_ge(s["h2"], TPS * B + TPS)
                hold(pool, s["slot"], B + 1, s["held_p"])
                for t in range(TPS):
                    for k in range(TOPK):
                        g.indirect_dma_start(m["xs"], bass.IndirectOffsetOnAxis(
                            ap=slot[:, t * TOPK + k:t * TOPK + k + 1], axis=0), h2[:, t, :], None) \
                            .then_inc(s["sent"], 16)

            side = {3: [rms2], 9: [norms], 11: [send]}

            def iteration(n, par):
                for u in range(UNITS):
                    if u % 2 == 0:
                        rope_add(n, par, u // 2)
                    for stage in side.get(u, []):
                        stage(n, par)

            g.memset(kpad[:], 0.0).then_inc(s["ready"], 1)
            pool.wait_ge(s["stat0"], 2 * TILES)
            g.tensor_scalar(rstd0[:], mv0[:, :, 1], EPS, None, ALU.add).then_inc(s["rs0"], 1)
            pool.wait_ge(s["rs0"], 1)
            g.tensor_tensor(rstd0[:], rstd0[:], m["neghalf"][:], ALU.pow).then_inc(s["rs0"], 1)
            pool.wait_ge(s["rs0"], 2)
            g.memset(rs[:], 0.0).then_inc(s["ready"], 1)
            run(pool, iteration)
            pool.wait_ge(s["sent"], SEQS * TPS * TOPK * 16)


def experts(m):
    nc, ident = m["nc"], m["ident"]
    with ExitStack() as ctx:
        def sb(name, shape, dt=F32):
            return ctx.enter_context(nc.sbuf_tensor(name, shape, dt))

        def sem(name):
            return ctx.enter_context(nc.semaphore("e_" + name))

        iota_t = sb("iota_t_sb", [P, MAX_TILES])
        upto = sb("upto", [P, EXPERTS, EXPERTS])
        cnt, ntile, cum = sb("cnt", [P, EXPERTS]), sb("ntile", [P, EXPERTS]), sb("cum", [P, EXPERTS])
        sq = sb("e_sq", [P, EXPERTS, EXPERTS])
        past = sb("past", [P, MAX_TILES, EXPERTS])
        cost = sb("cost", [P, MAX_TILES, EXPERTS])
        exp_t, skip_t = sb("exp_t", [P, MAX_TILES]), sb("skip_t", [P, MAX_TILES])
        row_t, w_t = sb("row_t", [P, MAX_TILES], I32), sb("w_t", [P, MAX_TILES], I32)
        pad_t = sb("pad_t", [P, EXPERTS], I32)
        zeros = m["zeros"]
        jump = sb("jump", [P, EXPERTS])
        turn, place = sb("turn", [P, 2, TILES, TOPK]), sb("e_place", [P, TILES, TOPK])
        xt = sb("xt", [P, 3, GROUP, D])
        xT, act, hid, hidT = (sb(n, [P, 2, GROUP, D]) for n in ("e_xT", "e_act", "e_hid", "e_hidT"))
        yo = sb("yo", [P, 2, GROUP, D])
        p_xy = [ctx.enter_context(nc.psum_tensor(f"e_xy{b}", [P, 512], F32)) for b in range(2)]
        p_h = [ctx.enter_context(nc.psum_tensor(f"e_h{b}", [P, 512], F32)) for b in range(2)]
        p_up = [ctx.enter_context(nc.psum_tensor(f"e_up{b}", [P, GROUP, 2 * DFF], F32)) for b in range(2)]
        names = "init cnt_ps place step planned padded used in_a in_b in_c xT_ps xT up_ps act hid hidT_ps hidT y_ps y out_a out_b held".split()
        s = {n: sem(n) for n in names}
        arrived = [s["in_a"], s["in_b"]]
        written = [s["out_a"], s["out_b"]]
        block = ctx.enter_context(nc.Block())
        N = GROUPS // 2

        @block.sync
        def _(sp):
            sp.dma_start(iota_t[:], m["a"]["iota_t"].partition_broadcast(P)).then_inc(s["init"], 16)
            sp.wait_ge(s["init"], 16 + 1)
            sp.wait_ge(s["planned"], 1)
            with sp.Fori(0, EXPERTS) as e:
                r = sp.value_load(pad_t[0:1, bass.ds(e, 1)], min_val=0, max_val=ROWS - P)
                sp.dma_start(m["xs"][bass.ds(r, P), :], zeros[:]).then_inc(s["padded"], 16)
            sp.wait_ge(s["padded"], EXPERTS * 16)
            sp.wait_ge(m["tail_zeroed"], TAIL * 16)

            def load(g, b):
                for j in range(GROUP):
                    r = sp.value_load(row_t[0:1, bass.ds(g * GROUP + j, 1)], min_val=0, max_val=ROWS - P)
                    sp.dma_start(xt[:, b, j, :], m["xs"][bass.ds(r, P), :]).then_inc(arrived[b], 16)

            load(0, 0)
            load(1, 1)
            with sp.Fori(1, N) as n:
                for b in range(2):
                    sp.wait_ge(s["xT_ps"], 2 * n + b - 1)
                    load(2 * n + b, b)
            sp.wait_ge(s["in_a"], N * GROUP * 16)
            sp.wait_ge(s["in_b"], N * GROUP * 16)

        @block.gpsimd
        def _(pool):
            nc.gpsimd.memset(place[:], 0.0)
            nc.gpsimd.memset(upto[:], 1.0).then_inc(s["step"], 1)
            pool.wait_ge(s["step"], 1)
            nc.gpsimd.affine_select(out=upto[:], in_=upto[:], compare_op=ALU.is_ge, fill=0.0, base=0,
                                    pattern=[[1, EXPERTS], [-1, EXPERTS]], channel_multiplier=0).then_inc(s["init"], 1)
            g = nc.gpsimd
            pool.wait_ge(s["planned"], 1)
            for e in range(1, EXPERTS):
                g.tensor_scalar(turn[:, e % 2], m["slots"][:], float(e * REGION), jump[:, e - 1:e], ALU.is_ge,
                                ALU.mult).then_inc(s["place"], 1)
                pool.wait_ge(s["place"], 2 * e - 1)
                g.tensor_tensor(place[:], place[:], turn[:, e % 2], ALU.add).then_inc(s["place"], 1)
                pool.wait_ge(s["place"], 2 * e)
            g.tensor_tensor(m["slots"][:], m["slots"][:], place[:], ALU.add)

        @block.vector
        def _(v):
            V = nc.vector
            n_ = [1]

            def step(ins):
                n_[0] += 1
                ins.then_inc(s["step"], 1)
                v.wait_ge(s["step"], n_[0])
            v.wait_ge(s["init"], 16 + 1)
            v.wait_ge(s["cnt_ps"], 1)
            step(V.tensor_copy(cnt[:], p_xy[0][:, 0:EXPERTS]))
            step(V.tensor_tensor(sq[:], cnt[:, :, None].broadcast_to([P, EXPERTS, EXPERTS]),
                                 m["tile_rows"][:, None, :].broadcast_to([P, EXPERTS, EXPERTS]), ALU.is_gt))
            step(V.tensor_reduce(ntile[:], sq[:], AX.X, ALU.add))
            step(V.tensor_scalar(jump[:], ntile[:], float(P), -float(REGION), ALU.mult, ALU.add))
            step(V.tensor_tensor(sq[:], upto[:], ntile[:, None, :].broadcast_to([P, EXPERTS, EXPERTS]), ALU.mult))
            step(V.tensor_reduce(cum[:], sq[:], AX.X, ALU.add))
            big = [P, MAX_TILES, EXPERTS]
            step(V.tensor_tensor(past[:], cum[:, None, :].broadcast_to(big), iota_t[:, :, None].broadcast_to(big),
                                 ALU.is_le))
            step(V.tensor_reduce(exp_t[:], past[:], AX.X, ALU.add))
            step(V.tensor_tensor(cost[:], past[:], ntile[:, None, :].broadcast_to(big), ALU.mult))
            step(V.tensor_reduce(skip_t[:], cost[:], AX.X, ALU.add))
            step(V.tensor_tensor(skip_t[:], iota_t[:], skip_t[:], ALU.subtract))
            step(V.tensor_scalar(skip_t[:], skip_t[:], float(P), None, ALU.mult))
            step(V.scalar_tensor_tensor(out=skip_t[:], in0=exp_t[:], scalar=float(REGION), in1=skip_t[:],
                                        op0=ALU.mult, op1=ALU.add))
            step(V.tensor_copy(row_t[:], skip_t[:]))
            step(V.tensor_scalar(w_t[:], exp_t[:], float(EXPERTS - 1), None, ALU.min))
            step(V.tensor_tensor(cnt[:], cnt[:], m["base_e"][:], ALU.add))
            step(V.tensor_copy(pad_t[:], cnt[:]))
            V.tensor_copy(cum[:], cnt[:]).then_inc(s["planned"], 1)
            with v.Fori(0, N) as n:
                for b in range(2):
                    v.wait_ge(s["act"], 2 * n + b + 1)
                    V.tensor_tensor(hid[:, b], act[:, b], p_up[b][:, :, 0:DFF], ALU.mult).then_inc(s["hid"], 1)
                for b in range(2):
                    v.wait_ge(s["hidT_ps"], 2 * n + b + 1)
                    V.tensor_copy(hidT[:, b], p_h[b][:].rearrange("p (j t) -> p j t", j=GROUP)).then_inc(s["hidT"], 1)
                for b in range(2):
                    v.wait_ge(s["y_ps"], 2 * n + b + 1)
                    v.wait_ge(s["used"], 2 * n + b + 1)
                    V.tensor_copy(yo[:, b], p_xy[b][:].rearrange("p (j t) -> p j t", j=GROUP)).then_inc(s["y"], 1)

        @block.scalar
        def _(act_):
            A = nc.scalar
            act_.wait_ge(s["planned"], 1)
            act_.sem_inc(s["used"], 2)
            with act_.Fori(0, N) as n:
                for b in range(2):
                    act_.wait_ge(s["xT_ps"], 2 * n + b + 1)
                    A.activation(xT[:, b], p_xy[b][:].rearrange("p (j t) -> p j t", j=GROUP), ACT.Copy,
                                 scale=m["norms"][:, 1:2]).then_inc(s["xT"], 1)
                for b in range(2):
                    act_.wait_ge(s["up_ps"], 2 * n + b + 1)
                    A.activation(act[:, b], p_up[b][:, :, DFF:2 * DFF], ACT.Silu).then_inc(s["act"], 1)
                for b in range(2):
                    act_.wait_ge(s["y"], 2 * n + b + 1)
                    act_.dma_start(m["ys"][bass.ds((2 * n + b) * (GROUP * P), GROUP * P), :]
                                   .rearrange("(j p) d -> p j d", p=P), yo[:, b]).then_inc(written[b], 16)
                for b in range(2):
                    act_.wait_ge(written[b], n * 16 + 16)
                    act_.sem_inc(s["used"], 1)

        @block.tensor
        def _(pe):
            mm, tr = nc.tensor.matmul, nc.tensor.transpose
            pe.wait_ge(m["moe_loaded"], MOE_LOADS * 16)
            mm(p_xy[0][:, 0:EXPERTS], m["ones_bf"][:], m["masksum"][:], start=True, stop=True) \
                .then_inc(s["cnt_ps"], 1)
            pe.wait_ge(s["planned"], 1)
            with pe.Fori(0, N) as n:
                w = []
                for b in range(2):
                    for j in range(GROUP):
                        w.append(pe.value_load(w_t[0:1, bass.ds((2 * n + b) * GROUP + j, 1)], min_val=0,
                                               max_val=EXPERTS - 1))
                for b in range(2):
                    pe.wait_ge(arrived[b], (n + 1) * (GROUP * 16))
                    for j in range(GROUP):
                        ins = tr(p_xy[b][:, j * P:(j + 1) * P], xt[:, b, j, :], ident[:])
                    ins.then_inc(s["xT_ps"], 1)
                    pe.wait_ge(s["xT"], 2 * n + b + 1)
                    for j in range(GROUP):
                        ins = mm(p_up[b][:, j, :], xT[:, b, j, :],
                                 m["wup"][:, bass.ds(w[b * GROUP + j] * (2 * DFF), 2 * DFF)], start=True, stop=True)
                    ins.then_inc(s["up_ps"], 1)
                for b in range(2):
                    pe.wait_ge(s["hid"], 2 * n + b + 1)
                    for j in range(GROUP):
                        ins = tr(p_h[b][:, j * P:(j + 1) * P], hid[:, b, j, :], ident[:])
                    ins.then_inc(s["hidT_ps"], 1)
                for b in range(2):
                    pe.wait_ge(s["hidT"], 2 * n + b + 1)
                    for j in range(GROUP):
                        ins = mm(p_xy[b][:, j * P:(j + 1) * P], hidT[:, b, j, :],
                                 m["wdown"][:, bass.ds(w[b * GROUP + j] * D, D)], start=True, stop=True)
                    ins.then_inc(s["y_ps"], 1)
                pe.wait_ge(s["y"], 2 * n + 2)


def combine(m):
    nc, x = m["nc"], m["x"]
    BUFS = 4
    with ExitStack() as ctx:
        def sb(name, shape, dt=F32):
            return ctx.enter_context(nc.sbuf_tensor(name, shape, dt))

        def sem(name):
            return ctx.enter_context(nc.semaphore("c_" + name))

        idx = sb("c_idx", [P, TILES * TOPK], U32)
        rows = sb("c_rows", [P, BUFS, TOPK, D])
        acc = sb("c_acc", [P, BUFS, D])
        gathered = [sem(f"gathered{b}") for b in range(BUFS)]
        written = [sem(f"written{b}") for b in range(BUFS)]
        ready, part, summed = sem("ready"), sem("part"), sem("summed")
        block = ctx.enter_context(nc.Block())

        @block.gpsimd
        def _(pool):
            pool.wait_ge(ready, 1)
            for t in range(TILES):
                b = t % BUFS
                if t >= BUFS:
                    pool.wait_ge(part, TOPK * (t - BUFS + 1))
                for k in range(TOPK):
                    nc.gpsimd.indirect_dma_start(rows[:, b, k, :], None, m["ys"], bass.IndirectOffsetOnAxis(
                        ap=idx[:, t * TOPK + k:t * TOPK + k + 1], axis=0)).then_inc(gathered[b], 16)

        @block.vector
        def _(v):
            V = nc.vector
            V.tensor_copy(idx[:].rearrange("p (t k) -> p t k", t=TILES), m["slots"][:]).then_inc(ready, 1)
            with v.Fori(0, TILES // BUFS) as n:
                for b in range(BUFS):
                    v.wait_ge(gathered[b], (n + 1) * (TOPK * 16))
                    v.wait_ge(written[b], n * 16 + 16)
                    t = n * BUFS + b
                    for k in range(TOPK):
                        base = x[:, bass.ds(t, 1), :].squeeze(1) if k == 0 else acc[:, b, :]
                        if k:
                            v.wait_ge(part, n * (BUFS * TOPK) + b * TOPK + k)
                        V.scalar_tensor_tensor(out=acc[:, b, :], in0=rows[:, b, k, :],
                                               scalar=m["weights"][:, bass.ds(t, 1), k], in1=base,
                                               op0=ALU.mult, op1=ALU.add).then_inc(part, 1)

        @block.sync
        def _(sp):
            for b in range(BUFS):
                sp.sem_inc(written[b], 16)
            out = m["out"]
            with sp.Fori(0, TILES // BUFS) as n:
                for b in range(BUFS):
                    sp.wait_ge(part, n * (BUFS * TOPK) + (b + 1) * TOPK)
                    sp.dma_start(out[bass.ds((n * BUFS + b) * P, P), :], acc[:, b, :]).then_inc(written[b], 16)
            for b in range(BUFS):
                sp.wait_ge(written[b], (TILES // BUFS + 1) * 16)


def _layout(v):
    import numpy as np
    g = {k: np.ascontiguousarray(x) for k, x in v.items()}
    heads = [h for p in range(PAIRS) for h in pair_heads(p)]
    split = np.concatenate([np.arange(0, DH, 2), np.arange(1, DH, 2)])
    cols = np.concatenate([h * DH + split for h in heads] + [(HEADS + g_) * DH + split for g_ in range(KV)]
                          + [np.arange((HEADS + KV) * DH, QKV)])
    rows = np.concatenate([h * DH + np.arange(DH) for h in heads])
    f = np.float32
    freq = (f(1.0) / f(150000.0) ** (np.arange(0, DH, 2, dtype=f) / f(DH))).astype(f)
    angle = (np.arange(TOK, dtype=f) / f(32.0))[:, None] * freq[None, :]
    i, j = np.arange(P)[:, None], np.arange(P)[None, :]
    neg = f(-1e30)
    sink = g["L0_ffn_attn_sink"][heads].reshape(PAIRS, 2)
    return {
        "x": g["L0_attn_in_seq"].reshape(SEQS * TOK, D),
        "tkT": g["L0_attn_t_k"].T, "tvT": g["L0_attn_t_v"].T, "tqT": g["L0_attn_t_q"].T,
        "W1T": g["L0_attn_W1"].T, "b1": g["L0_attn_b1"].reshape(HID, 1),
        "W2": g["L0_attn_W2"], "W2T": g["L0_attn_W2"].T, "b2": g["L0_attn_b2"].reshape(1, D),
        "norms": np.stack([g["L0_ffn_attn_norm_w"], g["L0_ffn_ffn_norm_w"]], 1),
        "wqkv": g["L0_ffn_qkv_w"][:, cols], "wproj": g["L0_ffn_proj_w"][rows],
        "bias": np.concatenate([g["L0_ffn_qkv_b"][cols], g["L0_ffn_proj_b"], g["L0_ffn_gate_b"]]),
        "sink": sink.reshape(-1),
        "gate": g["L0_ffn_gate_w"], "wup": g["L0_ffn_W_up"], "wdown": g["L0_ffn_W_down"],
        "ident": np.eye(P, dtype=f),
        "mask": np.concatenate([np.where(j >= i, f(0), neg), np.where(j <= i, f(0), neg)], 1).astype(f),
        "before": (i < j).astype(f),
        "rope": np.stack([np.cos(angle), np.sin(angle)], 1).astype(f),
        "iota_e": np.arange(EXPERTS, dtype=f), "iota_t": np.arange(MAX_TILES, dtype=f),
        "pad_e": (np.arange(EXPERTS) * REGION).astype(f),
    }


def kernel(**inputs):
    import numpy as np
    import concourse.bacc as bacc
    from concourse.bass_utils import run_bass_kernel_spmd

    nc = bacc.Bacc("TRN2", target_bir_lowering=False, num_devices=1)
    arrays = {"in_" + k: np.ascontiguousarray(v) for k, v in _layout(inputs).items()}
    a = {k[3:]: nc.dram_tensor(k, v.shape, mybir.dt.from_np(v.dtype), kind="ExternalInput").ap()
         for k, v in arrays.items()}
    out = nc.dram_tensor("out_x", [SEQS * TOK, D], F32, kind="ExternalOutput").ap()
    program(nc, a, out)
    r = run_bass_kernel_spmd(nc, [arrays], core_ids=[0])
    return r.results[0]["out_x"].reshape(SEQS, TOK, D)
```

```python
from contextlib import ExitStack

import concourse.bass as bass
import concourse.mybir as mybir

F32 = mybir.dt.float32
BF16 = mybir.dt.bfloat16
I32 = mybir.dt.int32
U32 = mybir.dt.uint32
ALU = mybir.AluOpType
ACT = mybir.ActivationFunctionType
AX = mybir.AxisListType

P = 128
SEQS, TOK, D = 16, 256, 128
TPS = TOK // P
TILES = SEQS * TPS
HID = 32
LR = 0.001
GRAD_SCALE = -LR * 2.0 / (TOK * D)
HEADS, KV, DH = 16, 4, 64
PAIRS = HEADS // 2
HALF = DH // 2
QKV = (HEADS + 2 * KV) * DH
UNITS = 12
CHUNKS = 3 * TPS
EXPERTS, TOPK, DFF = 32, 4, 128
EPS = 1e-5
TINY = 1e-30
INV_SQRT_2PI = 0.3989422804014327
REGION = SEQS * TOK + P
MAX_TILES = 160
COLS = -(-MAX_TILES // P)
WIDE = D + 3 * TOPK
GROUP = 4
GROUPS = MAX_TILES // GROUP
TAIL = MAX_TILES - SEQS * TOK * TOPK // P
SPARE = MAX_TILES * P
ROWS = EXPERTS * REGION + TAIL * P


def tiles(ap):
    return ap.rearrange("p (t d) -> p t d", t=TPS)


def hold(eng, sem, value, held):
    eng.wait_ge(sem, value)
    eng.sem_inc(held, 1)


def after(eng, sem, value):
    if not isinstance(value, int) or value > 0:
        eng.wait_ge(sem, value)


def pair_heads(p):
    g2, j = p // 4, p % 4
    return (2 * g2) * 4 + j, (2 * g2 + 1) * 4 + j


def unit(u):
    j, kind = u // 3, u % 3
    if kind < 2:
        p = 2 * j + kind
        return [p], True, slice(2 * p, 2 * p + 2)
    return [2 * j, 2 * j + 1], False, slice(4 * j, 4 * j + 4)


def program(nc, a, out):
    with ExitStack() as ctx:
        def sb(name, shape, dt=F32):
            return ctx.enter_context(nc.sbuf_tensor(name, shape, dt))

        m = {"nc": nc, "a": a, "out": out}
        m["x"] = sb("x_all", [P, TILES, D])
        m["ident"] = sb("ident_sb", [P, P])
        m["ident_bf"] = sb("ident_bf", [P, P], BF16)
        m["mask2"] = sb("mask2", [P, 2, 2 * P], BF16)
        m["mask1"] = sb("mask1", [P, 4, P], BF16)
        m["before"] = sb("before_bf", [P, P], BF16)
        m["ones_bf"] = sb("ones_bf", [P, P], BF16)
        m["rope"] = sb("rope_sb", [P, TPS, 2, HALF])
        m["neghalf"] = sb("neghalf", [P, TILES])
        m["wqkv"] = sb("wqkv_sb", [P, QKV])
        m["wproj"] = sb("wproj_sb", [P, PAIRS, D])
        m["norms"] = sb("norms_sb", [P, 2])
        m["gate"] = sb("gate_sb", [P, EXPERTS])
        m["bias3"] = sb("bias3_bf", [3, QKV + D + EXPERTS], BF16)
        m["negsink"] = sb("negsink", [P, HEADS])
        m["wup"] = sb("wup_sb", [P, EXPERTS * 2 * DFF])
        m["wdown"] = sb("wdown_sb", [P, EXPERTS * D])
        m["masksum"] = sb("masksum", [P, EXPERTS], BF16)
        m["iota_e"] = sb("iota_e", [P, EXPERTS])
        m["base_e"] = sb("base_e", [P, EXPERTS])
        m["pick_row"] = sb("pick_row", [P, TILES, TOPK])
        m["row_id"] = sb("row_id", [P, MAX_TILES])
        m["tile_id"] = sb("tile_id", [P, COLS])
        m["digits"] = sb("digits", [P, P // GROUP])
        m["ones"] = sb("ones", [P, P])
        m["fast"] = sb("fast", [P, 2 * HID])
        m["fast2"] = sb("fast2", [HID + 1, P])
        m["b1"] = sb("b1_sb", [HID, 1])
        m["tkT"], m["tvT"], m["tqT"] = sb("tkT_sb", [P, P]), sb("tvT_sb", [P, P]), sb("tqT_sb", [P, P])
        m["xs"] = nc.dram_tensor("expert_rows", [ROWS, WIDE], F32, kind="Internal").ap()
        m["ys"] = nc.dram_tensor("expert_out", [SPARE + SEQS * TOK * TOPK, D], F32, kind="Internal").ap()
        for n in ("attn_loaded", "moe_loaded", "tail_zeroed"):
            m[n] = ctx.enter_context(nc.semaphore(n))
        m["zeros"] = sb("zeros", [P, WIDE])
        prepare(m)
        layers(m)
        experts(m)
        combine(m)


ATTN_LOADS, MOE_LOADS = 4, 2


def prepare(m):
    nc, a = m["nc"], m["a"]
    with ExitStack() as ctx:
        def sb(name, shape, dt=F32):
            return ctx.enter_context(nc.sbuf_tensor(name, shape, dt))

        def sem(name):
            return ctx.enter_context(nc.semaphore(name))
        NB = QKV + D + EXPERTS
        mask_f = sb("mask_f", [P, 2 * P])
        before_f = sb("before_f", [P, P])
        b3, rest = sb("b3", [3, NB]), sb("rest", [3, NB])
        part, pick = sb("part", [3, NB], BF16), sb("pick", [3, NB], BF16)
        loaded, step_done, filled = sem("p_loaded"), sem("p_step"), sem("p_filled")
        block = ctx.enter_context(nc.Block())
        small = [
            (m["x"][:, 0:8, :], a["x"][0:8 * P, :].rearrange("(t p) d -> p t d", p=P)),
            (m["ident"][:], a["ident"]),
            (m["tkT"][:], a["tkT"]), (m["tvT"][:], a["tvT"]), (m["tqT"][:], a["tqT"]),
            (m["fast"][:, 0:HID], a["W1T"]), (m["fast"][:, HID:], a["W2"]),
            (m["fast2"][0:HID, :], a["W2T"]), (m["fast2"][HID:HID + 1, :], a["b2"]), (m["b1"][:], a["b1"]),
            (m["x"][:, 8:, :], a["x"][8 * P:, :].rearrange("(t p) d -> p t d", p=P)),
            (mask_f[:], a["mask"]),
            (before_f[:], a["before"]),
            (b3[:], a["bias"].partition_broadcast(3)),
            (m["negsink"][:], a["sink"].partition_broadcast(P)),
            (m["iota_e"][:], a["iota_e"].partition_broadcast(P)),
            (m["pick_row"][:], a["pick_row"].rearrange("(t p) k -> p t k", p=P)),
            (m["row_id"][:], a["row_id"]),
            (m["tile_id"][:], a["tile_id"]),
            (m["digits"][:], a["digits"]),
        ]
        attn = [
            (m["rope"][:], a["rope"].rearrange("(t p) c f -> p t c f", p=P)),
            (m["norms"][:], a["norms"]),
            (m["wqkv"][:], a["wqkv"]),
            (m["wproj"][:], a["wproj"].rearrange("(c p) d -> p c d", p=P)),
        ]
        moe = [
            (m["wup"][:].rearrange("p (e f) -> p e f", e=EXPERTS), a["wup"].rearrange("e d f -> d e f")),
            (m["wdown"][:].rearrange("p (e f) -> p e f", e=EXPERTS), a["wdown"].rearrange("e d f -> d e f")),
        ]
        assert len(attn) == ATTN_LOADS and len(moe) == MOE_LOADS

        @block.sync
        def _(sp):
            for dst, src in small + [(m["gate"][:], a["gate"])]:
                sp.dma_start(dst, src).then_inc(loaded, 16)
            for dst, src in attn:
                sp.dma_start(dst, src).then_inc(m["attn_loaded"], 16)
            for dst, src in moe:
                sp.dma_start(dst, src).then_inc(m["moe_loaded"], 16)
            sp.wait_ge(filled, 1)
            for j in range(TAIL):
                row = EXPERTS * REGION + j * P
                sp.dma_start(m["xs"][row:row + P, :], m["zeros"][:]).then_inc(m["tail_zeroed"], 16)
            sp.wait_ge(loaded, 16 * (len(small) + 1))

        @block.gpsimd
        def _(pool):
            nc.gpsimd.memset(m["zeros"][:], 0.0).then_inc(filled, 1)
            nc.gpsimd.memset(m["neghalf"][:], -0.5)
            nc.gpsimd.memset(m["ones_bf"][:], 1.0)
            nc.gpsimd.memset(m["ones"][:], 1.0)
            nc.gpsimd.memset(m["masksum"][:], 0.0)

        @block.vector
        def _(v):
            V, n = nc.vector, [0]

            def step(ins):
                n[0] += 1
                ins.then_inc(step_done, 1)
                v.wait_ge(step_done, n[0])
            v.wait_ge(loaded, 16 * (len(small) + 1))
            V.tensor_copy(m["ident_bf"][:], m["ident"][:])
            V.tensor_copy(m["before"][:], before_f[:])
            V.tensor_copy(m["mask2"][:], mask_f[:, None, :].broadcast_to([P, 2, 2 * P]))
            V.tensor_copy(m["mask1"][:], mask_f[:, None, P:].broadcast_to([P, 4, P]))
            V.tensor_scalar(m["base_e"][:], m["iota_e"][:], float(REGION), None, ALU.mult)
            V.tensor_scalar(m["negsink"][:], m["negsink"][:], -1.0, None, ALU.mult)
            step(V.tensor_copy(part[:], b3[:]))
            step(V.tensor_scalar(m["bias3"][:], part[:], m["ident"][0:3, 0:1], None, ALU.mult))
            src, dst = b3, rest
            for r in range(1, 3):
                step(V.tensor_tensor(dst[:], src[:], part[:], ALU.subtract))
                step(V.tensor_copy(part[:], dst[:]))
                step(V.tensor_scalar(pick[:], part[:], m["ident"][0:3, r:r + 1], None, ALU.mult))
                step(V.tensor_tensor(m["bias3"][:], m["bias3"][:], pick[:], ALU.add))
                src, dst = dst, src


def layers(m):
    nc, x, ident = m["nc"], m["x"], m["ident"]
    fast, fast2, b1 = m["fast"], m["fast2"], m["b1"]
    with ExitStack() as ctx:
        def sb(name, shape, dt=F32):
            return ctx.enter_context(nc.sbuf_tensor("l_" + name, shape, dt))

        def ps(name):
            return ctx.enter_context(nc.psum_tensor("l_" + name, [P, 512], F32))

        dkvT = sb("dkvT", [P, P])
        stats0, mv0, rstd0 = sb("stats0", [P, TILES, 6]), sb("mv0", [P, TILES, 2]), sb("rstd0", [P, TILES])
        xn, xnT = sb("xn", [P, TPS, D]), sb("xnT", [P, 2, TOK])
        zT, z = sb("zT", [P, 2, TOK]), sb("z", [P, TPS, D])
        aT, hT2 = sb("aT", [HID, 2, TOK]), sb("hT2", [HID + 1, 2, TOK])
        h, r, rT = sb("h", [P, TPS, HID + 1]), sb("r", [P, TPS, D]), sb("rT", [P, TOK])
        a_tok, expo, tanh, num, den, inv, cdf, apdf, da = (
            sb(n, [P, TPS, HID]) for n in "a_tok expo tanh num den inv cdf apdf da".split())
        warm = sb("warm", [1, 1])
        stats, mv = sb("stats", [P, TPS, 6]), sb("mv", [P, TPS, 2])
        mean_all, rs_all = sb("mean_all", [P, TILES]), sb("rs_all", [P, TILES])
        rs, sq, rms = sb("rs", [P, TPS]), sb("sq", [P, TPS]), sb("rms", [P, TPS])
        hn, hT = sb("hn", [P, TPS, D]), sb("hT", [P, TOK])
        t_cos, t_sin = sb("t_cos", [P, 512]), sb("t_sin", [P, 512])
        qT = sb("qT", [P, 2, PAIRS, TOK])
        kpad = sb("kpad", [P, 2, 2, 2, TOK])
        vv = sb("vv", [P, 2, TPS, KV * DH])
        mx, nm, es, sums, rec = (sb(n, [P, 2, 4]) for n in "mx nm es sums rec".split())
        prob, probT = sb("prob", [P, 2, 512]), sb("probT", [P, 2, 512])
        yT = sb("yT", [P, 2, PAIRS, TOK])
        xx, x2, x2sq = (sb(n, [P, TPS, D]) for n in "xx x2 x2sq".split())
        h2 = sb("h2", [P, 2, TPS, WIDE])
        ss, h2T = sb("ss", [P, TPS]), sb("h2T", [P, TOK])
        glog, top, idx = sb("glog", [P, TPS, EXPERTS]), sb("top", [P, TPS, 8]), sb("idx", [P, TPS, 8], U32)
        idxf, ntop, wsum = sb("idxf", [P, TPS, 8]), sb("ntop", [P, TPS]), sb("wsum", [P, TPS])
        wexp, wrec = sb("wexp", [P, TPS, TOPK]), sb("wrec", [P, TPS])
        hot, prod = sb("hot", [P, TPS, TOPK, EXPERTS]), sb("prod", [P, TPS, TOPK, EXPERTS])
        picked, place = sb("picked", [P, TPS, EXPERTS], BF16), sb("place", [P, TPS, EXPERTS])
        slot = sb("slot", [P, 2, TPS * TOPK], U32)
        score = [ps(f"score{i}") for i in range(3)]
        turned = [ps(f"turned{i}") for i in range(2)]
        side_q, side_f, side_g = ps("side_q"), ps("side_f"), ps("side_g")
        names = (
            "ready stat0 rs0 xn xT_ps xT z_ps zT a_ps aT az_ps a_tok z expo gelu tanh slope apdf sloped "
            "rT_ps rT hr_ps h r dh_ps da g_ps w out_ps x1 "
            "stat small norms hn hn_ps hT qkv_ps cos sin added qk_ps qk_out v_out "
            "s_ps mx nm es_in exped den rec normed t_ps probT y_ps yT "
            "proj_ps xx x2 ss rms2 h2 h2_ps h2T gate_ps glog top w_in wexp wrec idx idxf hot picked rank_ps "
            "place prod masksum slotf slot sent_a sent_b x_sum held_v held_p").split()
        s = {n: ctx.enter_context(nc.semaphore("l_" + n)) for n in names}
        sent = [s["sent_a"], s["sent_b"]]
        block = ctx.enter_context(nc.Block())
        FIRST, LAST = 6, SEQS - 3

        def live(k):
            return not isinstance(k, int) or 0 <= k < SEQS

        def run(eng, iteration):
            for n in range(FIRST):
                iteration(n, n % 2)
            with eng.Fori(0, (LAST + 1 - FIRST) // 2) as j:
                for par in range(2):
                    iteration(j * 2 + (FIRST + par), par)
            for n in range(LAST + 1, SEQS + 5):
                iteration(n, n % 2)

        def tile_of(q, t):
            return bass.ds(q * TPS + t, 1)

        def at_unit(n, par, u):
            A, p = n - 3, (par + 1) % 2
            if u >= UNITS:
                A, p, u = A + 1, 1 - p, u - UNITS
            elif u < 0:
                A, p, u = A - 1, 1 - p, u + UNITS
            return A, p, u, A * UNITS + (u + 1)

        @block.tensor
        def _(pe):
            mm, tr = nc.tensor.matmul, nc.tensor.transpose

            def bias(dst, c0, c1):
                mm(dst, m["ones_bf"][0:3, :], m["bias3"][:, c0:c1], start=True, stop=False)

            def scores(n, par, u):
                A, ap, u, done = at_unit(n, par, u)
                if not live(A):
                    return
                pairs, second, _ = unit(u)
                g2 = pairs[0] // 4
                dst = score[u % 3]
                if u == 0:
                    pe.wait_ge(s["qk_out"], A * CHUNKS + 4)
                if u == 6:
                    pe.wait_ge(s["qk_out"], A * CHUNKS + CHUNKS)
                after(pe, s["exped"], done - 3)
                if second:
                    mm(dst[:], m["ident_bf"][:], m["mask2"][:], start=True, stop=False)
                    mm(dst[:], qT[:, ap, pairs[0], P:TOK], kpad[:, ap, g2, :, :], start=False, stop=True) \
                        .then_inc(s["s_ps"], 1)
                else:
                    mm(dst[:], m["ident_bf"][:], m["mask1"][:], start=True, stop=False)
                    for k, p in enumerate(pairs):
                        ins = mm(dst[:, k * 2 * P:(k + 1) * 2 * P], qT[:, ap, p, 0:P], kpad[:, ap, g2, :, 0:P],
                                 start=False, stop=(k == 1))
                    ins.then_inc(s["s_ps"], 1)

            def turn_probs(n, par, u):
                A, ap, u, done = at_unit(n, par, u)
                if not live(A):
                    return
                after(pe, s["yT"], done - 2)
                pe.wait_ge(s["normed"], done)
                for k in range(4):
                    ins = tr(turned[u % 2][:, k * P:(k + 1) * P], prob[:, u % 2, k * P:(k + 1) * P], ident[:])
                ins.then_inc(s["t_ps"], 1)

            def values(n, par, u):
                A, ap, u, done = at_unit(n, par, u)
                if not live(A):
                    return
                pairs, second, _ = unit(u)
                g2 = pairs[0] // 4
                pe.wait_ge(s["probT"], done)
                for k in range(2):
                    for hh in range(2):
                        g = 2 * g2 + hh
                        blk = 2 * hh + k if second else 2 * k + hh
                        dst = turned[u % 2][hh * DH:(hh + 1) * DH, 0:P] if second else \
                            turned[u % 2][hh * DH:(hh + 1) * DH, k * P:(k + 1) * P]
                        ins = mm(dst, vv[:, ap, k if second else 0, g * DH:(g + 1) * DH],
                                 probT[:, u % 2, blk * P:(blk + 1) * P],
                                 start=(k == 0 or not second), stop=(k == 1 or not second))
                ins.then_inc(s["y_ps"], 1)

            def x_turn(n, par):
                F = n
                if not live(F):
                    return
                after(pe, s["hT"], n - 1)
                pe.wait_ge(s["xn"], F * TPS + TPS)
                for t in range(TPS):
                    ins = tr(side_f[:, t * P:(t + 1) * P], xn[:, t, :], ident[:])
                ins.then_inc(s["xT_ps"], 1)

            def z_products(n, par):
                F, O = n, n - 1
                if not (live(F) or live(O)):
                    return
                if live(F):
                    pe.wait_ge(s["xT"], F + 1)
                    ins = mm(side_f[:, 0:TOK], m["tkT"][:], xnT[:, par, :], start=True, stop=True)
                else:
                    pe.wait_ge(s["hT"], O)
                if live(O):
                    ins = mm(side_f[:, TOK:], m["tqT"][:], xnT[:, 1 - par, :], start=True, stop=True)
                ins.then_inc(s["z_ps"], 1)

            def a_products(n, par):
                F, O = n, n - 1
                if not (live(F) or live(O)):
                    return
                pe.wait_ge(s["zT"], n + 1)
                after(pe, s["w"], 3 * n)
                if live(F):
                    ins = mm(side_f[0:HID, 0:TOK], fast[:, 0:HID], zT[:, 0, :], start=True, stop=True)
                if live(O):
                    ins = mm(side_f[0:HID, TOK:], fast[:, 0:HID], zT[:, 1, :], start=True, stop=True)
                ins.then_inc(s["a_ps"], 1)

            def z_rows(n, par):
                F = n
                if not live(F):
                    return
                pe.wait_ge(s["aT"], n + 1)
                for t in range(TPS):
                    mm(side_f[:, P + t * P:P + (t + 1) * P], xnT[:, par, t * P:(t + 1) * P], m["tkT"][:],
                       start=True, stop=True)
                for t in range(TPS):
                    ins = tr(side_f[:, t * HID:(t + 1) * HID], aT[:, 0, t * P:(t + 1) * P], ident[0:HID, 0:HID])
                ins.then_inc(s["az_ps"], 1)

            def residual_cols(n, par):
                F = n
                if not live(F):
                    return
                pe.wait_ge(s["a_tok"], F + 1)
                pe.wait_ge(s["z"], F + 1)
                mm(side_f[:, 0:TOK], dkvT[:], xnT[:, par, :], start=True, stop=False)
                pe.wait_ge(s["gelu"], n + 1)
                mm(side_f[:, 0:TOK], fast2[:], hT2[:, 0, :], start=False, stop=True).then_inc(s["rT_ps"], 1)

            def residual_rows(n, par):
                F = n
                if not live(F):
                    return
                pe.wait_ge(s["rT"], F + 1)
                for t in range(TPS):
                    dst, tok = side_f[:, P + t * P:P + (t + 1) * P], slice(t * P, (t + 1) * P)
                    mm(dst, xnT[:, par, tok], dkvT[:], start=True, stop=False)
                    mm(dst, hT2[:, 0, tok], fast2[:], start=False, stop=True)
                for t in range(TPS):
                    ins = tr(side_f[:, t * (HID + 1):(t + 1) * (HID + 1)], hT2[:, 0, t * P:(t + 1) * P],
                             ident[0:HID + 1, 0:HID + 1])
                ins.then_inc(s["hr_ps"], 1)

            def hidden_grad(n, par):
                F = n
                if not live(F):
                    return
                pe.wait_ge(s["h"], F + 1)
                pe.wait_ge(s["r"], F + 1)
                for t in range(TPS):
                    ins = mm(side_f[:, t * HID:(t + 1) * HID], rT[:, t * P:(t + 1) * P], fast[:, HID:],
                             start=True, stop=True)
                ins.then_inc(s["dh_ps"], 1)

            def output(n, par):
                O = n - 1
                if not live(O):
                    return
                after(pe, s["da"], n + 1 if live(n) else 0)
                if not live(n):
                    pe.wait_ge(s["gelu"], n + 1)
                for t in range(TPS):
                    dst, tok = side_f[:, t * P:(t + 1) * P], slice(t * P, (t + 1) * P)
                    mm(dst, xnT[:, 1 - par, tok], m["tqT"][:], start=True, stop=False)
                    ins = mm(dst, hT2[:, 1, tok], fast2[:], start=False, stop=True)
                ins.then_inc(s["out_ps"], 1)

            def gradients(n, par):
                F, B = n, n - 4
                if not live(F):
                    return
                pe.wait_ge(s["da"], F + 1)
                after(pe, s["place"], B + 1)
                for t in range(TPS):
                    mm(side_g[:, HID:2 * HID], r[:, t, :], h[:, t, 0:HID], start=(t == 0), stop=(t == TPS - 1))
                for t in range(TPS):
                    mm(side_g[0:HID + 1, P:2 * P], h[:, t, :], r[:, t, :], start=(t == 0), stop=(t == TPS - 1))
                for t in range(TPS):
                    mm(side_g[:, 0:HID], z[:, t, :], da[:, t, :], start=(t == 0), stop=(t == TPS - 1))
                for t in range(TPS):
                    ins = mm(side_g[0:HID, 2 * P:2 * P + 1], da[:, t, :], h[:, t, HID:HID + 1],
                             start=(t == 0), stop=(t == TPS - 1))
                ins.then_inc(s["g_ps"], 1)

            def norm_turn(n, par):
                O = n - 1
                if not live(O):
                    return
                pe.wait_ge(s["x1"], O + 1)
                pe.wait_ge(s["hn"], O * TPS + TPS)
                for t in range(TPS):
                    ins = tr(side_f[:, t * P:(t + 1) * P], hn[:, t, :], ident[:])
                ins.then_inc(s["hn_ps"], 1)

            def qkv(n, par, c):
                N = n - 2
                if not live(N):
                    return
                t, part = c % 2, (2, 0, 1)[c // 2]
                if c == 0:
                    pe.wait_ge(s["hT"], N + 1)
                after(pe, s["qk_out"], N * CHUNKS + c)
                bias(side_q[:], part * 512, (part + 1) * 512)
                mm(side_q[:], hT[:, t * P:(t + 1) * P], m["wqkv"][:, part * 512:(part + 1) * 512],
                   start=False, stop=True).then_inc(s["qkv_ps"], 1)

            def qk_turn(n, par, c):
                N = n - 2
                if not live(N):
                    return
                if c < 2:
                    pe.wait_ge(s["v_out"], N * TPS + c + 1)
                pe.wait_ge(s["added"], N * CHUNKS + c + 1)
                for k in range(2 if c < 2 else 4):
                    ins = tr(side_q[:, k * P:(k + 1) * P], t_cos[:, k * P:(k + 1) * P], ident[:])
                ins.then_inc(s["qk_ps"], 1)

            def project(n, par, t):
                B = n - 4
                cols = slice(t * P, (t + 1) * P)
                bias(side_g[:, cols], QKV, QKV + D)
                for p in range(PAIRS):
                    ins = mm(side_g[:, cols], yT[:, par, p, cols], m["wproj"][:, p, :], start=False,
                             stop=(p == PAIRS - 1))
                ins.then_inc(s["proj_ps"], 1)

            def project_second(n, par):
                B = n - 4
                if not live(B):
                    return
                after(pe, s["w"], 3 * (n if live(n - 1) else 0))
                pe.wait_ge(s["yT"], B * UNITS + UNITS - 1)
                project(n, par, 1)

            def project_first(n, par):
                B = n - 4
                if not live(B):
                    return
                pe.wait_ge(s["yT"], B * UNITS + UNITS)
                project(n, par, 0)

            def h2_turn(n, par):
                B = n - 4
                if not live(B):
                    return
                pe.wait_ge(s["h2"], B * TPS + TPS)
                for t in range(TPS):
                    ins = tr(side_g[:, t * P:(t + 1) * P], h2[:, par, t, 0:D], ident[:])
                ins.then_inc(s["h2_ps"], 1)

            def gate(n, par):
                B = n - 4
                if not live(B):
                    return
                pe.wait_ge(s["h2T"], B + 1)
                for t in range(TPS):
                    cols = slice(t * EXPERTS, (t + 1) * EXPERTS)
                    bias(side_g[:, cols], QKV + D, QKV + D + EXPERTS)
                    ins = mm(side_g[:, cols], h2T[:, t * P:(t + 1) * P], m["gate"][:], start=False, stop=True)
                ins.then_inc(s["gate_ps"], 1)

            def ranks(n, par):
                B = n - 4
                if not live(B):
                    return
                pe.wait_ge(s["picked"], B * TPS + TPS)
                for t in range(TPS):
                    cols = slice(t * EXPERTS, (t + 1) * EXPERTS)
                    mm(side_g[:, cols], m["ones_bf"][:], m["masksum"][:], start=True, stop=False)
                    if t == 1:
                        mm(side_g[:, cols], m["ones_bf"][:], picked[:, 0, :], start=False, stop=False)
                    ins = mm(side_g[:, cols], m["before"][:], picked[:, t, :], start=False, stop=True)
                ins.then_inc(s["rank_ps"], 1)

            side = {0: [x_turn], 1: [z_products, project_second], 2: [a_products, project_first], 3: [z_rows],
                    5: [residual_cols, h2_turn], 6: [residual_rows, gate], 7: [hidden_grad], 8: [output],
                    9: [ranks], 11: [norm_turn, gradients]}

            def iteration(n, par):
                for u in range(UNITS):
                    scores(n, par, u + 2)
                    if u % 2 == 0:
                        qkv(n, par, u // 2)
                    values(n, par, u - 1)
                    if u % 2 == 1:
                        qk_turn(n, par, u // 2)
                    for stage in side.get(u, []):
                        stage(n, par)
                    turn_probs(n, par, u)

            pe.wait_ge(s["ready"], 4)
            pe.wait_ge(m["attn_loaded"], ATTN_LOADS * 16)
            run(pe, iteration)

        @block.vector
        def _(v):
            V = nc.vector

            def softmax(n, par, u):
                A, ap, u0, done = at_unit(n, par, u)
                A1, ap1, u1, done1 = at_unit(n, par, u + 2)
                if live(A):
                    cols = unit(u0)[2]
                    b, w = u0 % 2, cols.stop - cols.start
                    v.wait_ge(s["exped"], done)
                    V.tensor_tensor(sums[:, b, 0:w], sums[:, b, 0:w], es[:, b, 0:w], ALU.add).then_inc(s["den"], 1)
                if live(A1):
                    cols1 = unit(u1)[2]
                    b1_, w1 = u1 % 2, cols1.stop - cols1.start
                    sink = m["negsink"][:, cols1]
                    v.wait_ge(s["s_ps"], done1)
                    V.tensor_reduce(mx[:, b1_, 0:w1], score[u1 % 3][:].rearrange("p (h k) -> p h k", h=w1), AX.X,
                                    ALU.max).then_inc(s["mx"], 1)

                if live(A):
                    v.wait_ge(s["den"], done)
                    V.reciprocal(rec[:, b, 0:w], sums[:, b, 0:w]).then_inc(s["rec"], 1)
                if live(A1):
                    v.wait_ge(s["mx"], done1)
                    V.scalar_tensor_tensor(out=nm[:, b1_, 0:w1], in0=mx[:, b1_, 0:w1], scalar=-0.125, in1=sink,
                                           op0=ALU.mult, op1=ALU.min).then_inc(s["nm"], 1)
                if live(A):
                    v.wait_ge(s["rec"], done)
                    k = 512 // w
                    for j in range(w):
                        ins = V.tensor_scalar(prob[:, b, j * k:(j + 1) * k], prob[:, b, j * k:(j + 1) * k],
                                              rec[:, b, j:j + 1], None, ALU.mult)
                    ins.then_inc(s["normed"], 1)
                if live(A1):
                    v.wait_ge(s["nm"], done1)
                    V.tensor_tensor(es[:, b1_, 0:w1], nm[:, b1_, 0:w1], sink, ALU.subtract).then_inc(s["es_in"], 1)

            def x_norm(n, par):
                F = n + 1
                if not live(F):
                    return
                after(v, s["xT_ps"], F)
                for t in range(TPS):
                    V.tensor_scalar(xn[:, t, :], x[:, tile_of(F, t), :].squeeze(1), mv0[:, tile_of(F, t), 0],
                                    rstd0[:, tile_of(F, t)], ALU.subtract, ALU.mult).then_inc(s["xn"], 1)

            def a_bias(n, par):
                F, O = n, n - 1
                if not (live(F) or live(O)):
                    return
                lo, hi = (0 if live(F) else TOK), (512 if live(O) else TOK)
                v.wait_ge(s["a_ps"], n + 1)
                V.tensor_scalar(aT[:].rearrange("p a t -> p (a t)")[:, lo:hi], side_f[0:HID, lo:hi], b1[:], TINY,
                                ALU.add, ALU.add).then_inc(s["aT"], 1)

            def a_rows(n, par):
                F = n
                if not live(F):
                    return
                v.wait_ge(s["az_ps"], F + 1)
                V.tensor_copy(a_tok[:], tiles(side_f[:, 0:TPS * HID])).then_inc(s["a_tok"], 1)
                V.tensor_copy(z[:], tiles(side_f[:, P:P + TOK])).then_inc(s["z"], 1)
                v.wait_ge(s["a_tok"], F + 1)
                V.scalar_tensor_tensor(out=expo[:], in0=a_tok[:], scalar=0.25, in1=a_tok[:],
                                       op0=ALU.mult, op1=ALU.mult).then_inc(s["expo"], 1)
                V.reciprocal(inv[:], a_tok[:]).then_inc(s["slope"], 1)

            def slope_pdf(n, par):
                F = n
                if not live(F):
                    return
                v.wait_ge(s["tanh"], F + 1)
                V.tensor_scalar(den[:], tanh[:], 1.0, None, ALU.add).then_inc(s["slope"], 1)
                V.tensor_scalar(num[:], tanh[:], -INV_SQRT_2PI, INV_SQRT_2PI, ALU.mult, ALU.add) \
                    .then_inc(s["slope"], 1)
                v.wait_ge(s["slope"], 6 * F + 2)
                V.reciprocal(den[:], den[:]).then_inc(s["slope"], 1)
                v.wait_ge(s["slope"], 6 * F + 3)
                V.tensor_tensor(num[:], num[:], a_tok[:], ALU.mult).then_inc(s["slope"], 1)
                v.wait_ge(s["slope"], 6 * F + 5)
                V.tensor_tensor(apdf[:], num[:], den[:], ALU.mult).then_inc(s["apdf"], 1)

            def slope_cdf(n, par):
                F = n
                if not live(F):
                    return
                v.wait_ge(s["hr_ps"], F + 1)
                V.tensor_copy(h[:], tiles(side_f[:, 0:TPS * (HID + 1)])).then_inc(s["h"], 1)
                V.tensor_copy(r[:], tiles(side_f[:, P:P + TOK])).then_inc(s["r"], 1)
                v.wait_ge(s["h"], F + 1)
                V.tensor_tensor(cdf[:], inv[:], h[:, :, 0:HID], ALU.mult).then_inc(s["slope"], 1)
                v.wait_ge(s["apdf"], F + 1)
                v.wait_ge(s["slope"], 6 * F + 6)
                V.tensor_tensor(cdf[:], cdf[:], apdf[:], ALU.add).then_inc(s["sloped"], 1)

            def hidden_grad(n, par):
                F = n
                if not live(F):
                    return
                v.wait_ge(s["sloped"], F + 1)
                v.wait_ge(s["dh_ps"], F + 1)
                V.tensor_tensor(da[:], tiles(side_f[:, 0:TPS * HID]), cdf[:], ALU.mult).then_inc(s["da"], 1)

            def output(n, par):
                O = n - 1
                if not live(O):
                    return
                v.wait_ge(s["out_ps"], O + 1)
                xt = x[:, bass.ds(O * TPS, TPS), :]
                V.tensor_tensor(xt, tiles(side_f[:, 0:TOK]), xt, ALU.add).then_inc(s["x1"], 1)
                hold(v, s["x1"], O + 1, s["held_v"])
                for t in range(TPS):
                    V.bn_stats(stats[:, t, :], x[:, tile_of(O, t), :].squeeze(1)).then_inc(s["stat"], 1)
                hold(v, s["stat"], 4 * O + 2, s["held_v"])
                for t in range(TPS):
                    V.bn_aggr(mv[:, t, :], stats[:, t, :]).then_inc(s["stat"], 1)

            def normed_rows(n, par):
                O = n - 1
                if not live(O):
                    return
                v.wait_ge(s["norms"], O + 1)
                for t in range(TPS):
                    V.tensor_scalar(hn[:, t, :], x[:, tile_of(O, t), :].squeeze(1), mv[:, t, 0:1], rms[:, t:t + 1],
                                    ALU.subtract, ALU.mult).then_inc(s["hn"], 1)

            def update(n, par):
                F = n - 1
                if not live(F):
                    return
                v.wait_ge(s["g_ps"], F + 1)
                V.scalar_tensor_tensor(out=fast[:], in0=side_g[:, 0:2 * HID], scalar=GRAD_SCALE, in1=fast[:],
                                       op0=ALU.mult, op1=ALU.add).then_inc(s["w"], 1)
                V.scalar_tensor_tensor(out=fast2[:], in0=side_g[0:HID + 1, P:2 * P], scalar=GRAD_SCALE,
                                       in1=fast2[:], op0=ALU.mult, op1=ALU.add).then_inc(s["w"], 1)
                V.scalar_tensor_tensor(out=b1[:], in0=side_g[0:HID, 2 * P:2 * P + 1], scalar=GRAD_SCALE,
                                       in1=b1[:], op0=ALU.mult, op1=ALU.add).then_inc(s["w"], 1)

            def rope(n, par, c):
                N = n - 2
                if not live(N):
                    return
                t, heads = c % 2, (4 if c < 2 else 8)
                v.wait_ge(s["qkv_ps"], N * CHUNKS + c + 1)
                after(v, s["qk_ps"], N * CHUNKS + c)
                src = side_q[:, 0:heads * DH].rearrange("p (h a f) -> p h a f", h=heads, a=2)
                cos = m["rope"][:, t, 0, :][:, None, None, :].broadcast_to([P, heads, 2, HALF])
                sin = m["rope"][:, t, 1, :][:, None, :].broadcast_to([P, heads, HALF])
                dc = t_cos[:, 0:heads * DH].rearrange("p (h a f) -> p h a f", h=heads, a=2)
                dn = t_sin[:, 0:heads * DH].rearrange("p (h a f) -> p h a f", h=heads, a=2)
                V.tensor_tensor(dc, src, cos, ALU.mult).then_inc(s["cos"], 1)
                V.scalar_tensor_tensor(out=dn[:, :, 0, :], in0=src[:, :, 1, :], scalar=-1.0, in1=sin,
                                       op0=ALU.mult, op1=ALU.mult).then_inc(s["sin"], 1)
                V.tensor_tensor(dn[:, :, 1, :], src[:, :, 0, :], sin, ALU.mult).then_inc(s["sin"], 1)

            def attended(n, par):
                B = n - 4
                if not live(B):
                    return
                after(v, s["x_sum"], B)
                for t in range(TPS):
                    V.tensor_scalar(xx[:, t, :], x[:, tile_of(B, t), :].squeeze(1), mean_all[:, tile_of(B, t)],
                                    rs_all[:, tile_of(B, t)], ALU.subtract, ALU.mult).then_inc(s["xx"], 1)
                v.wait_ge(s["xx"], TPS * B + TPS)
                v.wait_ge(s["proj_ps"], TPS * B + TPS)
                V.tensor_tensor(x2[:], tiles(side_g[:, 0:TOK]), xx[:], ALU.add).then_inc(s["x2"], 1)
                v.wait_ge(s["x2"], B + 1)
                for t in range(TPS):
                    V.tensor_tensor_reduce(out=x2sq[:, t, :], in0=x2[:, t, :], in1=x2[:, t, :], scale=1.0,
                                           scalar=0.0, op0=ALU.mult, op1=ALU.add,
                                           accum_out=ss[:, t:t + 1]).then_inc(s["ss"], 1)

            def h2_rows(n, par):
                B = n - 4
                if not live(B):
                    return
                after(v, sent[par], (B - par) * (TPS * TOPK * 8))
                v.wait_ge(s["rms2"], 2 * B + 2)
                for t in range(TPS):
                    V.tensor_scalar(h2[:, par, t, 0:D], x2[:, t, :], ss[:, t:t + 1], None, ALU.mult).then_inc(s["h2"], 1)
                V.tensor_copy(h2[:, par, :, D + TOPK:D + 2 * TOPK], m["pick_row"][:, bass.ds(B * TPS, TPS), :])

            def pick(n, par):
                B = n - 4
                if not live(B):
                    return
                v.wait_ge(s["gate_ps"], B + 1)
                V.tensor_copy(glog[:], side_g[:, 0:TPS * EXPERTS].rearrange("p (t e) -> p t e", t=TPS)) \
                    .then_inc(s["glog"], 1)
                hold(v, s["glog"], B + 1, s["held_v"])
                for t in range(TPS):
                    V.max(top[:, t, :], glog[:, t, :]).then_inc(s["top"], 1)
                v.wait_ge(s["top"], TPS * B + TPS)
                V.tensor_scalar(ntop[:], top[:, :, 0], -1.0, None, ALU.mult).then_inc(s["w_in"], 1)
                for t in range(TPS):
                    V.max_index(idx[:, t, :], top[:, t, :], glog[:, t, :]).then_inc(s["idx"], 1)

            def one_hot(n, par):
                B = n - 4
                if not live(B):
                    return
                v.wait_ge(s["idx"], TPS * B + TPS)
                V.tensor_copy(idxf[:], idx[:]).then_inc(s["idxf"], 1)
                v.wait_ge(s["idxf"], B + 1)
                for t in range(TPS):
                    V.tensor_tensor(hot[:, t], m["iota_e"][:, None, :].broadcast_to([P, TOPK, EXPERTS]),
                                    idxf[:, t, 0:TOPK][:, :, None].broadcast_to([P, TOPK, EXPERTS]), ALU.is_equal) \
                        .then_inc(s["hot"], 1)
                v.wait_ge(s["hot"], TPS * B + TPS)
                with nc.allow_low_precision("sums of four 0/1 values, exact in bfloat16"):
                    for t in range(TPS):
                        V.tensor_reduce(picked[:, t, :], hot[:, t].rearrange("p k e -> p e k"), AX.X, ALU.add) \
                            .then_inc(s["picked"], 1)

            def places(n, par):
                B = n - 4
                if not live(B):
                    return
                v.wait_ge(s["rank_ps"], B + 1)
                V.tensor_tensor(place[:], side_g[:, 0:TPS * EXPERTS].rearrange("p (t e) -> p t e", t=TPS),
                                m["base_e"][:, None, :].broadcast_to([P, TPS, EXPERTS]), ALU.add) \
                    .then_inc(s["place"], 1)
                v.wait_ge(s["wexp"], TPS * B + TPS)
                V.reciprocal(wrec[:], wsum[:]).then_inc(s["wrec"], 1)

            def slots(n, par):
                B = n - 4
                if not live(B):
                    return
                v.wait_ge(s["prod"], B + 1)
                slotf = h2[:, par, :, D:D + TOPK]
                V.tensor_reduce(slotf, prod[:], AX.X, ALU.add).then_inc(s["slotf"], 1)
                v.wait_ge(s["wrec"], B + 1)
                V.tensor_tensor(h2[:, par, :, D + 2 * TOPK:WIDE], wexp[:],
                                wrec[:, :, None].broadcast_to([P, TPS, TOPK]), ALU.mult)
                v.wait_ge(s["slotf"], B + 1)
                V.tensor_copy(slot[:, par].rearrange("p (t k) -> p t k", t=TPS), slotf).then_inc(s["slot"], 1)

            side = {0: [update], 2: [a_bias], 3: [attended, a_rows], 4: [h2_rows], 5: [slope_pdf],
                    6: [slope_cdf], 7: [hidden_grad, pick], 8: [one_hot], 9: [output], 10: [normed_rows, places],
                    11: [x_norm, slots]}

            def iteration(n, par):
                for u in range(UNITS):
                    softmax(n, par, u)
                    if u % 2 == 0:
                        rope(n, par, u // 2)
                    for stage in side.get(u, []):
                        stage(n, par)

            V.memset(hT2[HID:HID + 1, :, :], 1.0).then_inc(s["ready"], 1)
            V.tensor_tensor(dkvT[:], m["tkT"][:], m["tvT"][:], ALU.subtract).then_inc(s["ready"], 1)
            for t in range(TILES):
                V.bn_stats(stats0[:, t, :], x[:, t, :]).then_inc(s["stat0"], 1)
            v.wait_ge(s["stat0"], TILES)
            for t in range(TILES):
                V.bn_aggr(mv0[:, t, :], stats0[:, t, :]).then_inc(s["stat0"], 1)
            v.wait_ge(s["rs0"], 2)
            x_norm(-1, 1)
            run(v, iteration)

        @block.scalar
        def _(act):
            A_ = nc.scalar

            def exps(n, par, u):
                A, ap, u, done = at_unit(n, par, u)
                if not live(A):
                    return
                _, second, cols = unit(u)
                b, w = u % 2, cols.stop - cols.start
                act.wait_ge(s["nm"], done)
                after(act, s["t_ps"], done - 2)
                k = 512 // w
                for j in range(w):
                    cols = slice(j * k, (j + 1) * k)
                    ins = A_.activation(prob[:, b, cols], score[u % 3][:, cols], ACT.Exp, bias=nm[:, b, j:j + 1],
                                        scale=0.125, accum_out=sums[:, b, j:j + 1])
                act.wait_ge(s["es_in"], done)
                A_.activation(es[:, b, 0:w], es[:, b, 0:w], ACT.Exp).then_inc(s["exped"], 1)

            def take_probs(n, par, u):
                A, ap, u, done = at_unit(n, par, u)
                if not live(A):
                    return
                act.wait_ge(s["t_ps"], done)
                after(act, s["y_ps"], done - 2)
                A_.copy(probT[:, u % 2, :], turned[u % 2][:]).then_inc(s["probT"], 1)

            def take_y(n, par, u):
                A, ap, u, done = at_unit(n, par, u)
                if not live(A):
                    return
                pairs, second, _ = unit(u)
                act.wait_ge(s["y_ps"], done)
                if second:
                    A_.copy(yT[:, ap, pairs[0], P:TOK], turned[u % 2][:, 0:P]).then_inc(s["yT"], 1)
                else:
                    A_.copy(yT[:, ap, pairs[0]:pairs[0] + 2, 0:P],
                            turned[u % 2][:, 0:2 * P].rearrange("p (k t) -> p k t", k=2)).then_inc(s["yT"], 1)

            def xT_out(n, par):
                if not live(n):
                    return
                act.wait_ge(s["xT_ps"], n + 1)
                A_.copy(xnT[:, par, :], side_f[:, 0:TOK]).then_inc(s["xT"], 1)

            def zT_out(n, par):
                F, O = n, n - 1
                if not (live(F) or live(O)):
                    return
                lo, hi = (0 if live(F) else 1), (2 if live(O) else 1)
                act.wait_ge(s["z_ps"], n + 1)
                A_.copy(zT[:, lo:hi, :], side_f[:].rearrange("p (a t) -> p a t", a=2)[:, lo:hi, :]) \
                    .then_inc(s["zT"], 1)

            def gelus(n, par):
                F, O = n, n - 1
                if not (live(F) or live(O)):
                    return
                lo, hi = (0 if live(F) else 1), (2 if live(O) else 1)
                act.wait_ge(s["aT"], n + 1)
                A_.activation(hT2[0:HID, lo:hi, :], aT[:, lo:hi, :], ACT.Gelu).then_inc(s["gelu"], 1)
                if live(F):
                    act.wait_ge(s["expo"], F + 1)
                    A_.activation(tanh[:], expo[:], ACT.Tanh).then_inc(s["tanh"], 1)

            def rT_out(n, par):
                if not live(n):
                    return
                act.wait_ge(s["rT_ps"], n + 1)
                A_.copy(rT[:], side_f[:, 0:TOK]).then_inc(s["rT"], 1)

            def hT_out(n, par):
                O = n - 1
                if not live(O):
                    return
                after(act, s["qkv_ps"], O * CHUNKS)
                act.wait_ge(s["hn_ps"], O + 1)
                A_.activation(hT[:], side_f[:, 0:TOK], ACT.Copy, scale=m["norms"][:, 0:1]).then_inc(s["hT"], 1)

            def v_out(n, par, c):
                N = n - 2
                if not live(N):
                    return
                act.wait_ge(s["sin"], 2 * (N * CHUNKS + c) + 2)
                after(act, s["y_ps"], (N - 1) * UNITS)
                A_.copy(vv[:, par, c, :], side_q[:, KV * DH:2 * KV * DH]).then_inc(s["v_out"], 1)

            def qk_out(n, par, c):
                N = n - 2
                if not live(N):
                    return
                t = c % 2
                tok = slice(t * P, (t + 1) * P)
                act.wait_ge(s["qk_ps"], N * CHUNKS + c + 1)
                if c < 2:
                    for half in range(2):
                        rows = slice(half * DH, (half + 1) * DH)
                        ins = A_.copy(kpad[rows, par, :, half, tok],
                                      side_q[rows, 0:2 * P].rearrange("p (g t) -> p g t", g=2))
                else:
                    p0 = 4 * (c // 2 - 1)
                    ins = A_.copy(qT[:, par, p0:p0 + 4, tok], side_q[:].rearrange("p (b t) -> p b t", b=4))
                ins.then_inc(s["qk_out"], 1)

            def h2T_out(n, par):
                B = n - 4
                if not live(B):
                    return
                act.wait_ge(s["h2_ps"], B + 1)
                A_.activation(h2T[:], side_g[:, 0:TOK], ACT.Copy, scale=m["norms"][:, 1:2]).then_inc(s["h2T"], 1)

            def weights(n, par):
                B = n - 4
                if not live(B):
                    return
                act.wait_ge(s["w_in"], B + 1)
                for t in range(TPS):
                    A_.activation(wexp[:, t, :], top[:, t, 0:TOPK], ACT.Exp, bias=ntop[:, t:t + 1],
                                  accum_out=wsum[:, t:t + 1]).then_inc(s["wexp"], 1)

            side = {0: [xT_out], 1: [zT_out], 4: [gelus], 5: [rT_out, h2T_out], 8: [weights], 11: [hT_out]}

            def iteration(n, par):
                for u in range(UNITS):
                    take_probs(n, par, u - 1)
                    take_y(n, par, u - 2)
                    exps(n, par, u + 1)
                    if u in (0, 2):
                        v_out(n, par, u // 2)
                    if u % 2 == 1:
                        qk_out(n, par, u // 2)
                    for stage in side.get(u, []):
                        stage(n, par)

            act.wait_ge(m["attn_loaded"], ATTN_LOADS * 16)
            run(act, iteration)

        @block.gpsimd
        def _(pool):
            g = nc.gpsimd

            def rope_add(n, par, c):
                N = n - 2
                if not live(N):
                    return
                w = (4 if c < 2 else 8) * DH
                pool.wait_ge(s["sin"], 2 * (N * CHUNKS + c) + 2)
                g.tensor_tensor(t_cos[:, 0:w], t_cos[:, 0:w], t_sin[:, 0:w], ALU.add).then_inc(s["added"], 1)

            def norms(n, par):
                O = n - 1
                if not live(O):
                    return
                hold(pool, s["stat"], 4 * O + 4, s["held_p"])
                g.tensor_scalar(rs[:], mv[:, :, 1], EPS, None, ALU.add).then_inc(s["small"], 1)
                g.tensor_copy(mean_all[:, bass.ds(O * TPS, TPS)], mv[:, :, 0])
                pool.wait_ge(s["small"], O * 6 + 1)
                g.tensor_tensor(rs[:], rs[:], m["neghalf"][:, 0:TPS], ALU.pow).then_inc(s["small"], 1)
                pool.wait_ge(s["small"], O * 6 + 2)
                g.tensor_tensor(sq[:], rs[:], rs[:], ALU.mult).then_inc(s["small"], 1)
                g.tensor_copy(rs_all[:, bass.ds(O * TPS, TPS)], rs[:])
                pool.wait_ge(s["small"], O * 6 + 3)
                g.tensor_tensor(sq[:], sq[:], mv[:, :, 1], ALU.mult).then_inc(s["small"], 1)
                hold(pool, s["small"], O * 6 + 4, s["held_p"])
                g.tensor_scalar(sq[:], sq[:], EPS, None, ALU.add).then_inc(s["small"], 1)
                pool.wait_ge(s["small"], O * 6 + 5)
                g.tensor_tensor(sq[:], sq[:], m["neghalf"][:, 0:TPS], ALU.pow).then_inc(s["small"], 1)
                pool.wait_ge(s["small"], O * 6 + 6)
                g.tensor_tensor(rms[:], sq[:], rs[:], ALU.mult).then_inc(s["norms"], 1)

            def rms2(n, par):
                B = n - 4
                if not live(B):
                    return
                hold(pool, s["ss"], B * 2 + 2, s["held_p"])
                g.tensor_scalar(ss[:], ss[:], 1.0 / D, EPS, ALU.mult, ALU.add).then_inc(s["rms2"], 1)
                pool.wait_ge(s["rms2"], 2 * B + 1)
                g.tensor_tensor(ss[:], ss[:], m["neghalf"][:, 0:TPS], ALU.pow).then_inc(s["rms2"], 1)
                xt = x[:, bass.ds(B * TPS, TPS), :]
                g.tensor_tensor(xt, xt, x2[:], ALU.add).then_inc(s["x_sum"], 1)

            def spread(n, par):
                B = n - 4
                if not live(B):
                    return
                pool.wait_ge(s["place"], B + 1)
                g.tensor_tensor(prod[:], hot[:], place[:, :, None, :].broadcast_to([P, TPS, TOPK, EXPERTS]),
                                ALU.mult).then_inc(s["prod"], 1)
                for t in range(TPS):
                    after(pool, s["masksum"], TPS * B + t)
                    g.tensor_tensor(m["masksum"][:], m["masksum"][:], picked[:, t, :], ALU.add) \
                        .then_inc(s["masksum"], 1)

            def send(n, par, i):
                B = n - 5
                if not live(B):
                    return
                if i == 0:
                    pool.wait_ge(s["h2"], TPS * B + TPS)
                    hold(pool, s["slot"], B + 1, s["held_p"])
                for c in range(2 * i, 2 * i + 2):
                    t, k = c // TOPK, c % TOPK
                    g.indirect_dma_start(m["xs"], bass.IndirectOffsetOnAxis(
                        ap=slot[:, 1 - par, c:c + 1], axis=0), h2[:, 1 - par, t, :], None).then_inc(sent[1 - par], 16)

            side = {3: [rms2], 9: [norms], 10: [spread]}

            def iteration(n, par):
                for u in range(UNITS):
                    if u % 2 == 0:
                        rope_add(n, par, u // 2)
                    if u < TPS * TOPK // 2:
                        send(n, par, u)
                    for stage in side.get(u, []):
                        stage(n, par)

            g.memset(kpad[:], 0.0).then_inc(s["ready"], 1)
            pool.wait_ge(s["stat0"], 2 * TILES)
            g.tensor_scalar(rstd0[:], mv0[:, :, 1], EPS, None, ALU.add).then_inc(s["rs0"], 1)
            pool.wait_ge(s["rs0"], 1)
            g.tensor_tensor(rstd0[:], rstd0[:], m["neghalf"][:], ALU.pow).then_inc(s["rs0"], 1)
            pool.wait_ge(s["rs0"], 2)
            g.memset(rs[:], 0.0).then_inc(s["ready"], 1)
            run(pool, iteration)
            for par in range(2):
                pool.wait_ge(sent[par], SEQS // 2 * TPS * TOPK * 16)


def experts(m):
    nc, ident = m["nc"], m["ident"]
    with ExitStack() as ctx:
        def sb(name, shape, dt=F32):
            return ctx.enter_context(nc.sbuf_tensor("e_" + name, shape, dt))

        def ps(name, shape):
            return ctx.enter_context(nc.psum_tensor("e_" + name, shape, F32))

        upto = sb("upto", [P, EXPERTS, EXPERTS])
        cnt, ntile, cum = sb("cnt", [P, EXPERTS]), sb("ntile", [P, EXPERTS]), sb("cum", [P, EXPERTS])
        cnt_i, pad_i = sb("cnt_i", [P, EXPERTS], I32), sb("pad_i", [P, EXPERTS], I32)
        sq = sb("sq", [P, EXPERTS, EXPERTS])
        past, cost = sb("past", [P, COLS, EXPERTS]), sb("cost", [P, COLS, EXPERTS])
        exp_t, skip_t = sb("exp_t", [P, COLS]), sb("skip_t", [P, COLS])
        diag = sb("diag", [P, COLS, P])
        own = sb("own", [P, COLS * P])
        row_i = sb("row_i", [1, COLS * P], I32)
        codes = sb("codes", [1, COLS * P // GROUP], I32)
        xt = sb("xt", [P, 4, GROUP, WIDE])
        xT, act, hid, hidT = (sb(n, [P, 2, GROUP, D]) for n in "xT act hid hidT".split())
        yo = sb("yo", [P, 2, GROUP, D])
        eq, pick = sb("eq", [P, GROUP, TOPK]), sb("pick", [P, GROUP, 2, TOPK])
        mine = sb("mine", [P, 4, GROUP, 2])
        dest = sb("dest", [P, 4, GROUP], U32)
        p_x, p_h, p_y = ps("p_x", [P, 512]), ps("p_h", [P, 512]), ps("p_y", [P, 512])
        p_up = [ps(f"p_up{b}", [P, GROUP, 2 * DFF]) for b in range(2)]
        s = {n: ctx.enter_context(nc.semaphore("e_" + n)) for n in
             ("upto cnt_ps counted step placed rows_ps planned padded_a padded_b xT_ps xT up_ps act hid hidT_ps hidT y_ps y "
              "eq pick mine dest held sent_a sent_b in_a in_b in_c in_d").split()}
        arrived = [s[n] for n in ("in_a", "in_b", "in_c", "in_d")]
        sent = [s["sent_a"], s["sent_b"]]
        block = ctx.enter_context(nc.Block())
        FIRST = 6
        BODIES = (GROUPS - 2 - FIRST) // 4

        def live(g):
            return not isinstance(g, int) or 0 <= g < GROUPS

        def run(eng, step, load=None):
            def some(first, last):
                c = load(first, last - first) if load else {}
                return lambda k: c[k - first] if load else None
            c = some(0, FIRST)
            for g in range(-1, FIRST):
                step(g, g % 4, c(max(g, 0)), c(max(g - 2, 0)))
            with eng.Fori(0, BODIES) as i:
                c = load(i * 4 + (FIRST - 2), 6) if load else [None] * 6
                for k in range(4):
                    step(i * 4 + (FIRST + k), (FIRST + k) % 4, c[k + 2], c[k])
            c = some(GROUPS - 4, GROUPS)
            for g in range(GROUPS - 2, GROUPS + 2):
                step(g, g % 4, c(min(g, GROUPS - 1)), c(g - 2))

        def zero_pads(eng, first, signal):
            half = EXPERTS // 2
            for e0 in range(first * half, (first + 1) * half, 8):
                rows = nc.values_load_multi_w_load_instructions(
                    pad_i[0:1, e0:e0 + 8], engines=[eng.engine], min_val=0, max_val=ROWS - P)[1]
                for r in rows:
                    eng.dma_start(m["xs"][bass.ds(r, P), :], m["zeros"][:]).then_inc(signal, 16)

        @block.sync
        def _(sp):
            sp.wait_ge(s["counted"], 1)
            zero_pads(sp, 0, s["padded_a"])
            sp.wait_ge(s["placed"], 1)
            sp.wait_ge(s["padded_a"], EXPERTS // 2 * 16)
            sp.wait_ge(s["padded_b"], EXPERTS // 2 * 16)
            sp.wait_ge(m["tail_zeroed"], TAIL * 16)

            def load(g, q):
                rows = nc.values_load_multi_w_load_instructions(
                    row_i[0:1, bass.ds(g * GROUP, GROUP)], engines=[sp.engine], min_val=0, max_val=ROWS - P)[1]
                for j, r in enumerate(rows):
                    sp.dma_start(xt[:, q, j, :], m["xs"][bass.ds(r, P), :]).then_inc(arrived[q], 16)

            for g in range(4):
                load(g, g)
            with sp.Fori(1, GROUPS // 4) as i:
                for q in range(4):
                    sp.wait_ge(s["xT_ps"], i * 4 + (q - 3))
                    sp.wait_ge(s["dest"], i * 4 + (q - 3))
                    load(i * 4 + q, q)
            for q in range(4):
                sp.wait_ge(arrived[q], GROUPS // 4 * GROUP * 16)

        @block.gpsimd
        def _(pool):
            g_ = nc.gpsimd
            g_.memset(upto[:], 1.0).then_inc(s["upto"], 1)
            pool.wait_ge(s["upto"], 1)
            g_.affine_select(out=upto[:], in_=upto[:], compare_op=ALU.is_ge, fill=0.0, base=0,
                             pattern=[[1, EXPERTS], [-1, EXPERTS]], channel_multiplier=0).then_inc(s["upto"], 1)
            with pool.Fori(0, GROUPS // 4) as i:
                for q in range(4):
                    hold(pool, s["y"], i * 4 + (q + 1), s["held"])
                    for j in range(GROUP):
                        g_.indirect_dma_start(m["ys"], bass.IndirectOffsetOnAxis(ap=dest[:, q, j:j + 1], axis=0),
                                              yo[:, q % 2, j, :], None).then_inc(sent[q % 2], 16)
            for b in range(2):
                pool.wait_ge(sent[b], GROUPS // 2 * GROUP * 16)

        @block.vector
        def _(v):
            V, n_ = nc.vector, [0]

            def step(ins):
                n_[0] += 1
                ins.then_inc(s["step"], 1)
                v.wait_ge(s["step"], n_[0])
            v.wait_ge(s["cnt_ps"], 1)
            step(V.tensor_copy(cnt[:], p_x[:, 0:EXPERTS]))
            V.tensor_tensor(pad_i[:], cnt[:], m["base_e"][:], ALU.add).then_inc(s["counted"], 1)
            step(V.tensor_scalar(cnt_i[:], cnt[:], float(P - 1), None, ALU.add))
            step(V.tensor_scalar(cnt_i[:], cnt_i[:], P.bit_length() - 1, None, ALU.arith_shift_right))
            step(V.tensor_copy(ntile[:], cnt_i[:]))
            v.wait_ge(s["upto"], 2)
            step(V.tensor_tensor(sq[:], upto[:], ntile[:, None, :].broadcast_to([P, EXPERTS, EXPERTS]), ALU.mult))
            step(V.tensor_reduce(cum[:], sq[:], AX.X, ALU.add))
            wide = [P, COLS, EXPERTS]
            step(V.tensor_tensor(past[:], cum[:, None, :].broadcast_to(wide),
                                 m["tile_id"][:, :, None].broadcast_to(wide), ALU.is_le))
            V.tensor_reduce(exp_t[:], past[:], AX.X, ALU.add)
            step(V.tensor_tensor(cost[:], past[:], ntile[:, None, :].broadcast_to(wide), ALU.mult))
            step(V.tensor_reduce(skip_t[:], cost[:], AX.X, ALU.add))
            step(V.tensor_tensor(skip_t[:], m["tile_id"][:], skip_t[:], ALU.subtract))
            step(V.scalar_tensor_tensor(out=skip_t[:], in0=exp_t[:], scalar=float(REGION // P), in1=skip_t[:],
                                        op0=ALU.mult, op1=ALU.add))
            V.tensor_scalar(exp_t[:], exp_t[:], float(EXPERTS - 1), None, ALU.min)
            for c in range(COLS):
                ins = V.tensor_scalar(diag[:, c, :], ident[:], skip_t[:, c:c + 1], None, ALU.mult)
            ins.then_inc(s["planned"], 1)
            v.wait_ge(s["rows_ps"], 1)
            V.tensor_scalar(row_i[:], p_x[0:1, 0:COLS * P], float(P), None, ALU.mult).then_inc(s["placed"], 1)
            V.tensor_copy(codes[:], p_y[0:1, 0:COLS * P // GROUP]).then_inc(s["placed"], 1)
            V.tensor_scalar(own[:], p_x[:, 0:COLS * P], float(P), m["tile_id"][:, 0:1], ALU.mult, ALU.add) \
                .then_inc(s["placed"], 1)
            v.wait_ge(s["placed"], 3)

            def find(g, q):
                if not live(g):
                    return
                info = xt[:, q, :, D:WIDE].rearrange("p j (a k) -> p j a k", k=TOPK)
                v.wait_ge(arrived[q], g * 16 + (GROUP * 16 - q * 16))
                V.tensor_tensor(eq[:], info[:, :, 0, :],
                                own[:, bass.ds(g * GROUP, GROUP)][:, :, None].broadcast_to([P, GROUP, TOPK]),
                                ALU.is_equal).then_inc(s["eq"], 1)

            def find_products(g, q):
                if not live(g):
                    return
                info = xt[:, q, :, D:WIDE].rearrange("p j (a k) -> p j a k", k=TOPK)
                v.wait_ge(s["eq"], g + 1)
                V.tensor_tensor(pick[:], info[:, :, 1:3, :], eq[:, :, None, :].broadcast_to([P, GROUP, 2, TOPK]),
                                ALU.mult).then_inc(s["pick"], 1)

            def find_sums(g, q):
                if not live(g):
                    return
                if not isinstance(g, int) or g >= 4:
                    v.wait_ge(sent[q % 2], g * 32 - (q % 2 + 2) * 32)
                v.wait_ge(s["pick"], g + 1)
                V.tensor_reduce(mine[:, q], pick[:], AX.X, ALU.add).then_inc(s["mine"], 1)

            def find_dest(g, q):
                if not live(g):
                    return
                v.wait_ge(s["mine"], g + 1)
                V.tensor_tensor(dest[:, q], mine[:, q, :, 0], m["row_id"][:, bass.ds(g * GROUP, GROUP)], ALU.max) \
                    .then_inc(s["dest"], 1)

            def work(g, q, up_code, down_code):
                b = q % 2
                find(g + 1, (q + 1) % 4)
                if live(g - 1):
                    h = g - 1
                    v.wait_ge(s["hidT_ps"], h + 1)
                    after(v, s["y_ps"], h - 1)
                    V.tensor_copy(hidT[:, 1 - b], p_h[:].rearrange("p (j t) -> p j t", j=GROUP)) \
                        .then_inc(s["hidT"], 1)
                find_products(g + 1, (q + 1) % 4)
                if live(g):
                    v.wait_ge(s["act"], g + 1)
                    after(v, s["hidT_ps"], g - 1)
                    V.tensor_tensor(hid[:, b], act[:, b], p_up[b][:, :, 0:DFF], ALU.mult).then_inc(s["hid"], 1)
                find_sums(g + 1, (q + 1) % 4)
                find_dest(g + 1, (q + 1) % 4)

            run(v, work)

        @block.scalar
        def _(act_):
            A = nc.scalar
            act_.wait_ge(s["counted"], 1)
            zero_pads(act_, 1, s["padded_b"])

            def work(g, q, up_code, down_code):
                b = q % 2
                if live(g):
                    act_.wait_ge(s["up_ps"], g + 1)
                    after(act_, s["hid"], g - 1)
                    A.activation(act[:, b], p_up[b][:, :, DFF:2 * DFF], ACT.Silu).then_inc(s["act"], 1)
                if live(g + 1):
                    act_.wait_ge(s["xT_ps"], g + 2)
                    after(act_, s["up_ps"], g)
                    A.activation(xT[:, 1 - b], p_x[:].rearrange("p (j t) -> p j t", j=GROUP), ACT.Copy,
                                 scale=m["norms"][:, 1:2]).then_inc(s["xT"], 1)
                if live(g - 2):
                    h, r = g - 2, (q - 2) % 4
                    act_.wait_ge(s["y_ps"], h + 1)
                    act_.wait_ge(s["dest"], h + 1)
                    if not isinstance(h, int) or h >= 2:
                        act_.wait_ge(sent[b], h * 32 - b * 32)
                    for j in range(GROUP):
                        ins = A.activation(yo[:, b, j, :], p_y[:, j * P:(j + 1) * P], ACT.Copy,
                                           scale=mine[:, r, j, 1:2])
                    ins.then_inc(s["y"], 1)
            run(act_, work)

        @block.tensor
        def _(pe):
            mm, tr = nc.tensor.matmul, nc.tensor.transpose
            mm(p_x[:, 0:EXPERTS], m["ones_bf"][:], m["masksum"][:], start=True, stop=True) \
                .then_inc(s["cnt_ps"], 1)
            pe.wait_ge(s["planned"], 1)
            for c in range(COLS):
                mm(p_y[0:1, c * P // GROUP:(c + 1) * P // GROUP], exp_t[:, c:c + 1], m["digits"][:],
                   start=True, stop=True)
                ins = mm(p_x[:, c * P:(c + 1) * P], m["ones"][:], diag[:, c, :], start=True, stop=True)
            ins.then_inc(s["rows_ps"], 1)
            pe.wait_ge(s["placed"], 3)
            pe.wait_ge(m["moe_loaded"], MOE_LOADS * 16)

            def load(first, count):
                return nc.values_load_multi_w_load_instructions(
                    codes[0:1, bass.ds(first, count)], engines=[pe.engine], min_val=0,
                    max_val=EXPERTS ** GROUP - 1)[1]

            def expert(code, j):
                return (code // EXPERTS ** j) % EXPERTS

            def work(g, q, up_code, down_code):
                b = q % 2
                if live(g + 1):
                    r = (q + 1) % 4
                    pe.wait_ge(arrived[r], g * 16 + (GROUP + 1 - r) * 16)
                    after(pe, s["xT"], g + 1)
                    for j in range(GROUP):
                        ins = tr(p_x[:, j * P:(j + 1) * P], xt[:, r, j, 0:D], ident[:])
                    ins.then_inc(s["xT_ps"], 1)
                if live(g):
                    pe.wait_ge(s["xT"], g + 1)
                    after(pe, s["hid"], g - 1)
                    for j in range(GROUP):
                        ins = mm(p_up[b][:, j, :], xT[:, b, j, :],
                                 m["wup"][:, bass.ds(expert(up_code, j) * (2 * DFF), 2 * DFF)],
                                 start=True, stop=True)
                    ins.then_inc(s["up_ps"], 1)
                if live(g - 1):
                    pe.wait_ge(s["hid"], g)
                    after(pe, s["hidT"], g - 1)
                    for j in range(GROUP):
                        ins = tr(p_h[:, j * P:(j + 1) * P], hid[:, 1 - b, j, :], ident[:])
                    ins.then_inc(s["hidT_ps"], 1)
                if live(g - 2):
                    pe.wait_ge(s["hidT"], g - 1)
                    after(pe, s["y"], g - 2)
                    for j in range(GROUP):
                        ins = mm(p_y[:, j * P:(j + 1) * P], hidT[:, b, j, :],
                                 m["wdown"][:, bass.ds(expert(down_code, j) * D, D)], start=True, stop=True)
                    ins.then_inc(s["y_ps"], 1)
            run(pe, work, load)


def combine(m):
    nc, x = m["nc"], m["x"]
    BUFS, LOADS = 4, 2
    with ExitStack() as ctx:
        def sb(name, shape, dt=F32):
            return ctx.enter_context(nc.sbuf_tensor("c_" + name, shape, dt))

        rows = sb("rows", [P, BUFS, LOADS, TOPK, D])
        two, one = sb("two", [P, BUFS, LOADS, 2, D]), sb("one", [P, BUFS, LOADS, D])
        res = sb("res", [P, BUFS, LOADS, D])
        loaded = [ctx.enter_context(nc.semaphore(f"c_loaded{b}")) for b in range(BUFS)]
        written = [ctx.enter_context(nc.semaphore(f"c_written{b}")) for b in range(BUFS)]
        halved, added, summed = (ctx.enter_context(nc.semaphore("c_" + n)) for n in ("halved", "added", "summed"))
        block = ctx.enter_context(nc.Block())
        N = TILES // LOADS

        def source(i):
            return m["ys"][SPARE + i * LOADS * P * TOPK:SPARE + (i + 1) * LOADS * P * TOPK, :] \
                .rearrange("(t p k) d -> p t k d", p=P, k=TOPK)

        @block.sync
        def _(sp):
            for i in range(N):
                if i >= BUFS:
                    sp.wait_ge(halved, i - BUFS + 1)
                sp.dma_start(rows[:, i % BUFS], source(i)).then_inc(loaded[i % BUFS], 16)

        @block.vector
        def _(v):
            V = nc.vector
            for i in range(N):
                b = i % BUFS
                v.wait_ge(loaded[b], (i // BUFS + 1) * 16)
                V.tensor_tensor(two[:, b], rows[:, b, :, 0:2, :], rows[:, b, :, 2:4, :], ALU.add) \
                    .then_inc(halved, 1)
                v.wait_ge(halved, i + 1)
                V.tensor_tensor(one[:, b], two[:, b, :, 0, :], two[:, b, :, 1, :], ALU.add).then_inc(added, 1)
                v.wait_ge(added, i + 1)
                if i >= BUFS:
                    v.wait_ge(written[b], (i // BUFS) * 16)
                V.tensor_tensor(res[:, b], one[:, b], x[:, i * LOADS:(i + 1) * LOADS, :], ALU.add) \
                    .then_inc(summed, 1)

        @block.scalar
        def _(act):
            for i in range(N):
                act.wait_ge(summed, i + 1)
                act.dma_start(m["out"][i * LOADS * P:(i + 1) * LOADS * P, :].rearrange("(t p) d -> p t d", p=P),
                              res[:, i % BUFS]).then_inc(written[i % BUFS], 16)
            for b in range(BUFS):
                act.wait_ge(written[b], N // BUFS * 16)




def _layout(v):
    import numpy as np
    g = {k: np.ascontiguousarray(x) for k, x in v.items()}
    heads = [h for p in range(PAIRS) for h in pair_heads(p)]
    split = np.concatenate([np.arange(0, DH, 2), np.arange(1, DH, 2)])
    cols = np.concatenate([h * DH + split for h in heads] + [(HEADS + g_) * DH + split for g_ in range(KV)]
                          + [np.arange((HEADS + KV) * DH, QKV)])
    rows = np.concatenate([h * DH + np.arange(DH) for h in heads])
    f = np.float32
    freq = (f(1.0) / f(150000.0) ** (np.arange(0, DH, 2, dtype=f) / f(DH))).astype(f)
    angle = (np.arange(TOK, dtype=f) / f(32.0))[:, None] * freq[None, :]
    i, j = np.arange(P)[:, None], np.arange(P)[None, :]
    neg = f(-1e30)
    sink = g["L0_ffn_attn_sink"][heads].reshape(PAIRS, 2)
    return {
        "x": g["L0_attn_in_seq"].reshape(SEQS * TOK, D),
        "tkT": g["L0_attn_t_k"].T, "tvT": g["L0_attn_t_v"].T, "tqT": g["L0_attn_t_q"].T,
        "W1T": g["L0_attn_W1"].T, "b1": g["L0_attn_b1"].reshape(HID, 1),
        "W2": g["L0_attn_W2"], "W2T": g["L0_attn_W2"].T, "b2": g["L0_attn_b2"].reshape(1, D),
        "norms": np.stack([g["L0_ffn_attn_norm_w"], g["L0_ffn_ffn_norm_w"]], 1),
        "wqkv": g["L0_ffn_qkv_w"][:, cols], "wproj": g["L0_ffn_proj_w"][rows],
        "bias": np.concatenate([g["L0_ffn_qkv_b"][cols], g["L0_ffn_proj_b"], g["L0_ffn_gate_b"]]),
        "sink": sink.reshape(-1),
        "gate": g["L0_ffn_gate_w"], "wup": g["L0_ffn_W_up"], "wdown": g["L0_ffn_W_down"],
        "ident": np.eye(P, dtype=f),
        "mask": np.concatenate([np.where(j >= i, f(0), neg), np.where(j <= i, f(0), neg)], 1).astype(f),
        "before": (i < j).astype(f),
        "rope": np.stack([np.cos(angle), np.sin(angle)], 1).astype(f),
        "iota_e": np.arange(EXPERTS, dtype=f),
        "pick_row": (SPARE + np.arange(SEQS * TOK * TOPK)).reshape(-1, TOPK).astype(f),
        "row_id": (i + P * np.arange(MAX_TILES)[None, :]).astype(f),
        "tile_id": (i + P * np.arange(COLS)[None, :]).astype(f),
        "digits": np.where(i // GROUP == np.arange(P // GROUP)[None, :], EXPERTS ** (i % GROUP), 0).astype(f),
    }


def kernel(**inputs):
    import numpy as np
    import concourse.bacc as bacc
    from concourse.bass_utils import run_bass_kernel_spmd

    nc = bacc.Bacc("TRN2", target_bir_lowering=False, num_devices=1)
    arrays = {"in_" + k: np.ascontiguousarray(v) for k, v in _layout(inputs).items()}
    a = {k[3:]: nc.dram_tensor(k, v.shape, mybir.dt.from_np(v.dtype), kind="ExternalInput").ap()
         for k, v in arrays.items()}
    out = nc.dram_tensor("out_x", [SEQS * TOK, D], F32, kind="ExternalOutput").ap()
    program(nc, a, out)
    r = run_bass_kernel_spmd(nc, [arrays], core_ids=[0])
    return r.results[0]["out_x"].reshape(SEQS, TOK, D)
```

```python
from contextlib import ExitStack

import concourse.bass as bass
import concourse.mybir as mybir

F32 = mybir.dt.float32
BF16 = mybir.dt.bfloat16
I32 = mybir.dt.int32
U32 = mybir.dt.uint32
ALU = mybir.AluOpType
ACT = mybir.ActivationFunctionType
AX = mybir.AxisListType

P = 128
SEQS, TOK, D = 16, 256, 128
TPS = TOK // P
TILES = SEQS * TPS
HID = 32
LR = 0.001
GRAD_SCALE = -LR * 2.0 / (TOK * D)
HEADS, KV, DH = 16, 4, 64
PAIRS = HEADS // 2
HALF = DH // 2
QKV = (HEADS + 2 * KV) * DH
UNITS = 12
CHUNKS = 3 * TPS
EXPERTS, TOPK, DFF = 32, 4, 128
EPS = 1e-5
TINY = 1e-30
INV_SQRT_2PI = 0.3989422804014327
REGION = SEQS * TOK + P
MAX_TILES = 160
COLS = -(-MAX_TILES // P)
WIDE = D + 3 * TOPK
GROUP = 4
GROUPS = MAX_TILES // GROUP
TAIL = MAX_TILES - SEQS * TOK * TOPK // P
SPARE = MAX_TILES * P
ROWS = EXPERTS * REGION + TAIL * P


def tiled(ap):
    return ap.rearrange("(t p) d -> p t d", p=P)


def tiles(ap):
    return ap.rearrange("p (t d) -> p t d", t=TPS)


def hold(eng, sem, value, held):
    eng.wait_ge(sem, value)
    eng.sem_inc(held, 1)


def after(eng, sem, value):
    if not isinstance(value, int) or value > 0:
        eng.wait_ge(sem, value)


def pair_heads(p):
    g2, j = p // 4, p % 4
    return (2 * g2) * 4 + j, (2 * g2 + 1) * 4 + j


def unit(u):
    j, kind = u // 3, u % 3
    if kind < 2:
        p = 2 * j + kind
        return [p], True, slice(2 * p, 2 * p + 2)
    return [2 * j, 2 * j + 1], False, slice(4 * j, 4 * j + 4)


def send_pick(m, par, c):
    m["nc"].gpsimd.indirect_dma_start(
        m["xs"], bass.IndirectOffsetOnAxis(ap=m["slot"][:, par, c:c + 1], axis=0),
        m["h2"][:, par, c // TOPK, :], None).then_inc(m["sent"][par], 16)


def program(nc, a, out):
    with ExitStack() as ctx:
        def sb(name, shape, dt=F32):
            return ctx.enter_context(nc.sbuf_tensor(name, shape, dt))

        m = {"nc": nc, "a": a, "out": out}
        m["x"] = sb("x_all", [P, TILES, D])
        m["ident"] = sb("ident_sb", [P, P])
        m["ident_bf"] = sb("ident_bf", [P, P], BF16)
        m["mask2"] = sb("mask2", [P, 2, 2 * P], BF16)
        m["mask1"] = sb("mask1", [P, 4, P], BF16)
        m["before"] = sb("before_bf", [P, P], BF16)
        m["ones_bf"] = sb("ones_bf", [P, P], BF16)
        m["rope"] = sb("rope_sb", [P, TPS, 2, HALF])
        m["neghalf"] = sb("neghalf", [P, TILES])
        m["wqkv"] = sb("wqkv_sb", [P, QKV])
        m["wproj"] = sb("wproj_sb", [P, PAIRS, D])
        m["norms"] = sb("norms_sb", [P, 2])
        m["gate"] = sb("gate_sb", [P, EXPERTS])
        m["bias3"] = sb("bias3_bf", [3, NB], BF16)
        m["negsink"] = sb("negsink", [P, HEADS])
        m["wup"] = sb("wup_sb", [P, EXPERTS * 2 * DFF])
        m["wdown"] = sb("wdown_sb", [P, EXPERTS * D])
        m["masksum"] = sb("masksum", [P, EXPERTS], BF16)
        m["iota_e"] = sb("iota_e", [P, EXPERTS])
        m["base_e"] = sb("base_e", [P, EXPERTS])
        m["pick_row"] = sb("pick_row", [P, TILES, TOPK])
        m["row_id"] = sb("row_id", [P, MAX_TILES])
        m["tile_id"] = sb("tile_id", [P, COLS])
        m["digits"] = sb("digits", [P, P // GROUP])
        m["ones"] = sb("ones", [P, P])
        m["upto"] = sb("upto", [P, EXPERTS, EXPERTS])
        m["fast"] = sb("fast", [P, 2 * HID])
        m["fast2"] = sb("fast2", [HID + 1, P])
        m["b1"] = sb("b1_sb", [HID, 1])
        m["tkT"], m["tvT"], m["tqT"] = sb("tkT_sb", [P, P]), sb("tvT_sb", [P, P]), sb("tqT_sb", [P, P])
        m["xs"] = nc.dram_tensor("expert_rows", [ROWS, WIDE], F32, kind="Internal").ap()
        m["ys"] = nc.dram_tensor("expert_out", [SPARE + SEQS * TOK * TOPK, D], F32, kind="Internal").ap()
        m["h2"] = sb("h2", [P, 2, TPS, WIDE])
        m["slot"] = sb("slot", [P, 2, TPS * TOPK], U32)
        m["sent"] = [ctx.enter_context(nc.semaphore(f"sent_{k}")) for k in ("even", "odd")]
        m["mask_f"], m["before_f"] = sb("mask_f", [P, 2 * P]), sb("before_f", [P, P])
        m["bias_f"] = sb("bias_f", [NB_ROWS, NB // NB_ROWS])
        for n in ("first_loaded", "x_loaded", "small_loaded", "attn_loaded", "moe_loaded", "tail_zeroed"):
            m[n] = ctx.enter_context(nc.semaphore(n))
        m["zeros"] = sb("zeros", [P, WIDE])
        prepare(m)
        layers(m)
        experts(m)
        combine(m)


FIRST_LOADS, X_LOADS, SMALL_LOADS, ATTN_LOADS, MOE_LOADS = 10, 2, 9, 5, 2
NB = QKV + D + EXPERTS
NB_ROWS = 106


def loads(m):
    a, x = m["a"], m["x"]
    signals = {
        "first_loaded": [
            (x[:, 0:TPS, :], tiled(a["x"][0:TOK, :])),
            (m["ident"][:], a["ident"]),
            (m["tkT"][:], a["tkT"]), (m["tvT"][:], a["tvT"]), (m["tqT"][:], a["tqT"]),
            (m["fast"][:, 0:HID], a["W1T"]), (m["fast"][:, HID:], a["W2"]),
            (m["fast2"][0:HID, :], a["W2T"]), (m["fast2"][HID:HID + 1, :], a["b2"]), (m["b1"][:], a["b1"])],
        "x_loaded": [
            (x[:, TPS:8, :], tiled(a["x"][TOK:8 * P, :])),
            (x[:, 8:, :], tiled(a["x"][8 * P:, :]))],
        "small_loaded": [
            (m["mask_f"][:], a["mask"]), (m["before_f"][:], a["before"]),
            (m["bias_f"][:], a["bias"].rearrange("(p c) -> p c", p=NB_ROWS)),
            (m["negsink"][:], a["sink"].partition_broadcast(P)),
            (m["iota_e"][:], a["iota_e"].partition_broadcast(P)),
            (m["pick_row"][:], a["pick_row"].rearrange("(t p) k -> p t k", p=P)),
            (m["row_id"][:], a["row_id"]), (m["tile_id"][:], a["tile_id"]), (m["digits"][:], a["digits"])],
        "attn_loaded": [
            (m["norms"][:], a["norms"]),
            (m["rope"][:], a["rope"].rearrange("(t p) c f -> p t c f", p=P)),
            (m["wqkv"][:], a["wqkv"]),
            (m["wproj"][:], a["wproj"].rearrange("(c p) d -> p c d", p=P)),
            (m["gate"][:], a["gate"])],
        "moe_loaded": [
            (m["wup"][:].rearrange("p (e f) -> p e f", e=EXPERTS), a["wup"].rearrange("e d f -> d e f")),
            (m["wdown"][:].rearrange("p (e f) -> p e f", e=EXPERTS), a["wdown"].rearrange("e d f -> d e f"))],
    }
    assert [len(v) for v in signals.values()] == [FIRST_LOADS, X_LOADS, SMALL_LOADS, ATTN_LOADS, MOE_LOADS]
    return signals


def start_loads(m, sp, signals):
    for signal in signals:
        for dst, src in loads(m)[signal]:
            sp.dma_start(dst, src).then_inc(m[signal], 16)


def prepare(m):
    nc = m["nc"]
    with ExitStack() as ctx:
        block = ctx.enter_context(nc.Block())

        @block.sync
        def _(sp):
            start_loads(m, sp, ["first_loaded"])

        @block.gpsimd
        def _(pool):
            nc.gpsimd.memset(m["zeros"][:], 0.0)
            nc.gpsimd.memset(m["neghalf"][:], -0.5)
            nc.gpsimd.memset(m["ones_bf"][:], 1.0)
            nc.gpsimd.memset(m["ones"][:], 1.0)
            nc.gpsimd.memset(m["masksum"][:], 0.0)
            nc.gpsimd.memset(m["upto"][:], 1.0)


def layers(m):
    nc, x, ident = m["nc"], m["x"], m["ident"]
    fast, fast2, b1 = m["fast"], m["fast2"], m["b1"]
    with ExitStack() as ctx:
        def sb(name, shape, dt=F32):
            return ctx.enter_context(nc.sbuf_tensor("l_" + name, shape, dt))

        def ps(name):
            return ctx.enter_context(nc.psum_tensor("l_" + name, [P, 512], F32))

        dkvT = sb("dkvT", [P, P])
        stats0, mv0, rstd0 = sb("stats0", [P, TILES, 6]), sb("mv0", [P, TILES, 2]), sb("rstd0", [P, TILES])
        xn, xnT = sb("xn", [P, TPS, D]), sb("xnT", [P, 2, TOK])
        zT, z = sb("zT", [P, 2, TOK]), sb("z", [P, TPS, D])
        aT, hT2 = sb("aT", [HID, 2, TOK]), sb("hT2", [HID + 1, 2, TOK])
        h, r, rT = sb("h", [P, TPS, HID + 1]), sb("r", [P, TPS, D]), sb("rT", [P, TOK])
        a_tok, expo, tanh, num, den, inv, cdf, apdf, da = (
            sb(n, [P, TPS, HID]) for n in "a_tok expo tanh num den inv cdf apdf da".split())
        filler = sb("filler", [P, 512], BF16)
        part = sb("part", [NB_ROWS, 3, NB // NB_ROWS], BF16)
        rest = sb("rest", [NB_ROWS, 2, NB // NB_ROWS])
        stats, mv = sb("stats", [P, TPS, 6]), sb("mv", [P, TPS, 2])
        mean_all, rs_all = sb("mean_all", [P, TILES]), sb("rs_all", [P, TILES])
        rs, sq, rms = sb("rs", [P, TPS]), sb("sq", [P, TPS]), sb("rms", [P, TPS])
        hn, hT = sb("hn", [P, TPS, D]), sb("hT", [P, TOK])
        t_cos, t_sin = sb("t_cos", [P, 512]), sb("t_sin", [P, 512])
        qT = sb("qT", [P, 2, PAIRS, TOK])
        kpad = sb("kpad", [P, 2, 2, 2, TOK])
        vv = sb("vv", [P, 2, TPS, KV * DH])
        mx, nm, es, sums, rec = (sb(n, [P, 2, 4]) for n in "mx nm es sums rec".split())
        prob, probT = sb("prob", [P, 2, 512]), sb("probT", [P, 2, 512])
        yT = sb("yT", [P, 2, PAIRS, TOK])
        xx, x2, x2sq = (sb(n, [P, TPS, D]) for n in "xx x2 x2sq".split())
        ss, h2T = sb("ss", [P, TPS]), sb("h2T", [P, TOK])
        glog, top, idx = sb("glog", [P, TPS, EXPERTS]), sb("top", [P, TPS, 8]), sb("idx", [P, TPS, 8], U32)
        idxf, ntop, wsum = sb("idxf", [P, TPS, 8]), sb("ntop", [P, TPS]), sb("wsum", [P, TPS])
        wexp, wrec = sb("wexp", [P, TPS, TOPK]), sb("wrec", [P, TPS])
        hot, prod = sb("hot", [P, TPS, TOPK, EXPERTS]), sb("prod", [P, TPS, TOPK, EXPERTS])
        picked, place = sb("picked", [P, TPS, EXPERTS], BF16), sb("place", [P, TPS, EXPERTS])
        h2, slot, sent = m["h2"], m["slot"], m["sent"]
        score = [ps(f"score{i}") for i in range(3)]
        turned = [ps(f"turned{i}") for i in range(2)]
        side_q, side_f, side_g = ps("side_q"), ps("side_f"), ps("side_g")
        names = (
            "filled part constants bias_in ready stat0 rs0 xn xT_ps xT z_ps zT a_ps aT az_ps a_tok z expo gelu tanh slope apdf sloped "
            "rT_ps rT hr_ps h r dh_ps da g_ps w out_ps x1 "
            "stat small norms hn hn_ps hT qkv_ps cos sin added qk_ps qk_out v_out "
            "s_ps mx nm es_in exped den rec normed t_ps probT y_ps yT "
            "proj_ps xx x2 ss rms2 h2 h2_ps h2T gate_ps glog top w_in wexp wrec idx idxf hot picked rank_ps "
            "place prod masksum slotf slot x_sum held_v held_p").split()
        s = {n: ctx.enter_context(nc.semaphore("l_" + n)) for n in names}
        block = ctx.enter_context(nc.Block())
        FIRST, LAST = 6, SEQS - 3

        def live(k):
            return not isinstance(k, int) or 0 <= k < SEQS

        def run(eng, iteration):
            for n in range(FIRST):
                iteration(n, n % 2)
            with eng.Fori(0, (LAST + 1 - FIRST) // 2) as j:
                for par in range(2):
                    iteration(j * 2 + (FIRST + par), par)
            for n in range(LAST + 1, SEQS + 4):
                iteration(n, n % 2)

        def tile_of(q, t):
            return bass.ds(q * TPS + t, 1)

        def at_unit(n, par, u):
            A, p = n - 3, (par + 1) % 2
            if u >= UNITS:
                A, p, u = A + 1, 1 - p, u - UNITS
            elif u < 0:
                A, p, u = A - 1, 1 - p, u + UNITS
            return A, p, u, A * UNITS + (u + 1)

        @block.sync
        def _(sp):
            start_loads(m, sp, ["x_loaded", "small_loaded", "attn_loaded", "moe_loaded"])
            for j in range(TAIL):
                row = EXPERTS * REGION + j * P
                sp.dma_start(m["xs"][row:row + P, :], m["zeros"][:]).then_inc(m["tail_zeroed"], 16)
            sp.wait_ge(s["part"], 5)
            for k in range(3):
                sp.dma_start(m["bias3"][k:k + 1, :], part[:, k, :]) \
                    .then_inc(s["bias_in"], 16)
            sp.wait_ge(s["bias_in"], 3 * 16)

        @block.tensor
        def _(pe):
            mm, tr = nc.tensor.matmul, nc.tensor.transpose

            def bias(dst, c0, c1):
                mm(dst, m["ones_bf"][0:3, :], m["bias3"][:, c0:c1], start=True, stop=False)

            def scores(n, par, u):
                A, ap, u, done = at_unit(n, par, u)
                if not live(A):
                    return
                pairs, second, _ = unit(u)
                g2 = pairs[0] // 4
                dst = score[u % 3]
                if u == 0:
                    pe.wait_ge(s["qk_out"], A * CHUNKS + 4)
                if u == 6:
                    pe.wait_ge(s["qk_out"], A * CHUNKS + CHUNKS)
                after(pe, s["exped"], done - 3)
                if second:
                    mm(dst[:], m["ident_bf"][:], m["mask2"][:], start=True, stop=False)
                    mm(dst[:], qT[:, ap, pairs[0], P:TOK], kpad[:, ap, g2, :, :], start=False, stop=True) \
                        .then_inc(s["s_ps"], 1)
                else:
                    mm(dst[:], m["ident_bf"][:], m["mask1"][:], start=True, stop=False)
                    for k, p in enumerate(pairs):
                        ins = mm(dst[:, k * 2 * P:(k + 1) * 2 * P], qT[:, ap, p, 0:P], kpad[:, ap, g2, :, 0:P],
                                 start=False, stop=(k == 1))
                    ins.then_inc(s["s_ps"], 1)

            def turn_probs(n, par, u):
                A, ap, u, done = at_unit(n, par, u)
                if not live(A):
                    return
                after(pe, s["yT"], done - 2)
                pe.wait_ge(s["normed"], done)
                for k in range(4):
                    ins = tr(turned[u % 2][:, k * P:(k + 1) * P], prob[:, u % 2, k * P:(k + 1) * P], ident[:])
                ins.then_inc(s["t_ps"], 1)

            def values(n, par, u):
                A, ap, u, done = at_unit(n, par, u)
                if not live(A):
                    return
                pairs, second, _ = unit(u)
                g2 = pairs[0] // 4
                pe.wait_ge(s["probT"], done)
                for k in range(2):
                    for hh in range(2):
                        g = 2 * g2 + hh
                        blk = 2 * hh + k if second else 2 * k + hh
                        dst = turned[u % 2][hh * DH:(hh + 1) * DH, 0:P] if second else \
                            turned[u % 2][hh * DH:(hh + 1) * DH, k * P:(k + 1) * P]
                        ins = mm(dst, vv[:, ap, k if second else 0, g * DH:(g + 1) * DH],
                                 probT[:, u % 2, blk * P:(blk + 1) * P],
                                 start=(k == 0 or not second), stop=(k == 1 or not second))
                ins.then_inc(s["y_ps"], 1)

            def x_turn(n, par):
                F = n
                if not live(F):
                    return
                after(pe, s["hT"], n - 1)
                pe.wait_ge(s["xn"], F * TPS + TPS)
                for t in range(TPS):
                    ins = tr(side_f[:, t * P:(t + 1) * P], xn[:, t, :], ident[:])
                ins.then_inc(s["xT_ps"], 1)

            def z_products(n, par):
                F, O = n, n - 1
                if not (live(F) or live(O)):
                    return
                if live(F):
                    pe.wait_ge(s["xT"], F + 1)
                    ins = mm(side_f[:, 0:TOK], m["tkT"][:], xnT[:, par, :], start=True, stop=True)
                else:
                    pe.wait_ge(s["hT"], O)
                if live(O):
                    ins = mm(side_f[:, TOK:], m["tqT"][:], xnT[:, 1 - par, :], start=True, stop=True)
                ins.then_inc(s["z_ps"], 1)

            def a_products(n, par):
                F, O = n, n - 1
                if not (live(F) or live(O)):
                    return
                pe.wait_ge(s["zT"], n + 1)
                after(pe, s["w"], 3 * n)
                if live(F):
                    ins = mm(side_f[0:HID, 0:TOK], fast[:, 0:HID], zT[:, 0, :], start=True, stop=True)
                if live(O):
                    ins = mm(side_f[0:HID, TOK:], fast[:, 0:HID], zT[:, 1, :], start=True, stop=True)
                ins.then_inc(s["a_ps"], 1)

            def z_rows(n, par):
                F = n
                if not live(F):
                    return
                pe.wait_ge(s["aT"], n + 1)
                for t in range(TPS):
                    mm(side_f[:, P + t * P:P + (t + 1) * P], xnT[:, par, t * P:(t + 1) * P], m["tkT"][:],
                       start=True, stop=True)
                for t in range(TPS):
                    ins = tr(side_f[:, t * HID:(t + 1) * HID], aT[:, 0, t * P:(t + 1) * P], ident[0:HID, 0:HID])
                ins.then_inc(s["az_ps"], 1)

            def residual_cols(n, par):
                F = n
                if not live(F):
                    return
                pe.wait_ge(s["a_tok"], F + 1)
                pe.wait_ge(s["z"], F + 1)
                mm(side_f[:, 0:TOK], dkvT[:], xnT[:, par, :], start=True, stop=False)
                pe.wait_ge(s["gelu"], n + 1)
                mm(side_f[:, 0:TOK], fast2[:], hT2[:, 0, :], start=False, stop=True).then_inc(s["rT_ps"], 1)

            def residual_rows(n, par):
                F = n
                if not live(F):
                    return
                pe.wait_ge(s["rT"], F + 1)
                for t in range(TPS):
                    dst, tok = side_f[:, P + t * P:P + (t + 1) * P], slice(t * P, (t + 1) * P)
                    mm(dst, xnT[:, par, tok], dkvT[:], start=True, stop=False)
                    mm(dst, hT2[:, 0, tok], fast2[:], start=False, stop=True)
                for t in range(TPS):
                    ins = tr(side_f[:, t * (HID + 1):(t + 1) * (HID + 1)], hT2[:, 0, t * P:(t + 1) * P],
                             ident[0:HID + 1, 0:HID + 1])
                ins.then_inc(s["hr_ps"], 1)

            def hidden_grad(n, par):
                F = n
                if not live(F):
                    return
                pe.wait_ge(s["h"], F + 1)
                pe.wait_ge(s["r"], F + 1)
                for t in range(TPS):
                    ins = mm(side_f[:, t * HID:(t + 1) * HID], rT[:, t * P:(t + 1) * P], fast[:, HID:],
                             start=True, stop=True)
                ins.then_inc(s["dh_ps"], 1)

            def output(n, par):
                O = n - 1
                if not live(O):
                    return
                after(pe, s["da"], n + 1 if live(n) else 0)
                if not live(n):
                    pe.wait_ge(s["gelu"], n + 1)
                for t in range(TPS):
                    dst, tok = side_f[:, t * P:(t + 1) * P], slice(t * P, (t + 1) * P)
                    mm(dst, xnT[:, 1 - par, tok], m["tqT"][:], start=True, stop=False)
                    ins = mm(dst, hT2[:, 1, tok], fast2[:], start=False, stop=True)
                ins.then_inc(s["out_ps"], 1)

            def gradients(n, par):
                F, O = n, n - 1
                if not live(F):
                    return
                pe.wait_ge(s["da"], F + 1)
                if live(O):
                    pe.wait_ge(s["x1"], O + 1)
                for t in range(TPS):
                    mm(side_f[:, HID:2 * HID], r[:, t, :], h[:, t, 0:HID], start=(t == 0), stop=(t == TPS - 1))
                for t in range(TPS):
                    mm(side_f[0:HID + 1, P:2 * P], h[:, t, :], r[:, t, :], start=(t == 0), stop=(t == TPS - 1))
                for t in range(TPS):
                    mm(side_f[:, 0:HID], z[:, t, :], da[:, t, :], start=(t == 0), stop=(t == TPS - 1))
                for t in range(TPS):
                    ins = mm(side_f[0:HID, 2 * P:2 * P + 1], da[:, t, :], h[:, t, HID:HID + 1],
                             start=(t == 0), stop=(t == TPS - 1))
                ins.then_inc(s["g_ps"], 1)

            def norm_turn(n, par):
                O = n - 1
                if not live(O):
                    return
                if live(n):
                    pe.wait_ge(s["w"], 3 * n + 3)
                else:
                    pe.wait_ge(s["x1"], O + 1)
                pe.wait_ge(s["hn"], O * TPS + TPS)
                for t in range(TPS):
                    ins = tr(side_f[:, t * P:(t + 1) * P], hn[:, t, :], ident[:])
                ins.then_inc(s["hn_ps"], 1)

            def qkv(n, par, c):
                N = n - 2
                if not live(N):
                    return
                t, part = c % 2, (2, 0, 1)[c // 2]
                if c == 0:
                    pe.wait_ge(s["hT"], N + 1)
                if isinstance(n, int) and n == 2 and c == 0:
                    pe.wait_ge(m["attn_loaded"], ATTN_LOADS * 16)
                    pe.wait_ge(s["constants"], 1)
                    pe.wait_ge(s["bias_in"], 3 * 16)
                after(pe, s["qk_out"], N * CHUNKS + c)
                bias(side_q[:], part * 512, (part + 1) * 512)
                mm(side_q[:], hT[:, t * P:(t + 1) * P], m["wqkv"][:, part * 512:(part + 1) * 512],
                   start=False, stop=True).then_inc(s["qkv_ps"], 1)

            def qk_turn(n, par, c):
                N = n - 2
                if not live(N):
                    return
                if c < 2:
                    pe.wait_ge(s["v_out"], N * TPS + c + 1)
                pe.wait_ge(s["added"], N * CHUNKS + c + 1)
                for k in range(2 if c < 2 else 4):
                    ins = tr(side_q[:, k * P:(k + 1) * P], t_cos[:, k * P:(k + 1) * P], ident[:])
                ins.then_inc(s["qk_ps"], 1)

            def project(t, k):
                def stage(n, par):
                    B = n - 4
                    if not live(B):
                        return
                    cols = slice(t * P, (t + 1) * P)
                    if t == 1 and k == 0:
                        after(pe, s["place"], B)
                    pe.wait_ge(s["yT"], B * UNITS + UNITS - t * (3 - 2 * k))
                    if k == 0:
                        bias(side_g[:, cols], QKV, QKV + D)
                    for p in range(4 * k, 4 * k + 4):
                        ins = mm(side_g[:, cols], yT[:, par, p, cols], m["wproj"][:, p, :], start=False,
                                 stop=(p == PAIRS - 1))
                    ins.then_inc(s["proj_ps"], 1)
                return stage

            def h2_turn(n, par):
                B = n - 4
                if not live(B):
                    return
                pe.wait_ge(s["h2"], B * TPS + TPS)
                for t in range(TPS):
                    ins = tr(side_g[:, t * P:(t + 1) * P], h2[:, par, t, 0:D], ident[:])
                ins.then_inc(s["h2_ps"], 1)

            def gate(n, par):
                B = n - 4
                if not live(B):
                    return
                pe.wait_ge(s["h2T"], B + 1)
                for t in range(TPS):
                    cols = slice(t * EXPERTS, (t + 1) * EXPERTS)
                    bias(side_g[:, cols], QKV + D, QKV + D + EXPERTS)
                    ins = mm(side_g[:, cols], h2T[:, t * P:(t + 1) * P], m["gate"][:], start=False, stop=True)
                ins.then_inc(s["gate_ps"], 1)

            def ranks(n, par):
                B = n - 4
                if not live(B):
                    return
                pe.wait_ge(s["picked"], B * TPS + TPS)
                for t in range(TPS):
                    cols = slice(t * EXPERTS, (t + 1) * EXPERTS)
                    mm(side_g[:, cols], m["ones_bf"][:], m["masksum"][:], start=True, stop=False)
                    if t == 1:
                        mm(side_g[:, cols], m["ones_bf"][:], picked[:, 0, :], start=False, stop=False)
                    ins = mm(side_g[:, cols], m["before"][:], picked[:, t, :], start=False, stop=True)
                ins.then_inc(s["rank_ps"], 1)

            side = {0: [x_turn, project(1, 0)], 1: [z_products, project(1, 1)], 2: [a_products, project(0, 0)],
                    3: [z_rows, project(0, 1)], 5: [residual_cols], 6: [residual_rows, h2_turn],
                    7: [hidden_grad, gate], 8: [output], 9: [ranks], 10: [gradients], 11: [norm_turn]}

            def keep_clock(count):
                for _ in range(count):
                    mm(score[2][:], m["ones_bf"][:], filler[:], start=True, stop=True)

            def iteration(n, par):
                for u in range(UNITS):
                    scores(n, par, u + 2)
                    if u % 2 == 0:
                        qkv(n, par, u // 2)
                    if u > 5 and u % 2 == 1:
                        values(n, par, u - 1)
                    for stage in side.get(u, []):
                        stage(n, par)
                    if not (u > 5 and u % 2 == 1):
                        values(n, par, u - 1)
                    if u % 2 == 1:
                        qk_turn(n, par, u // 2)
                    turn_probs(n, par, u)
                    if isinstance(n, int) and (n < 3 or n == SEQS + 3):
                        keep_clock(8 if n == 1 and u == UNITS - 2 else 1)

            pe.wait_ge(s["filled"], 1)
            keep_clock(8)
            pe.wait_ge(m["first_loaded"], FIRST_LOADS * 16)
            pe.wait_ge(s["ready"], 4)
            run(pe, iteration)

        @block.vector
        def _(v):
            V = nc.vector

            def quotients(n, par, u):
                A, ap, u, done = at_unit(n, par, u)
                if not live(A):
                    return
                cols = unit(u)[2]
                b, w = u % 2, cols.stop - cols.start
                v.wait_ge(s["exped"], done)
                V.tensor_tensor(sums[:, b, 0:w], sums[:, b, 0:w], es[:, b, 0:w], ALU.add).then_inc(s["den"], 1)
                v.wait_ge(s["den"], done)
                V.reciprocal(rec[:, b, 0:w], sums[:, b, 0:w]).then_inc(s["rec"], 1)
                v.wait_ge(s["rec"], done)
                k = 512 // w
                for j in range(w):
                    ins = V.tensor_scalar(prob[:, b, j * k:(j + 1) * k], prob[:, b, j * k:(j + 1) * k],
                                          rec[:, b, j:j + 1], None, ALU.mult)
                ins.then_inc(s["normed"], 1)

            def maxima(n, par, u, between=None):
                A, ap, u, done = at_unit(n, par, u)
                if live(A):
                    cols = unit(u)[2]
                    b, w = u % 2, cols.stop - cols.start
                    sink = m["negsink"][:, cols]
                    v.wait_ge(s["s_ps"], done)
                    V.tensor_reduce(mx[:, b, 0:w], score[u % 3][:].rearrange("p (h k) -> p h k", h=w), AX.X,
                                    ALU.max).then_inc(s["mx"], 1)
                if between:
                    between()
                if live(A):
                    v.wait_ge(s["mx"], done)
                    V.scalar_tensor_tensor(out=nm[:, b, 0:w], in0=mx[:, b, 0:w], scalar=-0.125, in1=sink,
                                           op0=ALU.mult, op1=ALU.min).then_inc(s["nm"], 1)
                    v.wait_ge(s["nm"], done)
                    V.tensor_tensor(es[:, b, 0:w], nm[:, b, 0:w], sink, ALU.subtract).then_inc(s["es_in"], 1)

            def x_norm(n, par):
                F = n + 1
                if not live(F):
                    return
                if isinstance(n, int) and n in (0, 1):
                    v.wait_ge(s["rs0"], 2 * n + 4)
                after(v, s["xT_ps"], F)
                for t in range(TPS):
                    V.tensor_scalar(xn[:, t, :], x[:, tile_of(F, t), :].squeeze(1), mv0[:, tile_of(F, t), 0],
                                    rstd0[:, tile_of(F, t)], ALU.subtract, ALU.mult).then_inc(s["xn"], 1)

            def a_bias(n, par):
                F, O = n, n - 1
                if not (live(F) or live(O)):
                    return
                lo, hi = (0 if live(F) else TOK), (512 if live(O) else TOK)
                v.wait_ge(s["a_ps"], n + 1)
                V.tensor_scalar(aT[:].rearrange("p a t -> p (a t)")[:, lo:hi], side_f[0:HID, lo:hi], b1[:], TINY,
                                ALU.add, ALU.add).then_inc(s["aT"], 1)

            def a_rows(n, par):
                F = n
                if not live(F):
                    return
                v.wait_ge(s["az_ps"], F + 1)
                V.tensor_copy(a_tok[:], tiles(side_f[:, 0:TPS * HID])).then_inc(s["a_tok"], 1)
                V.tensor_copy(z[:], tiles(side_f[:, P:P + TOK])).then_inc(s["z"], 1)
                v.wait_ge(s["a_tok"], F + 1)
                V.scalar_tensor_tensor(out=expo[:], in0=a_tok[:], scalar=0.25, in1=a_tok[:],
                                       op0=ALU.mult, op1=ALU.mult).then_inc(s["expo"], 1)
                V.reciprocal(inv[:], a_tok[:]).then_inc(s["slope"], 1)

            def slope_pdf(n, par):
                F = n
                if not live(F):
                    return
                v.wait_ge(s["tanh"], F + 1)
                V.tensor_scalar(den[:], tanh[:], 1.0, None, ALU.add).then_inc(s["slope"], 1)
                V.tensor_scalar(num[:], tanh[:], -INV_SQRT_2PI, INV_SQRT_2PI, ALU.mult, ALU.add) \
                    .then_inc(s["slope"], 1)
                v.wait_ge(s["slope"], 6 * F + 2)
                V.reciprocal(den[:], den[:]).then_inc(s["slope"], 1)
                v.wait_ge(s["slope"], 6 * F + 3)
                V.tensor_tensor(num[:], num[:], a_tok[:], ALU.mult).then_inc(s["slope"], 1)
                v.wait_ge(s["slope"], 6 * F + 5)
                V.tensor_tensor(apdf[:], num[:], den[:], ALU.mult).then_inc(s["apdf"], 1)

            def slope_cdf(n, par):
                F = n
                if not live(F):
                    return
                v.wait_ge(s["hr_ps"], F + 1)
                V.tensor_copy(h[:], tiles(side_f[:, 0:TPS * (HID + 1)])).then_inc(s["h"], 1)
                V.tensor_copy(r[:], tiles(side_f[:, P:P + TOK])).then_inc(s["r"], 1)
                v.wait_ge(s["h"], F + 1)
                V.tensor_tensor(cdf[:], inv[:], h[:, :, 0:HID], ALU.mult).then_inc(s["slope"], 1)
                v.wait_ge(s["apdf"], F + 1)
                v.wait_ge(s["slope"], 6 * F + 6)
                V.tensor_tensor(cdf[:], cdf[:], apdf[:], ALU.add).then_inc(s["sloped"], 1)

            def hidden_grad(n, par):
                F = n
                if not live(F):
                    return
                v.wait_ge(s["sloped"], F + 1)
                v.wait_ge(s["dh_ps"], F + 1)
                V.tensor_tensor(da[:], tiles(side_f[:, 0:TPS * HID]), cdf[:], ALU.mult).then_inc(s["da"], 1)

            def output(n, par):
                O = n - 1
                if not live(O):
                    return
                v.wait_ge(s["out_ps"], O + 1)
                xt = x[:, bass.ds(O * TPS, TPS), :]
                V.tensor_tensor(xt, tiles(side_f[:, 0:TOK]), xt, ALU.add).then_inc(s["x1"], 1)
                hold(v, s["x1"], O + 1, s["held_v"])
                for t in range(TPS):
                    V.bn_stats(stats[:, t, :], x[:, tile_of(O, t), :].squeeze(1)).then_inc(s["stat"], 1)
                hold(v, s["stat"], 4 * O + 2, s["held_v"])
                for t in range(TPS):
                    V.bn_aggr(mv[:, t, :], stats[:, t, :]).then_inc(s["stat"], 1)

            def normed_rows(n, par):
                O = n - 1
                if not live(O):
                    return
                v.wait_ge(s["norms"], O + 1)
                for t in range(TPS):
                    V.tensor_scalar(hn[:, t, :], x[:, tile_of(O, t), :].squeeze(1), mv[:, t, 0:1], rms[:, t:t + 1],
                                    ALU.subtract, ALU.mult).then_inc(s["hn"], 1)

            def update(n, par):
                F = n
                if not live(F):
                    return
                v.wait_ge(s["g_ps"], F + 1)
                V.scalar_tensor_tensor(out=fast[:], in0=side_f[:, 0:2 * HID], scalar=GRAD_SCALE, in1=fast[:],
                                       op0=ALU.mult, op1=ALU.add).then_inc(s["w"], 1)
                V.scalar_tensor_tensor(out=fast2[:], in0=side_f[0:HID + 1, P:2 * P], scalar=GRAD_SCALE,
                                       in1=fast2[:], op0=ALU.mult, op1=ALU.add).then_inc(s["w"], 1)
                V.scalar_tensor_tensor(out=b1[:], in0=side_f[0:HID, 2 * P:2 * P + 1], scalar=GRAD_SCALE,
                                       in1=b1[:], op0=ALU.mult, op1=ALU.add).then_inc(s["w"], 1)

            def rope(n, par, c):
                N = n - 2
                if not live(N):
                    return
                t, heads = c % 2, (4 if c < 2 else 8)
                if isinstance(n, int) and n == 2 and c == 0:
                    v.wait_ge(m["attn_loaded"], ATTN_LOADS * 16)
                v.wait_ge(s["qkv_ps"], N * CHUNKS + c + 1)
                after(v, s["qk_ps"], N * CHUNKS + c)
                src = side_q[:, 0:heads * DH].rearrange("p (h a f) -> p h a f", h=heads, a=2)
                cos = m["rope"][:, t, 0, :][:, None, None, :].broadcast_to([P, heads, 2, HALF])
                sin = m["rope"][:, t, 1, :][:, None, :].broadcast_to([P, heads, HALF])
                dc = t_cos[:, 0:heads * DH].rearrange("p (h a f) -> p h a f", h=heads, a=2)
                dn = t_sin[:, 0:heads * DH].rearrange("p (h a f) -> p h a f", h=heads, a=2)
                V.tensor_tensor(dc, src, cos, ALU.mult).then_inc(s["cos"], 1)
                V.scalar_tensor_tensor(out=dn[:, :, 0, :], in0=src[:, :, 1, :], scalar=-1.0, in1=sin,
                                       op0=ALU.mult, op1=ALU.mult).then_inc(s["sin"], 1)
                V.tensor_tensor(dn[:, :, 1, :], src[:, :, 0, :], sin, ALU.mult).then_inc(s["sin"], 1)

            def centred(n, par):
                B = n - 4
                if not live(B):
                    return
                for t in range(TPS):
                    V.tensor_scalar(xx[:, t, :], x[:, tile_of(B, t), :].squeeze(1), mean_all[:, tile_of(B, t)],
                                    rs_all[:, tile_of(B, t)], ALU.subtract, ALU.mult).then_inc(s["xx"], 1)

            def attended(n, par):
                B = n - 4
                if not live(B):
                    return
                v.wait_ge(s["xx"], TPS * B + TPS)
                after(v, s["x_sum"], B)
                v.wait_ge(s["proj_ps"], 4 * B + 4)
                V.tensor_tensor(x2[:], tiles(side_g[:, 0:TOK]), xx[:], ALU.add).then_inc(s["x2"], 1)
                v.wait_ge(s["x2"], B + 1)
                for t in range(TPS):
                    V.tensor_tensor_reduce(out=x2sq[:, t, :], in0=x2[:, t, :], in1=x2[:, t, :], scale=1.0,
                                           scalar=0.0, op0=ALU.mult, op1=ALU.add,
                                           accum_out=ss[:, t:t + 1]).then_inc(s["ss"], 1)

            def h2_rows(n, par):
                B = n - 4
                if not live(B):
                    return
                after(v, sent[par], (B - par) * (TPS * TOPK * 8))
                v.wait_ge(s["rms2"], 2 * B + 2)
                for t in range(TPS):
                    V.tensor_scalar(h2[:, par, t, 0:D], x2[:, t, :], ss[:, t:t + 1], None, ALU.mult).then_inc(s["h2"], 1)
                V.tensor_copy(h2[:, par, :, D + TOPK:D + 2 * TOPK], m["pick_row"][:, bass.ds(B * TPS, TPS), :])

            def pick(n, par):
                B = n - 4
                if not live(B):
                    return
                v.wait_ge(s["gate_ps"], B + 1)
                V.tensor_copy(glog[:], side_g[:, 0:TPS * EXPERTS].rearrange("p (t e) -> p t e", t=TPS)) \
                    .then_inc(s["glog"], 1)
                hold(v, s["glog"], B + 1, s["held_v"])
                for t in range(TPS):
                    V.max(top[:, t, :], glog[:, t, :]).then_inc(s["top"], 1)
                v.wait_ge(s["top"], TPS * B + TPS)
                V.tensor_scalar(ntop[:], top[:, :, 0], -1.0, None, ALU.mult).then_inc(s["w_in"], 1)
                for t in range(TPS):
                    V.max_index(idx[:, t, :], top[:, t, :], glog[:, t, :]).then_inc(s["idx"], 1)

            def one_hot(n, par):
                B = n - 4
                if not live(B):
                    return
                v.wait_ge(s["idx"], TPS * B + TPS)
                V.tensor_copy(idxf[:], idx[:]).then_inc(s["idxf"], 1)
                v.wait_ge(s["idxf"], B + 1)
                for t in range(TPS):
                    V.tensor_tensor(hot[:, t], m["iota_e"][:, None, :].broadcast_to([P, TOPK, EXPERTS]),
                                    idxf[:, t, 0:TOPK][:, :, None].broadcast_to([P, TOPK, EXPERTS]), ALU.is_equal) \
                        .then_inc(s["hot"], 1)
                v.wait_ge(s["hot"], TPS * B + TPS)
                with nc.allow_low_precision("sums of four 0/1 values, exact in bfloat16"):
                    for t in range(TPS):
                        V.tensor_reduce(picked[:, t, :], hot[:, t].rearrange("p k e -> p e k"), AX.X, ALU.add) \
                            .then_inc(s["picked"], 1)

            def places(n, par):
                B = n - 4
                if not live(B):
                    return
                v.wait_ge(s["rank_ps"], B + 1)
                V.tensor_tensor(place[:], side_g[:, 0:TPS * EXPERTS].rearrange("p (t e) -> p t e", t=TPS),
                                m["base_e"][:, None, :].broadcast_to([P, TPS, EXPERTS]), ALU.add) \
                    .then_inc(s["place"], 1)
                v.wait_ge(s["wexp"], TPS * B + TPS)
                V.reciprocal(wrec[:], wsum[:]).then_inc(s["wrec"], 1)

            def slots(n, par):
                B = n - 4
                if not live(B):
                    return
                v.wait_ge(s["prod"], B + 1)
                slotf = h2[:, par, :, D:D + TOPK]
                V.tensor_reduce(slotf, prod[:], AX.X, ALU.add).then_inc(s["slotf"], 1)
                v.wait_ge(s["wrec"], B + 1)
                V.tensor_tensor(h2[:, par, :, D + 2 * TOPK:WIDE], wexp[:],
                                wrec[:, :, None].broadcast_to([P, TPS, TOPK]), ALU.mult)
                v.wait_ge(s["slotf"], B + 1)
                V.tensor_copy(slot[:, par].rearrange("p (t k) -> p t k", t=TPS), slotf).then_inc(s["slot"], 1)

            side = {2: [a_bias], 3: [a_rows], 4: [attended], 5: [slope_pdf, h2_rows], 6: [slope_cdf],
                    7: [pick, hidden_grad], 8: [one_hot], 9: [output], 10: [normed_rows, places],
                    11: [x_norm, slots]}

            def iteration(n, par):
                for u in range(UNITS):
                    if u == 11:
                        update(n, par)
                    quotients(n, par, u)
                    if u == 3:
                        centred(n, par)
                    maxima(n, par, u + 2, between=(lambda: rope(n, par, u // 2)) if u % 2 == 0 else None)
                    if isinstance(n, int) and n == 0 and 3 <= u < 11:
                        if u == 3:
                            v.wait_ge(m["x_loaded"], X_LOADS * 16)
                        input_stats(4 * u - 10, min(4 * u - 6, TILES))
                    if isinstance(n, int) and n == 1 and u == 0:
                        constants()
                    for stage in side.get(u, []):
                        stage(n, par)

            def input_stats(first, last):
                for t in range(first, last):
                    V.bn_stats(stats0[:, t, :], x[:, t, :]).then_inc(s["stat0"], 1)
                v.wait_ge(s["stat0"], first + last)
                for t in range(first, last):
                    V.bn_aggr(mv0[:, t, :], stats0[:, t, :]).then_inc(s["stat0"], 1)

            def constants():
                v.wait_ge(m["small_loaded"], SMALL_LOADS * 16)
                src = m["bias_f"]
                for k in range(3):
                    V.tensor_copy(part[:, k, :], src[:]).then_inc(s["part"], 1)
                    if k < 2:
                        v.wait_ge(s["part"], 2 * k + 1)
                        V.tensor_tensor(rest[:, k, :], src[:], part[:, k, :], ALU.subtract).then_inc(s["part"], 1)
                        v.wait_ge(s["part"], 2 * k + 2)
                        src = rest[:, k, :]
                V.tensor_copy(m["ident_bf"][:], ident[:])
                V.tensor_copy(m["mask2"][:], m["mask_f"][:, None, :].broadcast_to([P, 2, 2 * P]))
                V.tensor_copy(m["mask1"][:], m["mask_f"][:, None, P:].broadcast_to([P, 4, P]))
                V.tensor_copy(m["before"][:], m["before_f"][:])
                V.tensor_scalar(m["base_e"][:], m["iota_e"][:], float(REGION), None, ALU.mult)
                V.tensor_scalar(m["negsink"][:], m["negsink"][:], -1.0, None, ALU.mult).then_inc(s["constants"], 1)
                v.wait_ge(s["constants"], 1)

            V.memset(hT2[HID:HID + 1, :, :], 1.0).then_inc(s["ready"], 1)
            v.wait_ge(m["first_loaded"], FIRST_LOADS * 16)
            V.tensor_tensor(dkvT[:], m["tkT"][:], m["tvT"][:], ALU.subtract).then_inc(s["ready"], 1)
            input_stats(0, TPS)
            v.wait_ge(s["rs0"], 2)
            x_norm(-1, 1)
            run(v, iteration)

        @block.scalar
        def _(act):
            A_ = nc.scalar

            def exps(n, par, u):
                A, ap, u, done = at_unit(n, par, u)
                if not live(A):
                    return
                _, second, cols = unit(u)
                b, w = u % 2, cols.stop - cols.start
                act.wait_ge(s["nm"], done)
                after(act, s["t_ps"], done - 2)
                k = 512 // w
                for j in range(w):
                    cols = slice(j * k, (j + 1) * k)
                    ins = A_.activation(prob[:, b, cols], score[u % 3][:, cols], ACT.Exp, bias=nm[:, b, j:j + 1],
                                        scale=0.125, accum_out=sums[:, b, j:j + 1])
                act.wait_ge(s["es_in"], done)
                A_.activation(es[:, b, 0:w], es[:, b, 0:w], ACT.Exp).then_inc(s["exped"], 1)

            def take_probs(n, par, u):
                A, ap, u, done = at_unit(n, par, u)
                if not live(A):
                    return
                act.wait_ge(s["t_ps"], done)
                after(act, s["y_ps"], done - 2)
                A_.copy(probT[:, u % 2, :], turned[u % 2][:]).then_inc(s["probT"], 1)

            def take_y(n, par, u):
                A, ap, u, done = at_unit(n, par, u)
                if not live(A):
                    return
                pairs, second, _ = unit(u)
                act.wait_ge(s["y_ps"], done)
                if second:
                    A_.copy(yT[:, ap, pairs[0], P:TOK], turned[u % 2][:, 0:P]).then_inc(s["yT"], 1)
                else:
                    A_.copy(yT[:, ap, pairs[0]:pairs[0] + 2, 0:P],
                            turned[u % 2][:, 0:2 * P].rearrange("p (k t) -> p k t", k=2)).then_inc(s["yT"], 1)

            def xT_out(n, par):
                if not live(n):
                    return
                act.wait_ge(s["xT_ps"], n + 1)
                A_.copy(xnT[:, par, :], side_f[:, 0:TOK]).then_inc(s["xT"], 1)

            def zT_out(n, par):
                F, O = n, n - 1
                if not (live(F) or live(O)):
                    return
                lo, hi = (0 if live(F) else 1), (2 if live(O) else 1)
                act.wait_ge(s["z_ps"], n + 1)
                A_.copy(zT[:, lo:hi, :], side_f[:].rearrange("p (a t) -> p a t", a=2)[:, lo:hi, :]) \
                    .then_inc(s["zT"], 1)

            def gelus(n, par):
                F, O = n, n - 1
                if not (live(F) or live(O)):
                    return
                lo, hi = (0 if live(F) else 1), (2 if live(O) else 1)
                act.wait_ge(s["aT"], n + 1)
                A_.activation(hT2[0:HID, lo:hi, :], aT[:, lo:hi, :], ACT.Gelu).then_inc(s["gelu"], 1)
                if live(F):
                    act.wait_ge(s["expo"], F + 1)
                    A_.activation(tanh[:], expo[:], ACT.Tanh).then_inc(s["tanh"], 1)

            def rT_out(n, par):
                if not live(n):
                    return
                act.wait_ge(s["rT_ps"], n + 1)
                A_.copy(rT[:], side_f[:, 0:TOK]).then_inc(s["rT"], 1)

            def hT_out(n, par):
                O = n - 1
                if not live(O):
                    return
                if isinstance(n, int) and n == 1:
                    act.wait_ge(m["attn_loaded"], ATTN_LOADS * 16)
                after(act, s["qkv_ps"], O * CHUNKS)
                act.wait_ge(s["hn_ps"], O + 1)
                A_.activation(hT[:], side_f[:, 0:TOK], ACT.Copy, scale=m["norms"][:, 0:1]).then_inc(s["hT"], 1)

            def v_out(n, par, c):
                N = n - 2
                if not live(N):
                    return
                act.wait_ge(s["sin"], 2 * (N * CHUNKS + c) + 2)
                after(act, s["y_ps"], (N - 1) * UNITS)
                A_.copy(vv[:, par, c, :], side_q[:, KV * DH:2 * KV * DH]).then_inc(s["v_out"], 1)

            def qk_out(n, par, c):
                N = n - 2
                if not live(N):
                    return
                t = c % 2
                tok = slice(t * P, (t + 1) * P)
                act.wait_ge(s["qk_ps"], N * CHUNKS + c + 1)
                if c < 2:
                    for half in range(2):
                        rows = slice(half * DH, (half + 1) * DH)
                        ins = A_.copy(kpad[rows, par, :, half, tok],
                                      side_q[rows, 0:2 * P].rearrange("p (g t) -> p g t", g=2))
                else:
                    p0 = 4 * (c // 2 - 1)
                    ins = A_.copy(qT[:, par, p0:p0 + 4, tok], side_q[:].rearrange("p (b t) -> p b t", b=4))
                ins.then_inc(s["qk_out"], 1)

            def h2T_out(n, par):
                B = n - 4
                if not live(B):
                    return
                act.wait_ge(s["h2_ps"], B + 1)
                A_.activation(h2T[:], side_g[:, 0:TOK], ACT.Copy, scale=m["norms"][:, 1:2]).then_inc(s["h2T"], 1)

            def weights(n, par):
                B = n - 4
                if not live(B):
                    return
                act.wait_ge(s["w_in"], B + 1)
                for t in range(TPS):
                    A_.activation(wexp[:, t, :], top[:, t, 0:TOPK], ACT.Exp, bias=ntop[:, t:t + 1],
                                  accum_out=wsum[:, t:t + 1]).then_inc(s["wexp"], 1)

            side = {0: [xT_out], 1: [zT_out], 4: [gelus], 5: [rT_out], 6: [h2T_out], 8: [weights], 11: [hT_out]}

            def iteration(n, par):
                for u in range(UNITS):
                    take_probs(n, par, u - 1)
                    take_y(n, par, u - 2)
                    exps(n, par, u + 1)
                    if u in (0, 2):
                        v_out(n, par, u // 2)
                    if u % 2 == 1:
                        qk_out(n, par, u // 2)
                    for stage in side.get(u, []):
                        stage(n, par)

            run(act, iteration)

        @block.gpsimd
        def _(pool):
            g = nc.gpsimd

            def rope_add(n, par, c):
                N = n - 2
                if not live(N):
                    return
                w = (4 if c < 2 else 8) * DH
                pool.wait_ge(s["sin"], 2 * (N * CHUNKS + c) + 2)
                g.tensor_tensor(t_cos[:, 0:w], t_cos[:, 0:w], t_sin[:, 0:w], ALU.add).then_inc(s["added"], 1)

            def norms(n, par):
                O = n - 1
                if not live(O):
                    return
                hold(pool, s["stat"], 4 * O + 4, s["held_p"])
                g.tensor_scalar(rs[:], mv[:, :, 1], EPS, None, ALU.add).then_inc(s["small"], 1)
                g.tensor_copy(mean_all[:, bass.ds(O * TPS, TPS)], mv[:, :, 0])
                pool.wait_ge(s["small"], O * 6 + 1)
                g.tensor_tensor(rs[:], rs[:], m["neghalf"][:, 0:TPS], ALU.pow).then_inc(s["small"], 1)
                pool.wait_ge(s["small"], O * 6 + 2)
                g.tensor_tensor(sq[:], rs[:], rs[:], ALU.mult).then_inc(s["small"], 1)
                g.tensor_copy(rs_all[:, bass.ds(O * TPS, TPS)], rs[:])
                pool.wait_ge(s["small"], O * 6 + 3)
                g.tensor_tensor(sq[:], sq[:], mv[:, :, 1], ALU.mult).then_inc(s["small"], 1)
                hold(pool, s["small"], O * 6 + 4, s["held_p"])
                g.tensor_scalar(sq[:], sq[:], EPS, None, ALU.add).then_inc(s["small"], 1)
                pool.wait_ge(s["small"], O * 6 + 5)
                g.tensor_tensor(sq[:], sq[:], m["neghalf"][:, 0:TPS], ALU.pow).then_inc(s["small"], 1)
                pool.wait_ge(s["small"], O * 6 + 6)
                g.tensor_tensor(rms[:], sq[:], rs[:], ALU.mult).then_inc(s["norms"], 1)

            def rms2(n, par):
                B = n - 4
                if not live(B):
                    return
                hold(pool, s["ss"], B * 2 + 2, s["held_p"])
                g.tensor_scalar(ss[:], ss[:], 1.0 / D, EPS, ALU.mult, ALU.add).then_inc(s["rms2"], 1)
                pool.wait_ge(s["rms2"], 2 * B + 1)
                g.tensor_tensor(ss[:], ss[:], m["neghalf"][:, 0:TPS], ALU.pow).then_inc(s["rms2"], 1)
                xt = x[:, bass.ds(B * TPS, TPS), :]
                g.tensor_tensor(xt, xt, x2[:], ALU.add).then_inc(s["x_sum"], 1)

            def spread(n, par):
                B = n - 4
                if not live(B):
                    return
                pool.wait_ge(s["place"], B + 1)
                g.tensor_tensor(prod[:], hot[:], place[:, :, None, :].broadcast_to([P, TPS, TOPK, EXPERTS]),
                                ALU.mult).then_inc(s["prod"], 1)
                for t in range(TPS):
                    after(pool, s["masksum"], TPS * B + t)
                    g.tensor_tensor(m["masksum"][:], m["masksum"][:], picked[:, t, :], ALU.add) \
                        .then_inc(s["masksum"], 1)

            def send(n, par, i):
                B = n - 5
                if not live(B):
                    return
                if i == 0:
                    pool.wait_ge(s["h2"], TPS * B + TPS)
                    hold(pool, s["slot"], B + 1, s["held_p"])
                for c in range(2 * i, 2 * i + 2):
                    send_pick(m, 1 - par, c)

            side = {4: [rms2], 9: [norms], 10: [spread]}

            def iteration(n, par):
                for u in range(UNITS):
                    if u % 2 == 0:
                        rope_add(n, par, u // 2)
                    if u < TPS * TOPK // 2:
                        send(n, par, u)
                    for stage in side.get(u, []):
                        stage(n, par)

            g.memset(filler[:], 0.0).then_inc(s["filled"], 1)
            g.memset(kpad[:], 0.0).then_inc(s["ready"], 1)
            def input_scales(k, first, last):
                cols = slice(first, last)
                pool.wait_ge(s["stat0"], 2 * last)
                g.tensor_scalar(rstd0[:, cols], mv0[:, cols, 1], EPS, None, ALU.add).then_inc(s["rs0"], 1)
                pool.wait_ge(s["rs0"], 2 * k + 1)
                g.tensor_tensor(rstd0[:, cols], rstd0[:, cols], m["neghalf"][:, cols], ALU.pow).then_inc(s["rs0"], 1)

            input_scales(0, 0, TPS)
            g.memset(rs[:], 0.0).then_inc(s["ready"], 1)
            g.affine_select(out=m["upto"][:], in_=m["upto"][:], compare_op=ALU.is_ge, fill=0.0, base=0,
                            pattern=[[1, EXPERTS], [-1, EXPERTS]], channel_multiplier=0)
            input_scales(1, TPS, 6)
            input_scales(2, 6, TILES)
            run(pool, iteration)



def experts(m):
    nc, ident = m["nc"], m["ident"]
    with ExitStack() as ctx:
        def sb(name, shape, dt=F32):
            return ctx.enter_context(nc.sbuf_tensor("e_" + name, shape, dt))

        def ps(name, shape):
            return ctx.enter_context(nc.psum_tensor("e_" + name, shape, F32))

        cnt, ntile, cum = sb("cnt", [P, EXPERTS]), sb("ntile", [P, EXPERTS]), sb("cum", [P, EXPERTS])
        cnt_i, pad_i = sb("cnt_i", [P, EXPERTS], I32), sb("pad_i", [P, EXPERTS], I32)
        sq = sb("sq", [P, EXPERTS, EXPERTS])
        past, cost = sb("past", [P, COLS, EXPERTS]), sb("cost", [P, COLS, EXPERTS])
        exp_t, skip_t = sb("exp_t", [P, COLS]), sb("skip_t", [P, COLS])
        diag = sb("diag", [P, COLS, P])
        own = sb("own", [P, COLS * P])
        row_i = sb("row_i", [1, COLS * P], I32)
        codes = sb("codes", [1, COLS * P // GROUP], I32)
        xt = sb("xt", [P, 4, GROUP, WIDE])
        xT, act, hid, hidT = (sb(n, [P, 2, GROUP, D]) for n in "xT act hid hidT".split())
        yo = sb("yo", [P, 2, GROUP, D])
        eq, pick = sb("eq", [P, GROUP, TOPK]), sb("pick", [P, GROUP, 2, TOPK])
        mine = sb("mine", [P, 4, GROUP, 2])
        dest = sb("dest", [P, 4, GROUP], U32)
        p_x, p_h, p_y = ps("p_x", [P, 512]), ps("p_h", [P, 512]), ps("p_y", [P, 512])
        p_up = [ps(f"p_up{b}", [P, GROUP, 2 * DFF]) for b in range(2)]
        s = {n: ctx.enter_context(nc.semaphore("e_" + n)) for n in
             ("cnt_ps counted padded_a padded_b step placed rows_ps planned xT_ps xT up_ps act hid hidT_ps hidT y_ps y "
              "eq pick mine dest held sent_a sent_b in_a in_b in_c in_d").split()}
        arrived = [s[n] for n in ("in_a", "in_b", "in_c", "in_d")]
        sent = [s["sent_a"], s["sent_b"]]
        block = ctx.enter_context(nc.Block())
        FIRST = 6
        BODIES = (GROUPS - 2 - FIRST) // 4

        def live(g):
            return not isinstance(g, int) or 0 <= g < GROUPS

        def run(eng, step, load=None):
            def some(first, last):
                c = load(first, last - first) if load else {}
                return lambda k: c[k - first] if load else None
            c = some(0, FIRST)
            for g in range(-1, FIRST):
                step(g, g % 4, c(max(g, 0)), c(max(g - 2, 0)))
            with eng.Fori(0, BODIES) as i:
                c = load(i * 4 + (FIRST - 2), 6) if load else [None] * 6
                for k in range(4):
                    step(i * 4 + (FIRST + k), (FIRST + k) % 4, c[k + 2], c[k])
            c = some(GROUPS - 4, GROUPS)
            for g in range(GROUPS - 2, GROUPS + 2):
                step(g, g % 4, c(min(g, GROUPS - 1)), c(g - 2))

        def zero_pads(eng, first, signal):
            half = EXPERTS // 2
            for e0 in range(first * half, (first + 1) * half, 8):
                rows = nc.values_load_multi_w_load_instructions(
                    pad_i[0:1, e0:e0 + 8], engines=[eng.engine], min_val=0, max_val=ROWS - P)[1]
                for r in rows:
                    eng.dma_start(m["xs"][bass.ds(r, P), :], m["zeros"][:]).then_inc(signal, 16)

        @block.sync
        def _(sp):
            sp.wait_ge(s["counted"], 1)
            zero_pads(sp, 0, s["padded_a"])
            sp.wait_ge(s["placed"], 1)

            def first_rows(i):
                return nc.values_load_multi_w_load_instructions(
                    row_i[0:1, bass.ds(i * 4 * GROUP, 4 * GROUP)], engines=[sp.engine], min_val=0,
                    max_val=ROWS - P)[1]

            def load(rows, q):
                for j in range(GROUP):
                    sp.dma_start(xt[:, q, j, :], m["xs"][bass.ds(rows[q * GROUP + j], P), :]) \
                        .then_inc(arrived[q], 16)

            rows = first_rows(0)
            sp.wait_ge(s["padded_a"], EXPERTS // 2 * 16)
            sp.wait_ge(s["padded_b"], EXPERTS // 2 * 16)
            sp.wait_ge(m["tail_zeroed"], TAIL * 16)
            for par in range(2):
                sp.wait_ge(m["sent"][par], SEQS // 2 * TPS * TOPK * 16)
            for q in range(4):
                load(rows, q)
            with sp.Fori(1, GROUPS // 4) as i:
                rows = first_rows(i)
                for q in range(4):
                    sp.wait_ge(s["xT_ps"], i * 4 + (q - 3))
                    sp.wait_ge(s["dest"], i * 4 + (q - 3))
                    load(rows, q)
            for q in range(4):
                sp.wait_ge(arrived[q], GROUPS // 4 * GROUP * 16)

        @block.gpsimd
        def _(pool):
            g_ = nc.gpsimd
            for c in range(TPS * TOPK):
                send_pick(m, (SEQS - 1) % 2, c)
            with pool.Fori(0, GROUPS // 4) as i:
                for q in range(4):
                    hold(pool, s["y"], i * 4 + (q + 1), s["held"])
                    for j in range(GROUP):
                        g_.indirect_dma_start(m["ys"], bass.IndirectOffsetOnAxis(ap=dest[:, q, j:j + 1], axis=0),
                                              yo[:, q % 2, j, :], None).then_inc(sent[q % 2], 16)
            for b in range(2):
                pool.wait_ge(sent[b], GROUPS // 2 * GROUP * 16)

        @block.vector
        def _(v):
            V, n_ = nc.vector, [0]

            def step(ins):
                n_[0] += 1
                ins.then_inc(s["step"], 1)
                v.wait_ge(s["step"], n_[0])
            v.wait_ge(s["cnt_ps"], 1)
            step(V.tensor_copy(cnt[:], p_x[:, 0:EXPERTS]))
            V.tensor_tensor(pad_i[:], cnt[:], m["base_e"][:], ALU.add).then_inc(s["counted"], 1)
            step(V.tensor_scalar(cnt_i[:], cnt[:], float(P - 1), None, ALU.add))
            step(V.tensor_scalar(cnt_i[:], cnt_i[:], P.bit_length() - 1, None, ALU.arith_shift_right))
            step(V.tensor_copy(ntile[:], cnt_i[:]))
            step(V.tensor_tensor(sq[:], m["upto"][:], ntile[:, None, :].broadcast_to([P, EXPERTS, EXPERTS]), ALU.mult))
            step(V.tensor_reduce(cum[:], sq[:], AX.X, ALU.add))
            wide = [P, COLS, EXPERTS]
            step(V.tensor_tensor(past[:], cum[:, None, :].broadcast_to(wide),
                                 m["tile_id"][:, :, None].broadcast_to(wide), ALU.is_le))
            V.tensor_reduce(exp_t[:], past[:], AX.X, ALU.add)
            step(V.tensor_tensor(cost[:], past[:], ntile[:, None, :].broadcast_to(wide), ALU.mult))
            step(V.tensor_reduce(skip_t[:], cost[:], AX.X, ALU.add))
            step(V.tensor_tensor(skip_t[:], m["tile_id"][:], skip_t[:], ALU.subtract))
            step(V.scalar_tensor_tensor(out=skip_t[:], in0=exp_t[:], scalar=float(REGION // P), in1=skip_t[:],
                                        op0=ALU.mult, op1=ALU.add))
            V.tensor_scalar(exp_t[:], exp_t[:], float(EXPERTS - 1), None, ALU.min)
            for c in range(COLS):
                ins = V.tensor_scalar(diag[:, c, :], ident[:], skip_t[:, c:c + 1], None, ALU.mult)
            ins.then_inc(s["planned"], 1)
            v.wait_ge(s["rows_ps"], 1)
            V.tensor_scalar(row_i[:], p_x[0:1, 0:COLS * P], float(P), None, ALU.mult).then_inc(s["placed"], 1)
            V.tensor_copy(codes[:], p_y[0:1, 0:COLS * P // GROUP]).then_inc(s["placed"], 1)
            V.tensor_scalar(own[:], p_x[:, 0:COLS * P], float(P), m["tile_id"][:, 0:1], ALU.mult, ALU.add) \
                .then_inc(s["placed"], 1)
            v.wait_ge(s["placed"], 3)

            def find(g, q):
                if not live(g):
                    return
                info = xt[:, q, :, D:WIDE].rearrange("p j (a k) -> p j a k", k=TOPK)
                v.wait_ge(arrived[q], g * 16 + (GROUP * 16 - q * 16))
                V.tensor_tensor(eq[:], info[:, :, 0, :],
                                own[:, bass.ds(g * GROUP, GROUP)][:, :, None].broadcast_to([P, GROUP, TOPK]),
                                ALU.is_equal).then_inc(s["eq"], 1)

            def find_products(g, q):
                if not live(g):
                    return
                info = xt[:, q, :, D:WIDE].rearrange("p j (a k) -> p j a k", k=TOPK)
                v.wait_ge(s["eq"], g + 1)
                V.tensor_tensor(pick[:], info[:, :, 1:3, :], eq[:, :, None, :].broadcast_to([P, GROUP, 2, TOPK]),
                                ALU.mult).then_inc(s["pick"], 1)

            def find_sums(g, q):
                if not live(g):
                    return
                if not isinstance(g, int) or g >= 4:
                    v.wait_ge(sent[q % 2], g * 32 - (q % 2 + 2) * 32)
                v.wait_ge(s["pick"], g + 1)
                V.tensor_reduce(mine[:, q], pick[:], AX.X, ALU.add).then_inc(s["mine"], 1)

            def find_dest(g, q):
                if not live(g):
                    return
                v.wait_ge(s["mine"], g + 1)
                V.tensor_tensor(dest[:, q], mine[:, q, :, 0], m["row_id"][:, bass.ds(g * GROUP, GROUP)], ALU.max) \
                    .then_inc(s["dest"], 1)

            def work(g, q, up_code, down_code):
                b = q % 2
                find(g + 1, (q + 1) % 4)
                if live(g - 1):
                    h = g - 1
                    v.wait_ge(s["hidT_ps"], h + 1)
                    after(v, s["y_ps"], h - 1)
                    V.tensor_copy(hidT[:, 1 - b], p_h[:].rearrange("p (j t) -> p j t", j=GROUP)) \
                        .then_inc(s["hidT"], 1)
                find_products(g + 1, (q + 1) % 4)
                if live(g):
                    v.wait_ge(s["act"], g + 1)
                    after(v, s["hidT_ps"], g - 1)
                    V.tensor_tensor(hid[:, b], act[:, b], p_up[b][:, :, 0:DFF], ALU.mult).then_inc(s["hid"], 1)
                find_sums(g + 1, (q + 1) % 4)
                find_dest(g + 1, (q + 1) % 4)

            run(v, work)

        @block.scalar
        def _(act_):
            A = nc.scalar
            act_.wait_ge(s["counted"], 1)
            zero_pads(act_, 1, s["padded_b"])
            A.activation(act[:, 0, 0, 0:COLS], m["tile_id"][:], ACT.Silu)

            def work(g, q, up_code, down_code):
                b = q % 2
                if live(g + 1):
                    act_.wait_ge(s["xT_ps"], g + 2)
                    after(act_, s["up_ps"], g)
                    A.activation(xT[:, 1 - b], p_x[:].rearrange("p (j t) -> p j t", j=GROUP), ACT.Copy,
                                 scale=m["norms"][:, 1:2]).then_inc(s["xT"], 1)
                if live(g):
                    act_.wait_ge(s["up_ps"], g + 1)
                    after(act_, s["hid"], g - 1)
                    A.activation(act[:, b], p_up[b][:, :, DFF:2 * DFF], ACT.Silu).then_inc(s["act"], 1)
                if live(g - 2):
                    h, r = g - 2, (q - 2) % 4
                    act_.wait_ge(s["y_ps"], h + 1)
                    act_.wait_ge(s["dest"], h + 1)
                    if not isinstance(h, int) or h >= 2:
                        act_.wait_ge(sent[b], h * 32 - b * 32)
                    for j in range(GROUP):
                        ins = A.activation(yo[:, b, j, :], p_y[:, j * P:(j + 1) * P], ACT.Copy,
                                           scale=mine[:, r, j, 1:2])
                    ins.then_inc(s["y"], 1)
            run(act_, work)

        @block.tensor
        def _(pe):
            mm, tr = nc.tensor.matmul, nc.tensor.transpose
            mm(p_x[:, 0:EXPERTS], m["ones_bf"][:], m["masksum"][:], start=True, stop=True) \
                .then_inc(s["cnt_ps"], 1)
            pe.wait_ge(s["planned"], 1)
            for c in range(COLS):
                mm(p_y[0:1, c * P // GROUP:(c + 1) * P // GROUP], exp_t[:, c:c + 1], m["digits"][:],
                   start=True, stop=True)
                ins = mm(p_x[:, c * P:(c + 1) * P], m["ones"][:], diag[:, c, :], start=True, stop=True)
            ins.then_inc(s["rows_ps"], 1)
            pe.wait_ge(s["placed"], 3)
            pe.wait_ge(m["moe_loaded"], MOE_LOADS * 16)
            def load(first, count):
                return nc.values_load_multi_w_load_instructions(
                    codes[0:1, bass.ds(first, count)], engines=[pe.engine], min_val=0,
                    max_val=EXPERTS ** GROUP - 1)[1]

            def expert(code, j):
                return (code // EXPERTS ** j) % EXPERTS

            def work(g, q, up_code, down_code):
                b = q % 2
                if live(g + 1):
                    r = (q + 1) % 4
                    pe.wait_ge(arrived[r], g * 16 + (GROUP + 1 - r) * 16)
                    after(pe, s["xT"], g + 1)
                    for j in range(GROUP):
                        ins = tr(p_x[:, j * P:(j + 1) * P], xt[:, r, j, 0:D], ident[:])
                    ins.then_inc(s["xT_ps"], 1)
                if live(g):
                    pe.wait_ge(s["xT"], g + 1)
                    after(pe, s["hid"], g - 1)
                    for j in range(GROUP):
                        ins = mm(p_up[b][:, j, :], xT[:, b, j, :],
                                 m["wup"][:, bass.ds(expert(up_code, j) * (2 * DFF), 2 * DFF)],
                                 start=True, stop=True)
                    ins.then_inc(s["up_ps"], 1)
                if live(g - 1):
                    pe.wait_ge(s["hid"], g)
                    after(pe, s["hidT"], g - 1)
                    for j in range(GROUP):
                        ins = tr(p_h[:, j * P:(j + 1) * P], hid[:, 1 - b, j, :], ident[:])
                    ins.then_inc(s["hidT_ps"], 1)
                if live(g - 2):
                    pe.wait_ge(s["hidT"], g - 1)
                    after(pe, s["y"], g - 2)
                    for j in range(GROUP):
                        ins = mm(p_y[:, j * P:(j + 1) * P], hidT[:, b, j, :],
                                 m["wdown"][:, bass.ds(expert(down_code, j) * D, D)], start=True, stop=True)
                    ins.then_inc(s["y_ps"], 1)
            run(pe, work, load)


def combine(m):
    nc, x = m["nc"], m["x"]
    BUFS, LOADS = 4, 2
    with ExitStack() as ctx:
        def sb(name, shape, dt=F32):
            return ctx.enter_context(nc.sbuf_tensor("c_" + name, shape, dt))

        rows = sb("rows", [P, BUFS, LOADS, TOPK, D])
        two, one = sb("two", [P, BUFS, LOADS, 2, D]), sb("one", [P, BUFS, LOADS, D])
        res = sb("res", [P, BUFS, LOADS, D])
        loaded = [ctx.enter_context(nc.semaphore(f"c_loaded{b}")) for b in range(BUFS)]
        written = [ctx.enter_context(nc.semaphore(f"c_written{b}")) for b in range(BUFS)]
        halved, added, summed = (ctx.enter_context(nc.semaphore("c_" + n)) for n in ("halved", "added", "summed"))
        block = ctx.enter_context(nc.Block())
        N = TILES // LOADS

        def source(i):
            return m["ys"][SPARE + i * LOADS * P * TOPK:SPARE + (i + 1) * LOADS * P * TOPK, :] \
                .rearrange("(t p k) d -> p t k d", p=P, k=TOPK)

        @block.sync
        def _(sp):
            for i in range(N):
                if i >= BUFS:
                    sp.wait_ge(halved, i - BUFS + 1)
                sp.dma_start(rows[:, i % BUFS], source(i)).then_inc(loaded[i % BUFS], 16)

        @block.vector
        def _(v):
            V = nc.vector
            for i in range(N):
                b = i % BUFS
                v.wait_ge(loaded[b], (i // BUFS + 1) * 16)
                V.tensor_tensor(two[:, b], rows[:, b, :, 0:2, :], rows[:, b, :, 2:4, :], ALU.add) \
                    .then_inc(halved, 1)
                v.wait_ge(halved, i + 1)
                V.tensor_tensor(one[:, b], two[:, b, :, 0, :], two[:, b, :, 1, :], ALU.add).then_inc(added, 1)
                v.wait_ge(added, i + 1)
                if i >= BUFS:
                    v.wait_ge(written[b], (i // BUFS) * 16)
                V.tensor_tensor(res[:, b], one[:, b], x[:, i * LOADS:(i + 1) * LOADS, :], ALU.add) \
                    .then_inc(summed, 1)

        @block.scalar
        def _(act):
            for i in range(N):
                act.wait_ge(summed, i + 1)
                act.dma_start(m["out"][i * LOADS * P:(i + 1) * LOADS * P, :].rearrange("(t p) d -> p t d", p=P),
                              res[:, i % BUFS]).then_inc(written[i % BUFS], 16)
            for b in range(BUFS):
                act.wait_ge(written[b], N // BUFS * 16)




def _layout(v):
    import numpy as np
    g = {k: np.ascontiguousarray(x) for k, x in v.items()}
    heads = [h for p in range(PAIRS) for h in pair_heads(p)]
    split = np.concatenate([np.arange(0, DH, 2), np.arange(1, DH, 2)])
    cols = np.concatenate([h * DH + split for h in heads] + [(HEADS + g_) * DH + split for g_ in range(KV)]
                          + [np.arange((HEADS + KV) * DH, QKV)])
    rows = np.concatenate([h * DH + np.arange(DH) for h in heads])
    f = np.float32
    freq = (f(1.0) / f(150000.0) ** (np.arange(0, DH, 2, dtype=f) / f(DH))).astype(f)
    angle = (np.arange(TOK, dtype=f) / f(32.0))[:, None] * freq[None, :]
    i, j = np.arange(P)[:, None], np.arange(P)[None, :]
    neg = f(-1e30)
    sink = g["L0_ffn_attn_sink"][heads].reshape(PAIRS, 2)
    return {
        "x": g["L0_attn_in_seq"].reshape(SEQS * TOK, D),
        "tkT": g["L0_attn_t_k"].T, "tvT": g["L0_attn_t_v"].T, "tqT": g["L0_attn_t_q"].T,
        "W1T": g["L0_attn_W1"].T, "b1": g["L0_attn_b1"].reshape(HID, 1),
        "W2": g["L0_attn_W2"], "W2T": g["L0_attn_W2"].T, "b2": g["L0_attn_b2"].reshape(1, D),
        "norms": np.stack([g["L0_ffn_attn_norm_w"], g["L0_ffn_ffn_norm_w"]], 1),
        "wqkv": g["L0_ffn_qkv_w"][:, cols], "wproj": g["L0_ffn_proj_w"][rows],
        "bias": np.concatenate([g["L0_ffn_qkv_b"][cols], g["L0_ffn_proj_b"], g["L0_ffn_gate_b"]]),
        "sink": sink.reshape(-1),
        "gate": g["L0_ffn_gate_w"], "wup": g["L0_ffn_W_up"], "wdown": g["L0_ffn_W_down"],
        "ident": np.eye(P, dtype=f),
        "mask": np.concatenate([np.where(j >= i, f(0), neg), np.where(j <= i, f(0), neg)], 1).astype(f),
        "before": (i < j).astype(f),
        "rope": np.stack([np.cos(angle), np.sin(angle)], 1).astype(f),
        "iota_e": np.arange(EXPERTS, dtype=f),
        "pick_row": (SPARE + np.arange(SEQS * TOK * TOPK)).reshape(-1, TOPK).astype(f),
        "row_id": (i + P * np.arange(MAX_TILES)[None, :]).astype(f),
        "tile_id": (i + P * np.arange(COLS)[None, :]).astype(f),
        "digits": np.where(i // GROUP == np.arange(P // GROUP)[None, :], EXPERTS ** (i % GROUP), 0).astype(f),
    }


def kernel(**inputs):
    import numpy as np
    import concourse.bacc as bacc
    from concourse.bass_utils import run_bass_kernel_spmd

    nc = bacc.Bacc("TRN2", target_bir_lowering=False, num_devices=1)
    arrays = {"in_" + k: np.ascontiguousarray(v) for k, v in _layout(inputs).items()}
    a = {k[3:]: nc.dram_tensor(k, v.shape, mybir.dt.from_np(v.dtype), kind="ExternalInput").ap()
         for k, v in arrays.items()}
    out = nc.dram_tensor("out_x", [SEQS * TOK, D], F32, kind="ExternalOutput").ap()
    program(nc, a, out)
    r = run_bass_kernel_spmd(nc, [arrays], core_ids=[0])
    return r.results[0]["out_x"].reshape(SEQS, TOK, D)
```
